# Optimizing a Trainium2 kernel written in Bass

```python
import numpy as np
import jax
import jax.numpy as jnp

def _softmax(x, axis=-1):
    return jax.nn.softmax(x, axis=axis)

def _gelu(x):
    return jax.nn.gelu(x, approximate=True)

def _silu(x):
    return jax.nn.silu(x)

def _sigmoid(x):
    return jax.nn.sigmoid(x)

def _layernorm(x, axis=-1, eps=1e-05):
    m = jnp.mean(x, axis=axis, keepdims=True)
    v = jnp.var(x, axis=axis, keepdims=True)
    return (x - m) / jnp.sqrt(v + eps)

def _scatter_add(tgt, idx, src, axis=0):
    return tgt.at[idx].add(src)

def _segment_sum(src, seg, n):
    return jax.ops.segment_sum(src, seg, n)
kernel_name = 'mk_decoder_postln_d2_seqx_r8_fd486c'

def setup_inputs(seed: int=0):
    np.random.seed(seed)
    _w = jnp.asarray

    def _rec_inputs():
        import jax
        import jax.numpy as jnp
        _rk = jax.random.key(seed)
        x = 7.22e-05 + 1 * jax.random.normal(jax.random.fold_in(_rk, 1), (16, 128, 256), jnp.float32)
        _lenS = 128 - jax.random.randint(jax.random.fold_in(_rk, 7), (16,), 0, max(1, 128 // 4) + 1, jnp.int32)
        _lenS2 = 128 - jax.random.randint(jax.random.fold_in(_rk, 8), (16,), 0, max(1, 128 // 4) + 1, jnp.int32)
        _ctx_2048P = jax.random.normal(jax.random.fold_in(_rk, 11), (16, 16, 256), jnp.float32)
        _ctx_2048c = jax.random.dirichlet(jax.random.fold_in(_rk, 511), 0.3 * jnp.ones((16,), jnp.float32), (16, 128))
        _ctx_2048t = jnp.einsum('bsk,bkd->bsd', _ctx_2048c, _ctx_2048P)
        _ctx_2048t = _ctx_2048t * jax.lax.rsqrt(jnp.mean(jnp.square(_ctx_2048t)) + 1e-12) * 0.953939
        ctx_2048 = -0.000514642 + 1.00011 * (_ctx_2048t + 0.3 * jax.random.normal(jax.random.fold_in(_rk, 611), (16, 128, 256), jnp.float32))
        return (x, ctx_2048)
    x, ctx_2048 = _rec_inputs()

    def _L0_attn_setup():
        import jax, jax.numpy as jnp
        import numpy as np
        B, S, HID = (1, 512, 256)
        NH, D = (16, 128)
        RATIO, TOPK, WIN = (4, 8, 128)
        ROPE_DIM = D // 2
        EPS = 1e-06
        NEG = -1e+30

        def rmsnorm(x, w):
            return x * jax.lax.rsqrt(jnp.mean(x * x, axis=-1, keepdims=True) + EPS) * w

        def apply_rope(x, pos):
            half = ROPE_DIM // 2
            inv = 1.0 / 10000.0 ** (jnp.arange(half, dtype=x.dtype) * (2.0 / ROPE_DIM))
            ang = pos.astype(x.dtype)[:, None] * inv[None, :]
            cos, sin = (jnp.cos(ang), jnp.sin(ang))
            x1, x2, rest = (x[..., :half], x[..., half:ROPE_DIM], x[..., ROPE_DIM:])
            return jnp.concatenate([x1 * cos - x2 * sin, x1 * sin + x2 * cos, rest], axis=-1)
        key = jax.random.key(seed)
        ks = jax.random.split(key, 16)
        n = jax.random.normal
        s = 0.02
        return {'hidden_states': n(ks[0], (B, S, HID), jnp.float32), 'Wq': n(ks[1], (HID, NH * D)) * s, 'bq': jnp.zeros((NH * D,)), 'Wcmp': n(ks[2], (HID, 1)) * s, 'bcmp': jnp.zeros((1,)), 'Wk': n(ks[3], (HID, D)) * s, 'bk': jnp.zeros((D,)), 'Wv': n(ks[4], (HID, D)) * s, 'bv': jnp.zeros((D,)), 'Wlk': n(ks[5], (HID, NH * D)) * s, 'blk': jnp.zeros((NH * D,)), 'Wlv': n(ks[6], (HID, NH * D)) * s, 'blv': jnp.zeros((NH * D,)), 'qn_w': jnp.ones((D,)), 'kn_w': jnp.ones((D,)), 'Wo': n(ks[7], (NH * D, HID)) * s, 'bo': jnp.zeros((HID,))}
    _L0_attn_all = _L0_attn_setup()
    _L0_attn_in = {k: v for k, v in _L0_attn_all.items() if k in ('Wq', 'bq', 'Wcmp', 'bcmp', 'Wk', 'bk', 'Wv', 'bv', 'Wlk', 'blk', 'Wlv', 'blv', 'qn_w', 'kn_w', 'Wo', 'bo')}
    del _L0_attn_all

    def _L0_xattn_setup():
        import jax, jax.numpy as jnp
        import numpy as np
        D_MODEL = 256
        NUM_HEADS = 16
        HEAD_DIM = D_MODEL // NUM_HEADS

        def _fq_sym(x, axis):
            s = jnp.max(jnp.abs(x), axis=axis, keepdims=True) / 127.0
            s = jnp.maximum(s, 1e-08)
            q = jnp.clip(jnp.round(x / s), -127.0, 127.0) * s
            return x + jax.lax.stop_gradient(q - x)

        def _fq_unsigned(x, axis):
            s = jnp.max(x, axis=axis, keepdims=True) / 255.0
            s = jnp.maximum(s, 1e-08)
            q = jnp.clip(jnp.round(x / s), 0.0, 255.0) * s
            return x + jax.lax.stop_gradient(q - x)
        key = jax.random.key(seed)
        ks = jax.random.split(key, 8)
        B, N, M, C = (2, 256, 64, D_MODEL)
        return {'x': jax.random.normal(ks[0], (B, N, C), jnp.float32), 'cond': jax.random.normal(ks[1], (B, M, C), jnp.float32), 'Wq': jax.random.normal(ks[2], (C, C), jnp.float32) * 0.02, 'bq': jnp.zeros((C,), jnp.float32), 'Wkv': jax.random.normal(ks[3], (C, 2 * C), jnp.float32) * 0.02, 'bkv': jnp.zeros((2 * C,), jnp.float32), 'Wp': jax.random.normal(ks[4], (C, C), jnp.float32) * 0.02, 'bp': jnp.zeros((C,), jnp.float32)}
    _L0_xattn_all = _L0_xattn_setup()
    _L0_xattn_in = {k: v for k, v in _L0_xattn_all.items() if k in ('Wq', 'bq', 'Wkv', 'bkv', 'Wp', 'bp')}
    del _L0_xattn_all

    def _L0_ffn_setup():
        import jax, jax.numpy as jnp
        import numpy as np
        HIDDEN = 256
        INTER = 1024
        BATCH, LOCAL_SEQ = (2, 512)
        key = jax.random.key(seed)
        k1, k2, k3 = jax.random.split(key, 3)
        h_shard = jax.random.normal(k1, (BATCH, LOCAL_SEQ, HIDDEN), dtype=jnp.float32)
        w_gate_up = jax.random.normal(k2, (2 * INTER, HIDDEN), dtype=jnp.float32) * 0.02
        w_down = jax.random.normal(k3, (HIDDEN, INTER), dtype=jnp.float32) * 0.02
        return {'h_shard': h_shard, 'w_gate_up': w_gate_up, 'w_down': w_down}
    _L0_ffn_all = _L0_ffn_setup()
    _L0_ffn_in = {k: v for k, v in _L0_ffn_all.items() if k in ('w_gate_up', 'w_down')}
    del _L0_ffn_all

    def _L1_attn_setup():
        import jax, jax.numpy as jnp
        import numpy as np
        N_HEADS = 32
        WINDOW = 128

        def _sliding_window_attention(x, Wq, Wk, Wv, Wo, n_heads=N_HEADS, window=WINDOW):
            B, T, D = x.shape
            H, dk = (n_heads, D // n_heads)
            bs = window
            assert T % bs == 0
            nb = T // bs

            def heads(y):
                return y.reshape(B, T, H, dk).transpose(0, 2, 1, 3)
            q = heads(x @ Wq.T)
            k = heads(x @ Wk.T)
            v = heads(x @ Wv.T)
            qb = q.reshape(B, H, nb, bs, dk)
            zpad = jnp.zeros((B, H, bs, dk), dtype=x.dtype)
            kp = jnp.concatenate([zpad, k], axis=2).reshape(B, H, nb + 1, bs, dk)
            vp = jnp.concatenate([zpad, v], axis=2).reshape(B, H, nb + 1, bs, dk)
            kw = jnp.concatenate([kp[:, :, :-1], kp[:, :, 1:]], axis=3)
            vw = jnp.concatenate([vp[:, :, :-1], vp[:, :, 1:]], axis=3)
            scale = 1.0 / np.sqrt(dk).astype(np.float32)
            scores = jnp.einsum('bhnrd,bhncd->bhnrc', qb, kw) * scale
            i = jnp.arange(nb)[:, None, None]
            r = jnp.arange(bs)[None, :, None]
            c = jnp.arange(2 * bs)[None, None, :]
            dist = bs + r - c
            key_global = i * bs - bs + c
            valid = (dist >= 0) & (dist <= window) & (key_global >= 0)
            scores = jnp.where(valid[None, None], scores, jnp.finfo(scores.dtype).min)
            probs = jax.nn.softmax(scores, axis=-1)
            out = jnp.einsum('bhnrc,bhncd->bhnrd', probs, vw)
            out = out.reshape(B, H, T, dk).transpose(0, 2, 1, 3).reshape(B, T, D)
            return out @ Wo.T
        key = jax.random.key(seed)
        ks = jax.random.split(key, 5)
        B, T, D = (2, 512, 256)
        w_std = 0.02
        return {'x': jax.random.normal(ks[0], (B, T, D), dtype=jnp.float32), 'Wq': jax.random.normal(ks[1], (D, D), dtype=jnp.float32) * w_std, 'Wk': jax.random.normal(ks[2], (D, D), dtype=jnp.float32) * w_std, 'Wv': jax.random.normal(ks[3], (D, D), dtype=jnp.float32) * w_std, 'Wo': jax.random.normal(ks[4], (D, D), dtype=jnp.float32) * w_std}
    _L1_attn_all = _L1_attn_setup()
    _L1_attn_in = {k: v for k, v in _L1_attn_all.items() if k in ('Wq', 'Wk', 'Wv', 'Wo')}
    del _L1_attn_all

    def _L1_xattn_setup():
        import jax, jax.numpy as jnp
        import numpy as np
        DIM = 256
        N_HEADS = 16
        HEAD_DIM = DIM // N_HEADS
        EPS = 1e-06
        IMG_LEN = 257

        def rms_norm(x, g, eps=EPS):
            var = jnp.mean(x * x, axis=-1, keepdims=True)
            return x * jax.lax.rsqrt(var + eps) * g

        def _attend(q, k, v, k_mask=None):
            scale = 1.0 / jnp.sqrt(jnp.asarray(HEAD_DIM, q.dtype))
            scores = jnp.einsum('bqnd,bknd->bnqk', q, k) * scale
            if k_mask is not None:
                neg = jnp.asarray(jnp.finfo(scores.dtype).min, scores.dtype)
                scores = jnp.where(k_mask[:, None, None, :], scores, neg)
            probs = jax.nn.softmax(scores, axis=-1)
            return jnp.einsum('bnqk,bknd->bqnd', probs, v)
        key = jax.random.key(seed)
        ks = jax.random.split(key, 16)
        B, L1, L2 = (1, 2048, 769)
        std = 0.02
        inp = {'x': jax.random.normal(ks[0], (B, L1, DIM), jnp.float32), 'context': jax.random.normal(ks[1], (B, L2, DIM), jnp.float32), 'context_lens': jax.random.randint(ks[2], (B,), 32, 513, jnp.int32), 'Wq': jax.random.normal(ks[3], (DIM, DIM), jnp.float32) * std, 'bq': jnp.zeros((DIM,), jnp.float32), 'gq': jnp.ones((DIM,), jnp.float32), 'Wk': jax.random.normal(ks[4], (DIM, DIM), jnp.float32) * std, 'bk': jnp.zeros((DIM,), jnp.float32), 'gk': jnp.ones((DIM,), jnp.float32), 'Wv': jax.random.normal(ks[5], (DIM, DIM), jnp.float32) * std, 'bv': jnp.zeros((DIM,), jnp.float32), 'Wk_img': jax.random.normal(ks[6], (DIM, DIM), jnp.float32) * std, 'bk_img': jnp.zeros((DIM,), jnp.float32), 'gk_img': jnp.ones((DIM,), jnp.float32), 'Wv_img': jax.random.normal(ks[7], (DIM, DIM), jnp.float32) * std, 'bv_img': jnp.zeros((DIM,), jnp.float32), 'Wo': jax.random.normal(ks[8], (DIM, DIM), jnp.float32) * std, 'bo': jnp.zeros((DIM,), jnp.float32)}
        return inp
    _L1_xattn_all = _L1_xattn_setup()
    _L1_xattn_in = {k: v for k, v in _L1_xattn_all.items() if k in ('context_lens', 'Wq', 'bq', 'gq', 'Wk', 'bk', 'gk', 'Wv', 'bv', 'Wk_img', 'bk_img', 'gk_img', 'Wv_img', 'bv_img', 'Wo', 'bo')}
    del _L1_xattn_all

    def _L1_ffn_setup():
        import jax, jax.numpy as jnp
        import numpy as np
        H, I, E, TOP_K = (256, 176, 16, 6)
        IS = 352
        NORM_TOPK_PROB = False

        def _silu_and_mul(gate_up):
            d = gate_up.shape[-1] // 2
            g, u = (gate_up[..., :d], gate_up[..., d:])
            return jax.nn.silu(g) * u
        key = jax.random.key(seed)
        ks = jax.random.split(key, 6)
        s = 0.02
        return {'x': jax.random.normal(ks[0], (1, 256, H), jnp.float32), 'gate_w': jax.random.normal(ks[1], (E, H), jnp.float32) * s, 'w1': jax.random.normal(ks[2], (E, 2 * I, H), jnp.float32) * s, 'w2': jax.random.normal(ks[3], (E, H, I), jnp.float32) * s, 'shared_w1': jax.random.normal(ks[4], (2 * IS, H), jnp.float32) * s, 'shared_w2': jax.random.normal(ks[5], (H, IS), jnp.float32) * s}
    _L1_ffn_all = _L1_ffn_setup()
    _L1_ffn_in = {k: v for k, v in _L1_ffn_all.items() if k in ('gate_w', 'w1', 'w2', 'shared_w1', 'shared_w2')}
    del _L1_ffn_all
    return {'x': x, 'ctx_2048': ctx_2048, 'L0_attn_Wq': _L0_attn_in['Wq'], 'L0_attn_bq': _L0_attn_in['bq'], 'L0_attn_Wcmp': _L0_attn_in['Wcmp'], 'L0_attn_bcmp': _L0_attn_in['bcmp'], 'L0_attn_Wk': _L0_attn_in['Wk'], 'L0_attn_bk': _L0_attn_in['bk'], 'L0_attn_Wv': _L0_attn_in['Wv'], 'L0_attn_bv': _L0_attn_in['bv'], 'L0_attn_Wlk': _L0_attn_in['Wlk'], 'L0_attn_blk': _L0_attn_in['blk'], 'L0_attn_Wlv': _L0_attn_in['Wlv'], 'L0_attn_blv': _L0_attn_in['blv'], 'L0_attn_qn_w': _L0_attn_in['qn_w'], 'L0_attn_kn_w': _L0_attn_in['kn_w'], 'L0_attn_Wo': _L0_attn_in['Wo'], 'L0_attn_bo': _L0_attn_in['bo'], 'L0_xattn_Wq': _L0_xattn_in['Wq'], 'L0_xattn_bq': _L0_xattn_in['bq'], 'L0_xattn_Wkv': _L0_xattn_in['Wkv'], 'L0_xattn_bkv': _L0_xattn_in['bkv'], 'L0_xattn_Wp': _L0_xattn_in['Wp'], 'L0_xattn_bp': _L0_xattn_in['bp'], 'L0_ffn_w_gate_up': _L0_ffn_in['w_gate_up'], 'L0_ffn_w_down': _L0_ffn_in['w_down'], 'L1_attn_Wq': _L1_attn_in['Wq'], 'L1_attn_Wk': _L1_attn_in['Wk'], 'L1_attn_Wv': _L1_attn_in['Wv'], 'L1_attn_Wo': _L1_attn_in['Wo'], 'L1_xattn_context_lens': _L1_xattn_in['context_lens'], 'L1_xattn_Wq': _L1_xattn_in['Wq'], 'L1_xattn_bq': _L1_xattn_in['bq'], 'L1_xattn_gq': _L1_xattn_in['gq'], 'L1_xattn_Wk': _L1_xattn_in['Wk'], 'L1_xattn_bk': _L1_xattn_in['bk'], 'L1_xattn_gk': _L1_xattn_in['gk'], 'L1_xattn_Wv': _L1_xattn_in['Wv'], 'L1_xattn_bv': _L1_xattn_in['bv'], 'L1_xattn_Wk_img': _L1_xattn_in['Wk_img'], 'L1_xattn_bk_img': _L1_xattn_in['bk_img'], 'L1_xattn_gk_img': _L1_xattn_in['gk_img'], 'L1_xattn_Wv_img': _L1_xattn_in['Wv_img'], 'L1_xattn_bv_img': _L1_xattn_in['bv_img'], 'L1_xattn_Wo': _L1_xattn_in['Wo'], 'L1_xattn_bo': _L1_xattn_in['bo'], 'L1_ffn_gate_w': _L1_ffn_in['gate_w'], 'L1_ffn_w1': _L1_ffn_in['w1'], 'L1_ffn_w2': _L1_ffn_in['w2'], 'L1_ffn_shared_w1': _L1_ffn_in['shared_w1'], 'L1_ffn_shared_w2': _L1_ffn_in['shared_w2']}

def reference(x, ctx_2048, L0_attn_Wq, L0_attn_bq, L0_attn_Wcmp, L0_attn_bcmp, L0_attn_Wk, L0_attn_bk, L0_attn_Wv, L0_attn_bv, L0_attn_Wlk, L0_attn_blk, L0_attn_Wlv, L0_attn_blv, L0_attn_qn_w, L0_attn_kn_w, L0_attn_Wo, L0_attn_bo, L0_xattn_Wq, L0_xattn_bq, L0_xattn_Wkv, L0_xattn_bkv, L0_xattn_Wp, L0_xattn_bp, L0_ffn_w_gate_up, L0_ffn_w_down, L1_attn_Wq, L1_attn_Wk, L1_attn_Wv, L1_attn_Wo, L1_xattn_context_lens, L1_xattn_Wq, L1_xattn_bq, L1_xattn_gq, L1_xattn_Wk, L1_xattn_bk, L1_xattn_gk, L1_xattn_Wv, L1_xattn_bv, L1_xattn_Wk_img, L1_xattn_bk_img, L1_xattn_gk_img, L1_xattn_Wv_img, L1_xattn_bv_img, L1_xattn_Wo, L1_xattn_bo, L1_ffn_gate_w, L1_ffn_w1, L1_ffn_w2, L1_ffn_shared_w1, L1_ffn_shared_w2):
    import jax
    import jax.numpy as jnp

    def _L0_attn_ref(hidden_states, Wq, bq, Wcmp, bcmp, Wk, bk, Wv, bv, Wlk, blk, Wlv, blv, qn_w, kn_w, Wo, bo):
        import jax, jax.numpy as jnp
        import numpy as np
        B, S, HID = (1, 512, 256)
        NH, D = (16, 128)
        RATIO, TOPK, WIN = (4, 8, 128)
        ROPE_DIM = D // 2
        EPS = 1e-06
        NEG = -1e+30

        def rmsnorm(x, w):
            return x * jax.lax.rsqrt(jnp.mean(x * x, axis=-1, keepdims=True) + EPS) * w

        def apply_rope(x, pos):
            half = ROPE_DIM // 2
            inv = 1.0 / 10000.0 ** (jnp.arange(half, dtype=x.dtype) * (2.0 / ROPE_DIM))
            ang = pos.astype(x.dtype)[:, None] * inv[None, :]
            cos, sin = (jnp.cos(ang), jnp.sin(ang))
            x1, x2, rest = (x[..., :half], x[..., half:ROPE_DIM], x[..., ROPE_DIM:])
            return jnp.concatenate([x1 * cos - x2 * sin, x1 * sin + x2 * cos, rest], axis=-1)
        Bq, Sq, _ = hidden_states.shape
        C = Sq // RATIO
        scale = 1.0 / jnp.sqrt(jnp.float32(D))
        pos = jnp.arange(Sq)
        q = (hidden_states @ Wq + bq).reshape(Bq, Sq, NH, D).transpose(0, 2, 1, 3)
        q = apply_rope(rmsnorm(q, qn_w), pos)
        w_log = (hidden_states @ Wcmp + bcmp).reshape(Bq, C, RATIO)
        w_cmp = jax.nn.softmax(w_log, axis=-1)
        entries = jnp.einsum('bcr,bcrh->bch', w_cmp, hidden_states.reshape(Bq, C, RATIO, HID))
        block_ends = jnp.arange(1, C + 1) * RATIO - 1
        ck = apply_rope(rmsnorm(entries @ Wk + bk, kn_w), block_ends)
        cv = entries @ Wv + bv
        sc = jnp.einsum('bhsd,bcd->bhsc', q, ck) * scale
        causal = block_ends[None, None, None, :] <= pos[None, None, :, None]
        sc = jnp.where(causal, sc, NEG)
        tv, ti = jax.lax.top_k(sc, TOPK)
        sel = (tv > NEG / 2).astype(sc.dtype)
        m = jnp.max(tv, axis=-1, keepdims=True)
        e = jnp.exp(tv - m) * sel
        pw = e / jnp.maximum(e.sum(axis=-1, keepdims=True), 1e-09)
        v_g = cv[jnp.arange(Bq)[:, None, None, None], ti]
        ctx_sparse = jnp.einsum('bhsk,bhskd->bhsd', pw, v_g)
        lk = apply_rope(rmsnorm((hidden_states @ Wlk + blk).reshape(Bq, Sq, NH, D).transpose(0, 2, 1, 3), kn_w), pos)
        lv = (hidden_states @ Wlv + blv).reshape(Bq, Sq, NH, D).transpose(0, 2, 1, 3)
        nc = Sq // WIN
        qc = q.reshape(Bq, NH, nc, WIN, D)

        def windowize(x):
            prev = jnp.pad(x, ((0, 0), (0, 0), (WIN, 0), (0, 0)))[:, :, :-WIN].reshape(Bq, NH, nc, WIN, D)
            cur = x.reshape(Bq, NH, nc, WIN, D)
            return jnp.concatenate([prev, cur], axis=3)
        kw, vw = (windowize(lk), windowize(lv))
        i = jnp.arange(WIN)[:, None]
        j = jnp.arange(2 * WIN)[None, :]
        rel = i + WIN - j
        band = (rel >= 0) & (rel <= WIN)
        kpos_ok = jnp.arange(nc)[:, None, None] * WIN - WIN + j[None] >= 0
        mask = band[None] & kpos_ok
        sl = jnp.einsum('bhcqd,bhckd->bhcqk', qc, kw) * scale
        sl = jnp.where(mask[None, None], sl, NEG)
        pl = jax.nn.softmax(sl, axis=-1)
        ctx_local = jnp.einsum('bhcqk,bhckd->bhcqd', pl, vw).reshape(Bq, NH, Sq, D)
        merged = (ctx_sparse + ctx_local) * 0.5
        out = merged.transpose(0, 2, 1, 3).reshape(Bq, Sq, NH * D) @ Wo + bo
        return out

    def _L0_xattn_ref(x, cond, Wq, bq, Wkv, bkv, Wp, bp):
        import jax, jax.numpy as jnp
        import numpy as np
        D_MODEL = 256
        NUM_HEADS = 16
        HEAD_DIM = D_MODEL // NUM_HEADS

        def _fq_sym(x, axis):
            s = jnp.max(jnp.abs(x), axis=axis, keepdims=True) / 127.0
            s = jnp.maximum(s, 1e-08)
            q = jnp.clip(jnp.round(x / s), -127.0, 127.0) * s
            return x + jax.lax.stop_gradient(q - x)

        def _fq_unsigned(x, axis):
            s = jnp.max(x, axis=axis, keepdims=True) / 255.0
            s = jnp.maximum(s, 1e-08)
            q = jnp.clip(jnp.round(x / s), 0.0, 255.0) * s
            return x + jax.lax.stop_gradient(q - x)
        B, N, C = x.shape
        H, hd = (NUM_HEADS, HEAD_DIM)
        q = (x @ Wq + bq).reshape(1, B * N, H, hd)
        kv = (cond @ Wkv + bkv).reshape(1, -1, 2, H, hd)
        k, v = (kv[:, :, 0], kv[:, :, 1])
        scale = 1.0 / np.sqrt(hd).astype(np.float32)
        q = jnp.transpose(q * scale, (0, 2, 1, 3))
        k = jnp.transpose(k, (0, 2, 1, 3))
        v = jnp.transpose(v, (0, 2, 1, 3))
        q = _fq_sym(q, axis=-1)
        k = _fq_sym(k, axis=-1)
        v = _fq_sym(v, axis=2)
        attn = jnp.einsum('bhqd,bhkd->bhqk', q, k)
        attn = jax.nn.softmax(attn.astype(jnp.float32), axis=-1)
        attn = _fq_unsigned(attn, axis=-1)
        out = jnp.einsum('bhqk,bhkd->bhqd', attn, v)
        out = jnp.transpose(out, (0, 2, 1, 3)).reshape(B, N, C)
        return out @ Wp + bp

    def _L0_ffn_ref(h_shard, w_gate_up, w_down):
        import jax, jax.numpy as jnp
        import numpy as np
        HIDDEN = 256
        INTER = 1024
        BATCH, LOCAL_SEQ = (2, 512)
        batch, local_seq, hidden = h_shard.shape
        gate_up = jnp.einsum('bsh,oh->bso', h_shard, w_gate_up)
        gate, up = jnp.split(gate_up, 2, axis=-1)
        h = jax.nn.silu(gate) * up
        out = jnp.einsum('bsi,hi->bsh', h, w_down)
        return out

    def _L1_attn_ref(x, Wq, Wk, Wv, Wo):
        import jax, jax.numpy as jnp
        import numpy as np
        N_HEADS = 32
        WINDOW = 128

        def _sliding_window_attention(x, Wq, Wk, Wv, Wo, n_heads=N_HEADS, window=WINDOW):
            B, T, D = x.shape
            H, dk = (n_heads, D // n_heads)
            bs = window
            assert T % bs == 0
            nb = T // bs

            def heads(y):
                return y.reshape(B, T, H, dk).transpose(0, 2, 1, 3)
            q = heads(x @ Wq.T)
            k = heads(x @ Wk.T)
            v = heads(x @ Wv.T)
            qb = q.reshape(B, H, nb, bs, dk)
            zpad = jnp.zeros((B, H, bs, dk), dtype=x.dtype)
            kp = jnp.concatenate([zpad, k], axis=2).reshape(B, H, nb + 1, bs, dk)
            vp = jnp.concatenate([zpad, v], axis=2).reshape(B, H, nb + 1, bs, dk)
            kw = jnp.concatenate([kp[:, :, :-1], kp[:, :, 1:]], axis=3)
            vw = jnp.concatenate([vp[:, :, :-1], vp[:, :, 1:]], axis=3)
            scale = 1.0 / np.sqrt(dk).astype(np.float32)
            scores = jnp.einsum('bhnrd,bhncd->bhnrc', qb, kw) * scale
            i = jnp.arange(nb)[:, None, None]
            r = jnp.arange(bs)[None, :, None]
            c = jnp.arange(2 * bs)[None, None, :]
            dist = bs + r - c
            key_global = i * bs - bs + c
            valid = (dist >= 0) & (dist <= window) & (key_global >= 0)
            scores = jnp.where(valid[None, None], scores, jnp.finfo(scores.dtype).min)
            probs = jax.nn.softmax(scores, axis=-1)
            out = jnp.einsum('bhnrc,bhncd->bhnrd', probs, vw)
            out = out.reshape(B, H, T, dk).transpose(0, 2, 1, 3).reshape(B, T, D)
            return out @ Wo.T
        return _sliding_window_attention(x, Wq, Wk, Wv, Wo)

    def _L1_xattn_ref(x, context, context_lens, Wq, bq, gq, Wk, bk, gk, Wv, bv, Wk_img, bk_img, gk_img, Wv_img, bv_img, Wo, bo):
        import jax, jax.numpy as jnp
        import numpy as np
        DIM = 256
        N_HEADS = 16
        HEAD_DIM = DIM // N_HEADS
        EPS = 1e-06
        IMG_LEN = 257

        def rms_norm(x, g, eps=EPS):
            var = jnp.mean(x * x, axis=-1, keepdims=True)
            return x * jax.lax.rsqrt(var + eps) * g

        def _attend(q, k, v, k_mask=None):
            scale = 1.0 / jnp.sqrt(jnp.asarray(HEAD_DIM, q.dtype))
            scores = jnp.einsum('bqnd,bknd->bnqk', q, k) * scale
            if k_mask is not None:
                neg = jnp.asarray(jnp.finfo(scores.dtype).min, scores.dtype)
                scores = jnp.where(k_mask[:, None, None, :], scores, neg)
            probs = jax.nn.softmax(scores, axis=-1)
            return jnp.einsum('bnqk,bknd->bqnd', probs, v)
        b = x.shape[0]
        n, d = (N_HEADS, HEAD_DIM)
        ctx_img = context[:, :IMG_LEN]
        ctx_txt = context[:, IMG_LEN:]
        q = rms_norm(x @ Wq + bq, gq).reshape(b, -1, n, d)
        k = rms_norm(ctx_txt @ Wk + bk, gk).reshape(b, -1, n, d)
        v = (ctx_txt @ Wv + bv).reshape(b, -1, n, d)
        k_img = rms_norm(ctx_img @ Wk_img + bk_img, gk_img).reshape(b, -1, n, d)
        v_img = (ctx_img @ Wv_img + bv_img).reshape(b, -1, n, d)
        img_x = _attend(q, k_img, v_img)
        k_mask = jnp.arange(k.shape[1])[None, :] < context_lens[:, None]
        txt_x = _attend(q, k, v, k_mask)
        out = (txt_x + img_x).reshape(b, -1, n * d)
        return out @ Wo + bo

    def _L1_ffn_ref(x, gate_w, w1, w2, shared_w1, shared_w2):
        import jax, jax.numpy as jnp
        import numpy as np
        H, I, E, TOP_K = (256, 176, 16, 6)
        IS = 352
        NORM_TOPK_PROB = False

        def _silu_and_mul(gate_up):
            d = gate_up.shape[-1] // 2
            g, u = (gate_up[..., :d], gate_up[..., d:])
            return jax.nn.silu(g) * u
        B, S, Hd = x.shape
        xf = x.reshape(-1, Hd)
        T = xf.shape[0]
        shared_out = _silu_and_mul(xf @ shared_w1.T) @ shared_w2.T
        logits = xf @ gate_w.T
        probs = jax.nn.softmax(logits.astype(jnp.float32), axis=-1)
        routing_weights, selected = jax.lax.top_k(probs, TOP_K)
        if NORM_TOPK_PROB:
            routing_weights = routing_weights / routing_weights.sum(-1, keepdims=True)
        combine = jnp.zeros((T, E), jnp.float32).at[jnp.arange(T)[:, None], selected].add(routing_weights).astype(x.dtype)
        gate_up = jnp.einsum('th,eoh->teo', xf, w1)
        act = _silu_and_mul(gate_up)
        moe_out = jnp.einsum('te,tei,ehi->th', combine, act, w2)
        return (moe_out + shared_out).reshape(B, S, Hd)
    x = _layernorm(x + _L0_attn_ref(x, L0_attn_Wq, L0_attn_bq, L0_attn_Wcmp, L0_attn_bcmp, L0_attn_Wk, L0_attn_bk, L0_attn_Wv, L0_attn_bv, L0_attn_Wlk, L0_attn_blk, L0_attn_Wlv, L0_attn_blv, L0_attn_qn_w, L0_attn_kn_w, L0_attn_Wo, L0_attn_bo), axis=-1)
    x = _layernorm(x + _L0_xattn_ref(x, ctx_2048, L0_xattn_Wq, L0_xattn_bq, L0_xattn_Wkv, L0_xattn_bkv, L0_xattn_Wp, L0_xattn_bp), axis=-1)
    x = _layernorm(x + _L0_ffn_ref(x, L0_ffn_w_gate_up, L0_ffn_w_down), axis=-1)
    x = _layernorm(x + _L1_attn_ref(x, L1_attn_Wq, L1_attn_Wk, L1_attn_Wv, L1_attn_Wo), axis=-1)
    x = _layernorm(x + _L1_xattn_ref(x, ctx_2048, L1_xattn_context_lens, L1_xattn_Wq, L1_xattn_bq, L1_xattn_gq, L1_xattn_Wk, L1_xattn_bk, L1_xattn_gk, L1_xattn_Wv, L1_xattn_bv, L1_xattn_Wk_img, L1_xattn_bk_img, L1_xattn_gk_img, L1_xattn_Wv_img, L1_xattn_bv_img, L1_xattn_Wo, L1_xattn_bo), axis=-1)
    x = _layernorm(x + _L1_ffn_ref(x, L1_ffn_gate_w, L1_ffn_w1, L1_ffn_w2, L1_ffn_shared_w1, L1_ffn_shared_w2), axis=-1)
    return x

_drawn_inputs = setup_inputs


def setup_inputs(seed=0):
    import zlib

    import numpy as np

    out = dict(_drawn_inputs(seed))
    spreads = {'L0_attn_bq': (0.0, 0.561),
     'L0_attn_bk': (0.0, 0.8),
     'L0_attn_bv': (0.0, 0.1),
     'L0_attn_blk': (0.0, 0.8),
     'L0_attn_blv': (0.0, 0.1),
     'L0_attn_qn_w': (1.0, 0.6),
     'L0_attn_kn_w': (1.0, 0.6),
     'L0_attn_bo': (0.0, 0.1),
     'L0_xattn_bq': (0.0, 0.8),
     'L0_xattn_bkv': (0.0, 0.1),
     'L0_xattn_bp': (0.0, 0.1),
     'L1_xattn_bq': (0.0, 0.8),
     'L1_xattn_gq': (1.0, 0.6),
     'L1_xattn_bk': (0.0, 0.1),
     'L1_xattn_gk': (1.0, 0.2),
     'L1_xattn_bv': (0.0, 0.1),
     'L1_xattn_bk_img': (0.0, 0.8),
     'L1_xattn_gk_img': (1.0, 0.6),
     'L1_xattn_bv_img': (0.0, 0.294),
     'L1_xattn_bo': (0.0, 0.1)}
    factors = {'L0_attn_Wcmp': 4.248,
     'L0_xattn_Wq': 8.0,
     'L0_xattn_Wkv': 4.318,
     'L1_attn_Wq': 8.0,
     'L1_attn_Wk': 8.0,
     'L1_xattn_Wq': 3.157,
     'L1_xattn_Wk_img': 3.007,
     'L1_ffn_gate_w': 8.0,
     'L1_ffn_w1': 8.0,
     'L1_ffn_w2': 8.0,
     'L1_ffn_shared_w1': 2.819,
     'L1_ffn_shared_w2': 2.815}
    for name, (base, spread) in spreads.items():
        noise = np.random.default_rng([zlib.crc32(name.encode()), seed]).standard_normal(out[name].shape)
        drawn = base * np.exp(spread * noise) if base else spread * noise
        out[name] = jnp.asarray(drawn.astype(out[name].dtype))
    for name, factor in factors.items():
        out[name] = (out[name] * factor).astype(out[name].dtype)
    return out
```

```python
from contextlib import ExitStack

import numpy as np

import concourse.bass as bass
from concourse import mybir

F32 = mybir.dt.float32
BF16 = mybir.dt.bfloat16
U16 = mybir.dt.uint16
ALU = mybir.AluOpType
ACT = mybir.ActivationFunctionType
AX = mybir.AxisListType

P = 128
B = 16
H = 256
KT = H // P
BANK = 512
NEG = -1e30
LN_EPS = 1e-5
RMS_EPS = 1e-6

BIASES = [("L0_attn_bq", 2048), ("L0_attn_blk", 2048), ("L0_attn_blv", 2048), ("L0_attn_bk", 128),
          ("L0_attn_bv", 128), ("L0_attn_bo", 256), ("L0_xattn_bq", 256), ("L0_xattn_bkv", 512),
          ("L0_xattn_bp", 256), ("L1_xattn_bq", 256), ("L1_xattn_bk_img", 256), ("L1_xattn_bv_img", 256),
          ("L1_xattn_bo", 256)]
BIAS_AT = {}
for _name, _n in BIASES:
    BIAS_AT[_name] = sum(n for _, n in BIASES[:len(BIAS_AT)])
BIAS_LEN = sum(n for _, n in BIASES)


class Count:

    def __init__(self, sem, per):
        self.sem, self.per = sem, per

    def open(self, eng):
        eng.sem_inc(self.sem, self.per)

    def of(self, b, k=None):
        return self.per * b + (self.per + (self.per if k is None else k))


class Chain:

    def __init__(self, eng, sem, per, base=0):
        self.eng, self.sem, self.per, self.base, self.n = eng, sem, per, base, 0

    def start(self, b):
        self.b, self.n = b, 0

    def mark(self, ins):
        self.n += 1
        ins.then_inc(self.sem, 1)
        return self.n

    def wait(self, n=None):
        self.eng.wait_ge(self.sem, self.per * self.b + (self.base + (self.n if n is None else n)))

    def link(self, ins):
        self.mark(ins)
        self.wait()

    def settle(self):
        self.n += 1
        self.eng.sem_inc(self.sem, 1)

    def end(self):
        assert self.n == self.per, f"{self.n} links in a pass, {self.per} counted"


def semaphores(nc, ctx):
    held = []

    def clear():
        nc.clear_and_free_semaphores(held)
        nc.all_engine_barrier()

    def sem(name):
        held.append(nc.alloc_semaphore(name))
        return held[-1]

    ctx.callback(clear)
    return sem


def bcast(ap, shape):
    return ap.unsqueeze(2).to_broadcast(shape)


def over_heads(ap, heads):
    return ap.unsqueeze(1).to_broadcast([ap.shape[0], heads, ap.shape[1]])


class Core:

    def __init__(self, nc, ctx, A, out):
        self.nc, self.A, self.out = nc, A, out

        def sb(name, shape, dt=F32):
            return ctx.enter_context(nc.sbuf_tensor(name, shape, dt))

        self.x = sb("x_res", [P, B, H])
        self.ident = sb("ident", [P, P])
        self.identb = sb("identb", [P, P], BF16)
        self.causal = sb("causal", [P, 4, P], BF16)
        self.bias_rows = sb("bias_rows", [3, BIAS_LEN], BF16)
        self.ones = sb("ones", [3, P], BF16)
        self.neghalf = sb("neghalf", [P, 32])

    def bias(self, name, lo=0, n=None):
        at = BIAS_AT[name] + lo
        return self.bias_rows[:, at:at + (dict(BIASES)[name] - lo if n is None else n)]


def setup(core):
    nc, A = core.nc, core.A
    rows = BIAS_LEN // P
    with ExitStack() as ctx:
        def sb(name, shape, dt=F32):
            return ctx.enter_context(nc.sbuf_tensor(name, shape, dt))

        causal_f = sb("causal_f", [P, P])
        whole = sb("bias_whole", [rows, P])
        rest = sb("bias_rest", [rows, 2, P])
        parts = sb("bias_parts", [rows, 3, P], BF16)
        sem = semaphores(nc, ctx)
        loaded, bias_in, made, spread = (sem("setup_" + n) for n in ("loaded", "bias_in", "made", "spread"))
        block = ctx.enter_context(nc.Block())

        @block.sync
        def _(sp):
            for name, n in BIASES:
                at = BIAS_AT[name] // P
                sp.dma_start(whole[at:at + n // P, :], A[name].rearrange("(a p) -> a p", p=P)).then_inc(bias_in, 16)
            sp.dma_start(core.ident[:, :], A["c_ident"]).then_inc(loaded, 16)
            sp.dma_start(causal_f[:, :], A["c_causal"]).then_inc(loaded, 16)
            sp.dma_start(core.x[:, :, :], A["x"].rearrange("b p h -> p b h")).then_inc(loaded, 16)
            sp.wait_ge(made, 5)
            for j in range(3):
                sp.dma_start(core.bias_rows[j:j + 1, :].rearrange("o (a p) -> o a p", p=P),
                             parts[:, j, :]).then_inc(spread, 16)
            sp.wait_ge(spread, 48)
            sp.wait_ge(loaded, 48)

        @block.vector
        def _(dve):
            dve.wait_ge(bias_in, 16 * len(BIASES))
            dve.tensor_copy(parts[:, 0, :], whole[:, :]).then_inc(made, 1)
            dve.wait_ge(made, 1)
            dve.tensor_tensor(rest[:, 0, :], whole[:, :], parts[:, 0, :], ALU.subtract).then_inc(made, 1)
            dve.wait_ge(made, 2)
            dve.tensor_copy(parts[:, 1, :], rest[:, 0, :]).then_inc(made, 1)
            dve.wait_ge(made, 3)
            dve.tensor_tensor(rest[:, 1, :], rest[:, 0, :], parts[:, 1, :], ALU.subtract).then_inc(made, 1)
            dve.wait_ge(made, 4)
            dve.tensor_copy(parts[:, 2, :], rest[:, 1, :]).then_inc(made, 1)
            dve.wait_ge(loaded, 48)
            dve.tensor_copy(core.identb[:, :], core.ident[:, :])
            for j in range(4):
                dve.tensor_copy(core.causal[:, j, :], causal_f[:, :])
            dve.memset(core.ones[:, :], 1.0)
            dve.memset(core.neghalf[:, :], -0.5)


NH, D = 16, 128
RATIO, NC = 4, 32
ROPE = D // 2
G = 4
CHOSEN = 3e38


def l0_attention(core, wcol):
    nc, A = core.nc, core.A
    NG = NH // G
    with ExitStack() as ctx:
        def sb(name, shape, dt=F32):
            return ctx.enter_context(nc.sbuf_tensor(name, shape, dt))

        def ps(name, shape, dt=F32):
            return ctx.enter_context(nc.psum_tensor(name, shape, dt))

        named = semaphores(nc, ctx)

        def sem(name):
            return named("a0_" + name)

        def count(name, per):
            return Count(sem(name), per)

        w_qkv = [sb(f"a0_w{n}", [P, KT, NH * D]) for n in "qkv"]
        w_o = sb("a0_wo", [P, NH, H])
        w_c = sb("a0_wc", [P, KT, 2 * D])
        cq, ck_tab, cc = (sb(n, [P, D]) for n in ("a0_cos_q", "a0_cos_k", "a0_cos_c"))
        sq_tab, sk_tab, sc_tab = (sb(n, [P, ROPE]) for n in ("a0_sin_q", "a0_sin_k", "a0_sin_c"))
        wn = sb("a0_norm_w", [P, 2, D])
        cmask_f = sb("a0_cmask_f", [P, NC])
        cmask = sb("a0_cmask", [P, NH, NC], BF16)
        member = sb("a0_member", [P, NC])

        xb = sb("a0_xb", [P, H])
        xT = sb("a0_xT", [P, KT, P])
        raw = [sb(f"a0_raw{n}", [P, NH * D]) for n in "qkv"]
        rot = [sb(f"a0_rot{n}", [P, NH * D]) for n in "qk"]
        sq = sb("a0_sq", [P, NH * D])
        half = sb("a0_half", [P, NH * ROPE])
        ssq = sb("a0_ssq", [P, 2 * NH])
        rstd = sb("a0_rstd", [P, 2 * NH])
        qT = sb("a0_qT", [P, NH, P])
        kT = sb("a0_kT", [P, NH, P])
        wsel = sb("a0_wsel", [P, NC])
        entT = sb("a0_entT", [P, KT, 4, NC])
        ckr = sb("a0_ckr", [P, D])
        cv = sb("a0_cv", [P, G, D])
        crot = sb("a0_crot", [P, D])
        chalf = sb("a0_chalf", [P, ROPE])
        csq = sb("a0_csq", [P, D])
        cst = sb("a0_cst", [P, 3])
        ckT = sb("a0_ckT", [P, P])
        scm = sb("a0_scm", [P, NH, NC])
        top = sb("a0_top", [P, NH, 8])
        repl = sb("a0_repl", [P, NH, NC])
        tmax = sb("a0_tmax", [P, NH])
        es = sb("a0_es", [P, NH, NC])
        tsum = sb("a0_tsum", [P, NH])
        psT = sb("a0_psT", [P, NG, P])
        rqs = sb("a0_rqs", [P, NH])
        lmax = sb("a0_lmax", [P, NH])
        nbias = sb("a0_nbias", [P, NH])
        lsum = sb("a0_lsum", [P, NH])
        lrec = sb("a0_lrec", [P, NH])
        prob = [sb(f"a0_prob{i}", [P, G, P]) for i in range(2)]
        pT = [sb(f"a0_pT{i}", [P, G, P]) for i in range(2)]
        cT = [sb(f"a0_cT{i}", [P, G, P]) for i in range(2)]
        y = sb("a0_y", [P, H])
        stats = sb("a0_stats", [P, 6])
        mv = sb("a0_mv", [P, 2])
        ln_r = sb("a0_ln_r", [P, 1])

        proj = [ps(f"a0_p_proj{i}", [P, BANK]) for i in range(2)]
        work = [ps(f"a0_p_work{i}", [P, BANK]) for i in range(2)]
        p_pT = ps("a0_p_pT", [P, BANK])
        p_cT = ps("a0_p_cT", [P, BANK])
        p_c = ps("a0_p_c", [P, BANK])
        p_o = ps("a0_p_o", [P, BANK])

        loaded, tables = sem("loaded"), sem("tables")
        dve_steps = sem("dve_steps")
        LOADS, TABLES, DVE_STEPS = 16, 11, 66
        tile_in = count("tile_in", 1)
        work_made = count("work_made", 13)
        work_read = count("work_read", 9)
        proj_made = count("proj_made", 12)
        proj_read = count("proj_read", 12)
        squared = count("squared", 2)
        q_rot = count("q_rot", 1)
        k_rot = count("k_rot", 1)
        summed = count("summed", 1)
        rooted = count("rooted", 3)
        k_normed = count("k_normed", 1)
        c_made = count("c_made", 5)
        c_read = count("c_read", 4)
        c_up = count("c_up", 2)
        c_sum = count("c_sum", 1)
        s_exp = count("sparse_exp", 1)
        s_arg = count("sparse_arg", 1)
        s_prob = count("sparse_prob", 1)
        bias_up = count("bias_up", NG)
        l_exp = count("local_exp", NG)
        l_prob = count("local_prob", NG)
        pT_made, pT_read = count("pT_made", NG), count("pT_read", NG)
        cT_made, cT_read = count("cT_made", NG), count("cT_read", NG)
        o_made, o_read = count("o_made", 1), count("o_read", 1)
        var_up = count("var_up", 1)
        x_up = count("x_up", 1)

        block = ctx.enter_context(nc.Block())

        @block.sync
        def _(sp):
            for w, name in zip(w_qkv, ("L0_attn_Wq", "L0_attn_Wlk", "L0_attn_Wlv")):
                sp.dma_start(w[:, :, :], A[name].rearrange("(t p) n -> p t n", p=P)).then_inc(loaded, 16)
            sp.dma_start(w_o[:, :, :], A["L0_attn_Wo"].rearrange("(h p) n -> p h n", p=P)).then_inc(loaded, 16)
            for j, name in enumerate(("L0_attn_Wk", "L0_attn_Wv")):
                sp.dma_start(w_c[:, :, j * D:(j + 1) * D],
                             A[name].rearrange("(t p) n -> p t n", p=P)).then_inc(loaded, 16)
            for j, name in enumerate(("L0_attn_qn_w", "L0_attn_kn_w")):
                sp.dma_start(wn[:, j, :], A[name].partition_broadcast(P)).then_inc(loaded, 16)
            for t, name in ((cq, "c_cos"), (ck_tab, "c_cos"), (cc, "c_cos_c"), (sq_tab, "c_sin"),
                            (sk_tab, "c_sin"), (sc_tab, "c_sin_c"), (cmask_f, "c_cmask"), (member, "c_member")):
                sp.dma_start(t[:, :], A[name]).then_inc(loaded, 16)
            sp.wait_ge(loaded, 16 * LOADS)

        @block.gpsimd
        def _(pool):
            for c in (tile_in, squared, rooted, k_normed):
                c.open(pool)
            with pool.Fori(0, B) as b:
                pool.wait_ge(work_made.sem, work_made.of(b - 1))
                pool.wait_ge(c_made.sem, c_made.of(b - 1))
                pool.tensor_copy(xb[:, :], core.x[:, bass.ds(b, 1), :].rearrange("p o h -> p (o h)")).then_inc(tile_in.sem, 1)
                for j in range(2):
                    pool.wait_ge(proj_read.sem, proj_read.of(b, 4 * (j + 1)))
                    if j == 0:
                        pool.wait_ge(summed.sem, summed.of(b - 1))
                    else:
                        pool.wait_ge(c_sum.sem, c_sum.of(b))
                        pool.tensor_tensor(cst[:, 2:3], cst[:, 1:2], core.neghalf[:, 0:1], ALU.pow).then_inc(rooted.sem, 1)
                        pool.wait_ge(q_rot.sem, q_rot.of(b))
                    pool.tensor_tensor(sq[:, :], raw[j][:, :], raw[j][:, :], ALU.mult).then_inc(squared.sem, 1)
                pool.wait_ge(summed.sem, summed.of(b))
                pool.tensor_tensor(rstd[:, :], ssq[:, :], core.neghalf[:, :], ALU.pow).then_inc(rooted.sem, 1)
                pool.wait_ge(rooted.sem, rooted.of(b, 2))
                pool.wait_ge(k_rot.sem, k_rot.of(b))
                kr = rot[1][:, :].rearrange("p (h d) -> p h d", h=NH)
                pool.tensor_tensor(kr, kr, bcast(rstd[:, NH:], [P, NH, D]), ALU.mult).then_inc(k_normed.sem, 1)
                pool.wait_ge(var_up.sem, var_up.of(b))
                pool.tensor_tensor(ln_r[:, :], mv[:, 1:2], core.neghalf[:, 0:1], ALU.pow).then_inc(rooted.sem, 1)

        @block.tensor
        def _(pe):
            for c in (work_made, proj_made, c_made, pT_made, cT_made, o_made):
                c.open(pe)
            pe.wait_ge(loaded, 16 * LOADS)
            pe.wait_ge(tables, TABLES)
            with pe.Fori(0, B) as b:
                pe.wait_ge(tile_in.sem, tile_in.of(b))
                pe.wait_ge(l_exp.sem, l_exp.of(b - 1))
                for t in range(KT):
                    mm = pe.transpose(work[0][:, t * P:(t + 1) * P], xb[:, t * P:(t + 1) * P], core.ident[:, :])
                mm.then_inc(work_made.sem, 1)
                pe.wait_ge(c_up.sem, c_up.of(b, 1))
                pe.wait_ge(c_read.sem, c_read.of(b - 1))
                for t in range(KT):
                    mm = pe.matmul(p_c[:, t * NC:(t + 1) * NC], xb[:, t * P:(t + 1) * P], wsel[:, :],
                                   start=True, stop=True)
                mm.then_inc(c_made.sem, 1)
                pe.wait_ge(work_read.sem, work_read.of(b, 1))

                def project(n):
                    i, c = n // 4, n % 4
                    bank = proj[n % 2]
                    pe.wait_ge(proj_read.sem, proj_read.of(b, n - 1) if n >= 1 else proj_read.of(b - 1, 11))
                    name = ("L0_attn_bq", "L0_attn_blk", "L0_attn_blv")[i]
                    pe.matmul(bank[:, :], core.ones[:, :], core.bias(name, c * BANK, BANK), start=True, stop=False)
                    for t in range(KT):
                        mm = pe.matmul(bank[:, :], xT[:, t, :], w_qkv[i][:, t, c * BANK:(c + 1) * BANK],
                                       start=False, stop=(t == KT - 1))
                    mm.then_inc(proj_made.sem, 1)

                for n in range(4):
                    project(n)
                pe.wait_ge(c_read.sem, c_read.of(b, 1))
                pe.matmul(p_c[:, 0:2 * D], core.ones[:, :],
                          core.bias_rows[:, BIAS_AT["L0_attn_bk"]:BIAS_AT["L0_attn_bk"] + 2 * D], start=True, stop=False)
                for t in range(KT):
                    mm = pe.matmul(p_c[:, 0:2 * D], entT[:, t, :, :].rearrange("p a c -> p (a c)"), w_c[:, t, :],
                                   start=False, stop=(t == KT - 1))
                mm.then_inc(c_made.sem, 1)
                for n in range(4, 12):
                    project(n)
                pe.wait_ge(c_up.sem, c_up.of(b, 2))
                pe.transpose(p_c[:, 0:P], crot[:, :], core.ident[:, :]).then_inc(c_made.sem, 1)
                for n in range(2 * NG):
                    j, g = n // NG, n % NG
                    if n == 0:
                        pe.wait_ge(q_rot.sem, q_rot.of(b))
                    if n == NG:
                        pe.wait_ge(k_normed.sem, k_normed.of(b))
                    if n:
                        pe.wait_ge(work_read.sem, work_read.of(b, n))
                    for h in range(G):
                        at = (g * G + h) * D
                        mm = pe.transpose(work[(n + 1) % 2][:, h * P:(h + 1) * P], rot[j][:, at:at + D], core.ident[:, :])
                    mm.then_inc(work_made.sem, 1)
                pe.wait_ge(work_read.sem, work_read.of(b, 1 + NG))
                pe.wait_ge(c_read.sem, c_read.of(b, 3))
                pe.matmul(p_c[:, :], core.identb[:, :], cmask[:, :, :].rearrange("p h c -> p (h c)"),
                          start=True, stop=False)
                for h in range(NH):
                    mm = pe.matmul(p_c[:, h * NC:(h + 1) * NC], qT[:, h, :], ckT[:, 0:NC],
                                   start=False, stop=(h == NH - 1))
                mm.then_inc(c_made.sem, 1)

                def scores(g):
                    if g == 0:
                        pe.wait_ge(work_read.sem, work_read.of(b))
                    if g >= 2:
                        pe.wait_ge(l_exp.sem, l_exp.of(b, g - 1))
                    bank = work[(9 + g) % 2]
                    pe.matmul(bank[:, :], core.identb[:, :], core.causal[:, :, :].rearrange("p g k -> p (g k)"),
                              start=True, stop=False)
                    for h in range(G):
                        mm = pe.matmul(bank[:, h * P:(h + 1) * P], qT[:, g * G + h, :], kT[:, g * G + h, :],
                                       start=False, stop=(h == G - 1))
                    mm.then_inc(work_made.sem, 1)

                def turn(g):
                    pe.wait_ge(l_prob.sem, l_prob.of(b, g + 1))
                    pe.wait_ge(pT_read.sem, pT_read.of(b, g))
                    for h in range(G):
                        mm = pe.transpose(p_pT[:, h * P:(h + 1) * P], prob[g % 2][:, h, :], core.ident[:, :])
                    mm.then_inc(pT_made.sem, 1)

                def context(g):
                    pe.wait_ge(pT_read.sem, pT_read.of(b, g + 1))
                    pe.wait_ge(cT_read.sem, cT_read.of(b, g))
                    if g == 0:
                        pe.wait_ge(proj_read.sem, proj_read.of(b, 12))
                        pe.wait_ge(c_read.sem, c_read.of(b, 4))
                    for h in range(G):
                        o = p_cT[:, h * P:(h + 1) * P]
                        at = (g * G + h) * D
                        pe.matmul(o, raw[2][:, at:at + D], pT[g % 2][:, h, :], start=(h == 0), stop=False)
                        mm = pe.matmul(o, cv[:, h, :], psT[:, g, :],
                                       start=False, stop=(h == G - 1))
                    mm.then_inc(cT_made.sem, 1)

                def output(g):
                    pe.wait_ge(cT_read.sem, cT_read.of(b, g + 1))
                    if g == 0:
                        pe.wait_ge(o_read.sem, o_read.of(b - 1))
                        pe.matmul(p_o[:, 0:H], core.ones[:, :], core.bias("L0_attn_bo"), start=True, stop=False)
                    for h in range(G):
                        mm = pe.matmul(p_o[:, 0:H], cT[g % 2][:, h, :], w_o[:, g * G + h, :],
                                       start=False, stop=(g == NG - 1 and h == G - 1))
                    if g == NG - 1:
                        mm.then_inc(o_made.sem, 1)

                scores(0)
                scores(1)
                pe.wait_ge(s_prob.sem, s_prob.of(b))
                for g in range(NG):
                    mm = pe.transpose(p_c[:, g * P:(g + 1) * P],
                                      es[:, g * G:(g + 1) * G, :].rearrange("p h c -> p (h c)"), core.ident[:, :])
                mm.then_inc(c_made.sem, 1)
                for g in range(NG):
                    turn(g)
                    if g + 2 < NG:
                        scores(g + 2)
                    context(g)
                    if g >= 1:
                        output(g - 1)
                output(NG - 1)

        @block.scalar
        def _(act):
            for c in (work_read, proj_read, c_read, s_exp, l_exp, pT_read, cT_read):
                c.open(act)
            act.wait_ge(tables, TABLES)
            with act.Fori(0, B) as b:
                act.wait_ge(work_made.sem, work_made.of(b, 1))
                act.wait_ge(proj_made.sem, proj_made.of(b - 1))
                act.copy(xT[:, :, :].rearrange("p t n -> p (t n)"), work[0][:, 0:KT * P]).then_inc(work_read.sem, 1)
                act.wait_ge(c_made.sem, c_made.of(b, 1))
                act.wait_ge(c_made.sem, c_made.of(b - 1, 2))
                for j in range(4):
                    i = act.copy(entT[:, :, j, :], p_c[:, 0:KT * NC].rearrange("p (t c) -> p t c", t=KT))
                i.then_inc(c_read.sem, 1)

                for n in range(12):
                    i, c = n // 4, n % 4
                    act.wait_ge(proj_made.sem, proj_made.of(b, n + 1))
                    if n == 0:
                        act.wait_ge(q_rot.sem, q_rot.of(b - 1))
                        act.wait_ge(squared.sem, squared.of(b - 1))
                    if n == 4:
                        act.wait_ge(k_rot.sem, k_rot.of(b - 1))
                        act.wait_ge(c_made.sem, c_made.of(b, 2))
                        act.wait_ge(cT_made.sem, cT_made.of(b - 1))
                        act.wait_ge(c_up.sem, c_up.of(b - 1, 2))
                        act.copy(ckr[:, :], p_c[:, 0:D])
                        for h in range(G):
                            q = slice(NC * h, NC * (h + 1))
                            last = act.copy(cv[q, h, :], p_c[q, D:2 * D])
                        last.then_inc(c_read.sem, 1)
                    if n == 8:
                        act.wait_ge(cT_made.sem, cT_made.of(b - 1))
                    act.copy(raw[i][:, c * BANK:(c + 1) * BANK], proj[n % 2][:, :]).then_inc(proj_read.sem, 1)
                act.wait_ge(c_made.sem, c_made.of(b, 3))
                act.copy(ckT[:, :], p_c[:, 0:P]).then_inc(c_read.sem, 1)
                for n in range(2 * NG):
                    act.wait_ge(work_made.sem, work_made.of(b, n + 2))
                    dst = (qT, kT)[n // NG][:, (n % NG) * G:(n % NG + 1) * G, :]
                    act.copy(dst.rearrange("p h t -> p (h t)"), work[(n + 1) % 2][:, :]).then_inc(work_read.sem, 1)
                act.wait_ge(s_arg.sem, s_arg.of(b))
                act.wait_ge(c_made.sem, c_made.of(b - 1))
                act.activation(es[:, :, :], scm[:, :, :], ACT.Exp).then_inc(s_exp.sem, 1)

                def exps(g):
                    act.wait_ge(bias_up.sem, bias_up.of(b, g + 1))
                    act.wait_ge(l_prob.sem, l_prob.of(b, g - 1) if g >= 1 else l_prob.of(b - 1, NG - 1))
                    act.wait_ge(pT_made.sem, pT_made.of(b, g - 1) if g >= 1 else pT_made.of(b - 1, NG - 1))
                    for h in range(G):
                        n = g * G + h
                        i = act.activation(prob[g % 2][:, h, :], work[(9 + g) % 2][:, h * P:(h + 1) * P], ACT.Exp,
                                           bias=nbias[:, n:n + 1], scale=rqs[:, n:n + 1],
                                           accum_out=lsum[:, n:n + 1])
                    i.then_inc(l_exp.sem, 1)

                def leave(g):
                    act.wait_ge(pT_made.sem, pT_made.of(b, g + 1))
                    act.wait_ge(cT_made.sem, cT_made.of(b, g - 1) if g >= 1 else cT_made.of(b - 1, NG - 1))
                    act.copy(pT[g % 2][:, :, :].rearrange("p g t -> p (g t)"), p_pT[:, :]).then_inc(pT_read.sem, 1)
                    act.wait_ge(cT_made.sem, cT_made.of(b, g + 1))
                    if g == 0:
                        act.wait_ge(o_made.sem, o_made.of(b - 1))
                    act.copy(cT[g % 2][:, :, :].rearrange("p g t -> p (g t)"), p_cT[:, :]).then_inc(cT_read.sem, 1)

                exps(0)
                exps(1)
                act.wait_ge(c_made.sem, c_made.of(b, 5))
                act.copy(psT[:, :, :].rearrange("p g t -> p (g t)"), p_c[:, :]).then_inc(c_read.sem, 1)
                for g in range(NG):
                    leave(g)
                    if g + 2 < NG:
                        exps(g + 2)

        @block.vector
        def _(dve):
            for c in (q_rot, k_rot, summed, c_up, c_sum, s_arg, s_prob, bias_up, l_prob, o_read, var_up, x_up):
                c.open(dve)
            dve.wait_ge(loaded, 16 * LOADS)
            for j, (cos, sin) in enumerate(((cq, sq_tab), (ck_tab, sk_tab), (cc, sc_tab))):
                w = wn[:, min(j, 1), :]
                dve.tensor_tensor(cos[:, :], cos[:, :], w, ALU.mult).then_inc(tables, 1)
                for lo, hi in ((0, ROPE // 2), (ROPE // 2, 0)):
                    dve.tensor_tensor(sin[:, lo:lo + ROPE // 2], sin[:, lo:lo + ROPE // 2],
                                      w[:, hi:hi + ROPE // 2], ALU.mult).then_inc(tables, 1)
            dve.memset(cv[:, :, :], 0.0).then_inc(tables, 1)
            dve.tensor_copy(cmask[:, :, :], over_heads(cmask_f[:, :], NH)).then_inc(tables, 1)
            dve.wait_ge(tables, TABLES)
            ch = Chain(dve, dve_steps, DVE_STEPS)

            def rotate(dst, hbuf, src, cos, sin, heads):
                d3 = dst.rearrange("p (h d) -> p h d", h=heads)
                s3 = src.rearrange("p (h d) -> p h d", h=heads)
                h3 = hbuf.rearrange("p (h d) -> p h d", h=heads)
                ch.mark(dve.tensor_tensor(d3, s3, over_heads(cos[:, :], heads), ALU.mult))
                for lo, hi in ((0, ROPE // 2), (ROPE // 2, 0)):
                    ch.mark(dve.tensor_tensor(h3[:, :, lo:lo + ROPE // 2], s3[:, :, hi:hi + ROPE // 2],
                                              over_heads(sin[:, lo:lo + ROPE // 2], heads), ALU.mult))
                ch.wait()
                return dve.tensor_tensor(d3[:, :, 0:ROPE], d3[:, :, 0:ROPE], h3, ALU.add)

            with dve.Fori(0, B) as b:
                ch.start(b)
                dve.wait_ge(c_made.sem, c_made.of(b - 1, 1))
                dve.tensor_scalar(wsel[:, :], member[:, :], wcol[:, bass.ds(b, 1)], None, ALU.mult).then_inc(c_up.sem, 1)
                dve.wait_ge(c_read.sem, c_read.of(b, 2))
                dve.wait_ge(c_made.sem, c_made.of(b - 1, 3))
                ch.link(dve.tensor_tensor_reduce(out=csq[:, :], in0=ckr[:, :], in1=ckr[:, :], scale=1.0, scalar=0.0,
                                                 op0=ALU.mult, op1=ALU.add, accum_out=cst[:, 0:1]))
                dve.tensor_scalar(cst[:, 1:2], cst[:, 0:1], 1.0 / D, RMS_EPS, ALU.mult, ALU.add).then_inc(c_sum.sem, 1)
                ch.link(rotate(crot[:, :], chalf[:, :], ckr[:, :], cc, sc_tab, 1))
                dve.wait_ge(rooted.sem, rooted.of(b, 1))
                dve.tensor_scalar(crot[:, :], crot[:, :], cst[:, 2:3], None, ALU.mult).then_inc(c_up.sem, 1)
                for j, (cos, sin, done) in enumerate(((cq, sq_tab, q_rot), (ck_tab, sk_tab, k_rot))):
                    dve.wait_ge(squared.sem, squared.of(b, j + 1))
                    if j == 0:
                        dve.wait_ge(rooted.sem, rooted.of(b - 1, 2))
                    dve.wait_ge(work_made.sem, work_made.of(b - 1, 5 + 4 * j))
                    ch.mark(dve.tensor_reduce(ssq[:, j * NH:(j + 1) * NH],
                                              sq[:, :].rearrange("p (h d) -> p h d", h=NH), AX.X, ALU.add))
                    rotate(rot[j][:, :], half[:, :], raw[j][:, :], cos, sin, NH).then_inc(done.sem, 1)
                    dve.wait_ge(done.sem, done.of(b))
                dve.tensor_scalar(ssq[:, :], ssq[:, :], 1.0 / D, RMS_EPS, ALU.mult, ALU.add).then_inc(summed.sem, 1)
                dve.wait_ge(rooted.sem, rooted.of(b, 2))
                dve.wait_ge(l_exp.sem, l_exp.of(b - 1))
                ch.link(dve.tensor_scalar(rqs[:, :], rstd[:, 0:NH], float(D) ** -0.5, None, ALU.mult))
                dve.wait_ge(c_made.sem, c_made.of(b, 4))
                dve.wait_ge(s_exp.sem, s_exp.of(b - 1))
                ch.link(dve.tensor_copy(scm[:, :, :].rearrange("p h c -> p (h c)"), p_c[:, :]))
                for h in range(NH):
                    if h == 0:
                        ch.settle()
                    ch.mark(dve.max(top[:, h, :], scm[:, h, :]))
                ch.wait()
                ch.settle()
                for h in range(NH):
                    ch.mark(dve.match_replace(repl[:, h, :], top[:, h, :], scm[:, h, :], CHOSEN))
                ch.link(dve.tensor_scalar(tmax[:, :], top[:, :, 0], NEG / 2, None, ALU.max))
                ch.link(dve.tensor_tensor(scm[:, :, :], scm[:, :, :], bcast(tmax[:, :], [P, NH, NC]), ALU.subtract))
                dve.tensor_tensor(scm[:, :, :], scm[:, :, :], bcast(rqs[:, :], [P, NH, NC]), ALU.mult).then_inc(s_arg.sem, 1)
                dve.wait_ge(s_exp.sem, s_exp.of(b))
                ch.link(dve.scalar_tensor_tensor(out=es[:, :, :].rearrange("p h c -> p (h c)"),
                                                 in0=repl[:, :, :].rearrange("p h c -> p (h c)"), scalar=CHOSEN,
                                                 in1=es[:, :, :].rearrange("p h c -> p (h c)"),
                                                 op0=ALU.is_ge, op1=ALU.mult))
                ch.link(dve.tensor_reduce(tsum[:, :], es[:, :, :], AX.X, ALU.add))
                ch.link(dve.tensor_scalar(tsum[:, :], tsum[:, :], 1e-9, None, ALU.max))
                ch.link(dve.reciprocal(tmax[:, :], tsum[:, :]))
                dve.scalar_tensor_tensor(out=es[:, :, :], in0=es[:, :, :], scalar=0.5,
                                         in1=bcast(tmax[:, :], [P, NH, NC]), op0=ALU.mult,
                                         op1=ALU.mult).then_inc(s_prob.sem, 1)

                def row_max(g):
                    dve.wait_ge(work_made.sem, work_made.of(b, 10 + g))
                    hs = slice(g * G, (g + 1) * G)
                    ch.link(dve.tensor_reduce(lmax[:, hs], work[(9 + g) % 2][:, :].rearrange("p (h k) -> p h k", h=G),
                                              AX.X, ALU.max))
                    dve.scalar_tensor_tensor(out=nbias[:, hs], in0=lmax[:, hs], scalar=-1.0, in1=rqs[:, hs],
                                             op0=ALU.mult, op1=ALU.mult).then_inc(bias_up.sem, 1)

                def normalize(g):
                    hs = slice(g * G, (g + 1) * G)
                    dve.wait_ge(l_exp.sem, l_exp.of(b, g + 1))
                    ch.link(dve.reciprocal(lrec[:, hs], lsum[:, hs]))
                    dve.scalar_tensor_tensor(out=prob[g % 2][:, :, :], in0=prob[g % 2][:, :, :], scalar=0.5,
                                             in1=bcast(lrec[:, hs], [P, G, P]), op0=ALU.mult,
                                             op1=ALU.mult).then_inc(l_prob.sem, 1)

                row_max(0)
                row_max(1)
                for g in range(NG):
                    normalize(g)
                    if g + 2 < NG:
                        row_max(g + 2)
                xt = core.x[:, bass.ds(b, 1), :].rearrange("p o h -> p (o h)")
                dve.wait_ge(o_made.sem, o_made.of(b))
                dve.tensor_tensor(y[:, :], p_o[:, 0:H], xt, ALU.add).then_inc(o_read.sem, 1)
                dve.wait_ge(o_read.sem, o_read.of(b))
                ch.link(dve.bn_stats(stats[:, :], y[:, :]))
                ch.settle()
                ch.link(dve.bn_aggr(mv[:, :], stats[:, :]))
                dve.tensor_scalar(mv[:, 1:2], mv[:, 1:2], LN_EPS, None, ALU.add).then_inc(var_up.sem, 1)
                dve.wait_ge(rooted.sem, rooted.of(b, 3))
                dve.tensor_scalar(xt, y[:, :], mv[:, 0:1], ln_r[:, 0:1], ALU.subtract, ALU.mult).then_inc(x_up.sem, 1)
                dve.wait_ge(x_up.sem, x_up.of(b))
                ch.end()


def l0_token_weights(core, wcol):
    nc, A = core.nc, core.A
    with ExitStack() as ctx:
        def sb(name, shape, dt=F32):
            return ctx.enter_context(nc.sbuf_tensor(name, shape, dt))

        wcmp = sb("w0_wcmp", [P, H])
        bcmp = sb("w0_bcmp", [P, 1])
        prod = sb("w0_prod", [P, B, H])
        logit = sb("w0_logit", [P, B])
        shifted = sb("w0_shifted", [B, P])
        grown = sb("w0_grown", [B, P])
        stat = sb("w0_stat", [B, 3, NC])
        turned = ctx.enter_context(nc.psum_tensor("w0_turned", [B, P], F32))
        back = ctx.enter_context(nc.psum_tensor("w0_back", [P, B], F32))
        sem = semaphores(nc, ctx)
        loaded, steps, turns, exped = (sem("w0_" + n)
                                       for n in ("loaded", "steps", "turns", "exped"))
        block = ctx.enter_context(nc.Block())

        @block.sync
        def _(sp):
            sp.dma_start(wcmp[:, :], A["L0_attn_Wcmp"].rearrange("h o -> (h o)").partition_broadcast(P)).then_inc(loaded, 16)
            sp.dma_start(bcmp[:, :], A["L0_attn_bcmp"].partition_broadcast(P)).then_inc(loaded, 16)
            sp.wait_ge(loaded, 32)

        @block.vector
        def _(dve):
            ch = Chain(dve, steps, 9)
            ch.start(0)
            dve.wait_ge(loaded, 32)
            ch.link(dve.tensor_tensor(prod[:, :, :], core.x[:, :, :], over_heads(wcmp[:, :], B), ALU.mult))
            ch.link(dve.tensor_reduce(logit[:, :], prod[:, :, :], AX.X, ALU.add))
            ch.link(dve.tensor_scalar(logit[:, :], logit[:, :], bcmp[:, 0:1], None, ALU.add))
            dve.wait_ge(turns, 1)
            logits = turned[:, :].rearrange("b (c r) -> b c r", r=RATIO)
            ch.link(dve.tensor_reduce(stat[:, 0, :], logits, AX.X, ALU.max))
            ch.link(dve.tensor_tensor(shifted[:, :].rearrange("b (c r) -> b c r", r=RATIO), logits,
                                      bcast(stat[:, 0, :], [B, NC, RATIO]), ALU.subtract))
            dve.wait_ge(exped, 1)
            g3 = grown[:, :].rearrange("b (c r) -> b c r", r=RATIO)
            ch.link(dve.tensor_reduce(stat[:, 1, :], g3, AX.X, ALU.add))
            ch.link(dve.reciprocal(stat[:, 2, :], stat[:, 1, :]))
            ch.link(dve.tensor_tensor(g3, g3, bcast(stat[:, 2, :], [B, NC, RATIO]), ALU.mult))
            dve.wait_ge(turns, 2)
            ch.link(dve.tensor_copy(wcol[:, :], back[:, :]))
            ch.end()

        @block.scalar
        def _(act):
            act.wait_ge(steps, 5)
            act.activation(grown[:, :], shifted[:, :], ACT.Exp).then_inc(exped, 1)

        @block.tensor
        def _(pe):
            pe.wait_ge(steps, 3)
            pe.transpose(turned[:, :], logit[:, :], core.ident[:, :]).then_inc(turns, 1)
            pe.wait_ge(steps, 8)
            pe.transpose(back[:, :], grown[:, :], core.ident[0:B, 0:B]).then_inc(turns, 1)


XH, XD = 16, 16
PAIRS = XH // 2
ROUND = 1.5 * 2.0 ** 23
QMAX = 127.0
AMAX = 255.0
FLOOR = 1e-8


def norm_steps(dve, ch, core, b, y, stats, mv, ln_r, made, p_y, read, var_up, rooted, root_k, x_up):
    xt = core.x[:, bass.ds(b, 1), :].rearrange("p o h -> p (o h)")
    dve.wait_ge(made.sem, made.of(b))
    dve.tensor_tensor(y[:, :], p_y, xt, ALU.add).then_inc(read.sem, 1)
    dve.wait_ge(read.sem, read.of(b))
    ch.link(dve.bn_stats(stats[:, :], y[:, :]))
    ch.settle()
    ch.link(dve.bn_aggr(mv[:, :], stats[:, :]))
    dve.tensor_scalar(mv[:, 1:2], mv[:, 1:2], LN_EPS, None, ALU.add).then_inc(var_up.sem, 1)
    dve.wait_ge(rooted.sem, rooted.of(b, root_k))
    dve.tensor_scalar(xt, y[:, :], mv[:, 0:1], ln_r[:, 0:1], ALU.subtract, ALU.mult).then_inc(x_up.sem, 1)
    dve.wait_ge(x_up.sem, x_up.of(b))


def l0_cross_attention(core):
    nc = core.nc
    with ExitStack() as ctx:
        def sb(name, shape, dt=F32):
            return ctx.enter_context(nc.sbuf_tensor("x0_" + name, shape, dt))

        qz = sb("qz", [P, 2, PAIRS, B, P], BF16)
        kT = sb("kT", [P, PAIRS, B * P], BF16)
        vi = sb("vi", [P, B, H], BF16)
        sv = sb("sv", [P, H])
        sq = sb("sq", [P, B, XH])
        att = sb("att", [P, B, H])
        esum = sb("esum", [P, PAIRS, B, 2, 2])
        x0_operands(core, qz, kT, vi, sv, sq, att)
        x0_attend(core, qz, kT, vi, sq, att, esum)
        x0_output(core, sv, att, esum)


def x0_operands(core, qz, kT, vi, sv, sq, vraw):
    nc, A = core.nc, core.A
    with ExitStack() as ctx:
        def sb(name, shape, dt=F32):
            return ctx.enter_context(nc.sbuf_tensor("x1_" + name, shape, dt))

        def ps(name, shape, dt=F32):
            return ctx.enter_context(nc.psum_tensor("x1_" + name, shape, dt))

        named = semaphores(nc, ctx)

        def sem(name):
            return named("x1_" + name)

        def count(name, per):
            return Count(sem(name), per)

        wq = sb("wq", [P, KT, H])
        wkv = sb("wkv", [P, KT, 2 * H])
        xb, cb = sb("xb", [P, H]), sb("cb", [P, H])
        inT = sb("inT", [P, 2 * KT, P])
        kq = sb("kq", [P, 2, H])
        amax, scl, rec = (sb(n, [P, 2 * XH]) for n in ("amax", "scl", "rec"))
        kval = sb("kval", [P, H])
        krep = sb("krep", [P, XH, 4, XD], BF16)
        qrep = sb("qrep", [P, XH, 4, XD], BF16)
        cmax = sb("cmax", [P, H])
        vstat = sb("vstat", [P, 2, KT])
        svcol = sb("svcol", [P, KT, P])
        rsv = sb("rsv", [P, H])
        p_in, p_kv, p_q = (ps(n, [P, BANK]) for n in ("p_in", "p_kv", "p_q"))
        p_kT, p_qT = (ps(n, [P, 2 * BANK], BF16) for n in ("p_kT", "p_qT"))
        p_v = ps("p_v", [P, BANK])

        loaded, zeroed = sem("loaded"), sem("zeroed")
        ctx_in = count("ctx_in", 16)
        tile_in = count("tile_in", 1)
        turned, in_up = count("turned", 1), count("in_up", 1)
        made, read = count("made", 2), count("read", 2)
        reps = count("reps", 1)
        rep_made, rep_read = count("rep_made", 1), count("rep_read", 2)
        steps = sem("steps")
        v_steps, v_turn = sem("v_steps"), sem("v_turn")
        DVE_STEPS = 12
        block = ctx.enter_context(nc.Block())

        @block.sync
        def _(sp):
            ctx_in.open(sp)
            sp.dma_start(wq[:, :, :], A["L0_xattn_Wq"].rearrange("(t p) n -> p t n", p=P)).then_inc(loaded, 16)
            sp.dma_start(wkv[:, :, :], A["L0_xattn_Wkv"].rearrange("(t p) n -> p t n", p=P)).then_inc(loaded, 16)
            with sp.Fori(0, B) as b:
                sp.wait_ge(turned.sem, turned.of(b - 1))
                sp.dma_start(cb[:, :], A["ctx_2048"][bass.ds(b, 1), :, :].rearrange("o p h -> (o p) h")).then_inc(ctx_in.sem, 16)
            sp.wait_ge(ctx_in.sem, ctx_in.of(B - 1))
            sp.wait_ge(loaded, 32)

        @block.gpsimd
        def _(pool):
            tile_in.open(pool)
            pool.memset(qz[XD * 4:P, 0, :, :, :].rearrange("p a b t -> p (a b t)"), 0.0).then_inc(zeroed, 1)
            pool.wait_ge(zeroed, 1)
            pool.memset(qz[0:XD * 4, 1, :, :, :].rearrange("p a b t -> p (a b t)"), 0.0).then_inc(zeroed, 1)
            pool.wait_ge(zeroed, 2)
            with pool.Fori(0, B) as b:
                pool.wait_ge(turned.sem, turned.of(b - 1))
                pool.tensor_copy(xb[:, :], core.x[:, bass.ds(b, 1), :].rearrange("p o h -> p (o h)")).then_inc(tile_in.sem, 1)

        @block.tensor
        def _(pe):
            for c in (turned, made, rep_made):
                c.open(pe)
            pe.wait_ge(loaded, 32)
            with pe.Fori(0, B) as b:
                pe.wait_ge(tile_in.sem, tile_in.of(b))
                pe.wait_ge(ctx_in.sem, ctx_in.of(b))
                pe.wait_ge(in_up.sem, in_up.of(b - 1))
                for t in range(KT):
                    pe.transpose(p_in[:, t * P:(t + 1) * P], xb[:, t * P:(t + 1) * P], core.ident[:, :])
                for t in range(KT):
                    mm = pe.transpose(p_in[:, (KT + t) * P:(KT + t + 1) * P], cb[:, t * P:(t + 1) * P], core.ident[:, :])
                mm.then_inc(turned.sem, 1)
                pe.wait_ge(in_up.sem, in_up.of(b))
                for j, (bank, w, name, n) in enumerate(((p_kv, wkv, "L0_xattn_bkv", 2 * H), (p_q, wq, "L0_xattn_bq", H))):
                    pe.wait_ge(read.sem, read.of(b - 1, j + 1))
                    pe.matmul(bank[:, 0:n], core.ones[:, :], core.bias(name), start=True, stop=False)
                    for t in range(KT):
                        mm = pe.matmul(bank[:, 0:n], inT[:, (1 - j) * KT + t, :], w[:, t, :],
                                       start=False, stop=(t == KT - 1))
                    mm.then_inc(made.sem, 1)
                pe.wait_ge(reps.sem, reps.of(b))
                pe.wait_ge(rep_read.sem, rep_read.of(b - 1))
                for bank, src in ((p_kT, krep), (p_qT, qrep)):
                    for h in range(PAIRS):
                        mm = pe.transpose(bank[:, h * P:(h + 1) * P],
                                          src[:, 2 * h:2 * h + 2, :, :].rearrange("p a c d -> p (a c d)"), core.identb[:, :])
                mm.then_inc(rep_made.sem, 1)
            pe.wait_ge(v_steps, 1)
            for t in range(KT):
                mm = pe.transpose(p_v[:, t * P:(t + 1) * P], cmax[:, t * P:(t + 1) * P], core.ident[:, :])
            mm.then_inc(v_turn, 1)
            pe.wait_ge(v_steps, 4)
            for t in range(KT):
                mm = pe.matmul(p_v[:, t * P:(t + 1) * P], svcol[:, t, :], core.ident[:, :], start=True, stop=True)
            mm.then_inc(v_turn, 1)

        @block.scalar
        def _(act):
            for c in (in_up, read, rep_read):
                c.open(act)
            act.wait_ge(zeroed, 2)
            with act.Fori(0, B) as b:
                act.wait_ge(turned.sem, turned.of(b))
                act.wait_ge(made.sem, made.of(b - 1))
                act.copy(inT[:, :, :].rearrange("p t n -> p (t n)"), p_in[:, :]).then_inc(in_up.sem, 1)
                act.wait_ge(made.sem, made.of(b, 1))
                act.wait_ge(reps.sem, reps.of(b - 1))
                act.copy(kq[:, 0, :], p_kv[:, 0:H])
                act.copy(vraw[:, bass.ds(b, 1), :].rearrange("p o h -> p (o h)"), p_kv[:, H:2 * H]).then_inc(read.sem, 1)
                act.wait_ge(made.sem, made.of(b, 2))
                act.mul(kq[:, 1, :], p_q[:, 0:H], float(XD) ** -0.5).then_inc(read.sem, 1)
                act.wait_ge(rep_made.sem, rep_made.of(b))
                for par in range(2):
                    r = slice(64 * par, 64 * par + 64)
                    i = act.copy(qz[r, par, :, bass.ds(b, 1), :].rearrange("p a o t -> p a (o t)"),
                                 p_qT[r, :].rearrange("p (a t) -> p a t", a=PAIRS))
                i.then_inc(rep_read.sem, 1)
                act.copy(kT[:, :, bass.ds(b * P, P)], p_kT[:, :].rearrange("p (a t) -> p a t", a=PAIRS)).then_inc(rep_read.sem, 1)
            act.wait_ge(rep_read.sem, rep_read.of(B - 1))

        @block.vector
        def _(dve):
            reps.open(dve)
            dve.memset(krep[:, :, 3, :], 0.0)
            dve.memset(qrep[:, :, 3, :], 0.0)
            ch = Chain(dve, steps, DVE_STEPS)
            kq3 = kq[:, :, :].rearrange("p j (h d) -> p (j h) d", d=XD)
            kv3 = kval[:, :].rearrange("p (h d) -> p h d", d=XD)
            with dve.Fori(0, B) as b:
                ch.start(b)
                dve.wait_ge(read.sem, read.of(b))
                ch.link(dve.tensor_reduce(amax[:, :], kq3, AX.X, ALU.max, apply_absolute_value=True))
                ch.link(dve.tensor_scalar(scl[:, :], amax[:, :], 1.0 / QMAX, FLOOR, ALU.mult, ALU.max))
                ch.mark(dve.reciprocal(rec[:, :], scl[:, :]))
                ch.link(dve.tensor_copy(sq[:, bass.ds(b, 1), :].rearrange("p o h -> p (o h)"), scl[:, XH:]))
                ch.link(dve.tensor_tensor(kq3, kq3, bcast(rec[:, :], [P, 2 * XH, XD]), ALU.mult))
                ch.link(dve.tensor_scalar(kq[:, :, :], kq[:, :, :], ROUND, ROUND, ALU.add, ALU.subtract))
                dve.wait_ge(rep_made.sem, rep_made.of(b - 1))
                ch.mark(dve.tensor_tensor(kv3, kq3[:, 0:XH, :], bcast(scl[:, 0:XH], [P, XH, XD]), ALU.mult))
                ch.mark(dve.tensor_copy(qrep[:, :, 0:3, :],
                                        kq3[:, XH:, :].unsqueeze(2).to_broadcast([P, XH, 3, XD])))
                ch.wait()
                for j in range(3):
                    i = dve.tensor_copy(krep[:, :, j, :], kv3)
                    if j < 2:
                        ch.link(i)
                        i = dve.tensor_tensor(kv3, kv3, krep[:, :, j, :], ALU.subtract)
                        ch.link(i)
                    else:
                        i.then_inc(reps.sem, 1)
                ch.end()
            dve.wait_ge(read.sem, read.of(B - 1))
            dve.tensor_reduce(cmax[:, :], vraw[:, :, :].rearrange("p b h -> p h b"), AX.X, ALU.max,
                              apply_absolute_value=True).then_inc(v_steps, 1)
            dve.wait_ge(v_turn, 1)
            dve.tensor_reduce(vstat[:, 0, :], p_v[:, 0:H].rearrange("p (t n) -> p t n", t=KT), AX.X, ALU.max).then_inc(v_steps, 1)
            dve.wait_ge(v_steps, 2)
            dve.tensor_scalar(vstat[:, 1, :], vstat[:, 0, :], 1.0 / QMAX, FLOOR, ALU.mult, ALU.max).then_inc(v_steps, 1)
            dve.wait_ge(v_steps, 3)
            dve.tensor_copy(svcol[:, :, :], bcast(vstat[:, 1, :], [P, KT, P])).then_inc(v_steps, 1)
            dve.wait_ge(v_turn, 2)
            dve.tensor_copy(sv[:, :], p_v[:, 0:H]).then_inc(v_steps, 1)
            dve.wait_ge(v_steps, 5)
            dve.reciprocal(rsv[:, :], sv[:, :]).then_inc(v_steps, 1)
            dve.wait_ge(v_steps, 6)
            dve.tensor_tensor(vraw[:, :, :], vraw[:, :, :], over_heads(rsv[:, :], B), ALU.mult).then_inc(v_steps, 1)
            dve.wait_ge(v_steps, 7)
            dve.tensor_scalar(vi[:, :, :], vraw[:, :, :], ROUND, ROUND, ALU.add, ALU.subtract).then_inc(v_steps, 1)
            dve.wait_ge(v_steps, 8)


def x0_attend(core, qz, kT, vi, sq, att, esum):
    nc = core.nc
    HALF = B * P // 2
    LOG_AMAX = float(np.log(AMAX))
    with ExitStack() as ctx:
        def sb(name, shape, dt=F32):
            return ctx.enter_context(nc.sbuf_tensor("x2_" + name, shape, dt))

        def ps(name, shape, dt=F32):
            return ctx.enter_context(nc.psum_tensor("x2_" + name, shape, dt))

        sem = semaphores(nc, ctx)

        def count(name, per):
            return Count(sem("x2_" + name), per)

        ints = [sb(f"ints{i}", [P, 2, HALF], U16) for i in range(2)]
        turned = [sb(f"turned{i}", [P, B, P], BF16) for i in range(2)]
        hmax = sb("hmax", [P, 2, 2])
        top = sb("top", [P, 2])
        nb = sb("nb", [P, 2])
        p_s = [ps(f"p_s{i}", [P, HALF]) for i in range(2)]
        p_t = [ps(f"p_t{i}", [P, HALF], BF16) for i in range(2)]
        p_o = [ps(f"p_o{i}", [P, BANK]) for i in range(2)]

        s_made = count("s_made", 4)
        max_up = count("max_up", 4)
        top_up = count("top_up", 2)
        bias_up = count("bias_up", 2)
        e_up = count("e_up", 4)
        t_made = count("t_made", 4)
        t_act = count("t_act", 2)
        t_dve = count("t_dve", 2)
        o_made = count("o_made", 2)
        o_read = count("o_read", 2)
        block = ctx.enter_context(nc.Block())

        def walk(eng, emit):
            emit((0, 0, 0), None)
            with eng.Fori(1, B) as t:
                emit((0, t, t), (0, t - 1, t - 1))
            with eng.Fori(1, PAIRS) as a:
                emit((a, 0, a * B), (a - 1, B - 1, a * B - 1))
                with eng.Fori(1, B) as t:
                    emit((a, t, a * B + t), (a, t - 1, a * B + t - 1))
            emit(None, (PAIRS - 1, B - 1, PAIRS * B - 1))

        def halves(now, before):
            for par in range(2):
                here = now and (*now, par)
                last = (*before, 1) if par == 0 and before else (*now, 0) if par == 1 and now else None
                if here or last:
                    yield here, last

        @block.tensor
        def _(pe):
            for c in (s_made, t_made, o_made):
                c.open(pe)

            def scores(a, t, n, par, half):
                pe.wait_ge(e_up.sem, e_up.of(n, half + 1) if par else e_up.of(n - 1, 3 + half))
                for c in range(2):
                    mm = pe.matmul(p_s[half][:, c * BANK:(c + 1) * BANK],
                                   qz[:, par, bass.ds(a, 1), bass.ds(t, 1), :].rearrange("p a t n -> p (a t n)"),
                                   kT[:, bass.ds(a, 1), half * HALF + c * BANK:half * HALF + (c + 1) * BANK].rearrange("p a n -> p (a n)"),
                                   start=True, stop=True)
                mm.then_inc(s_made.sem, 1)

            def turn(a, t, n, par, half):
                pe.wait_ge(e_up.sem, e_up.of(n, 2 * par + half + 1))
                freed = t_dve if half else t_act
                pe.wait_ge(freed.sem, freed.of(n, 1) if par else freed.of(n - 1))
                for c in range(8):
                    mm = pe.transpose(p_t[half][:, c * P:(c + 1) * P],
                                      ints[par][:, half, c * P:(c + 1) * P].bitcast(BF16), core.identb[:, :])
                mm.then_inc(t_made.sem, 1)

            def values(a, t, n, par):
                pe.wait_ge(o_read.sem, o_read.of(n - 1, par + 1))
                for half, freed in enumerate((t_act, t_dve)):
                    pe.wait_ge(freed.sem, freed.of(n, par + 1))
                    for c in range(8):
                        k = 8 * half + c
                        mm = pe.matmul(p_o[par][:, 0:XD], turned[par][:, k, :],
                                       vi[:, k, bass.ds(a * (2 * XD) + par * XD, XD)],
                                       start=(k == 0), stop=(k == 15))
                mm.then_inc(o_made.sem, 1)

            def emit(now, before):
                for here, last in halves(now, before):
                    for half in range(2):
                        if here:
                            scores(*here, half)
                        if last:
                            turn(*last, half)
                    if last:
                        values(*last)

            walk(pe, emit)

        @block.scalar
        def _(act):
            for c in (e_up, t_act):
                c.open(act)

            def leave(a, t, n, par):
                act.wait_ge(t_made.sem, t_made.of(n, 2 * par + 1))
                act.wait_ge(o_made.sem, o_made.of(n - 1, par + 1))
                act.copy(turned[par][:, 0:8, :].rearrange("p k n -> p (k n)"), p_t[0][:, :].bitcast(U16)).then_inc(t_act.sem, 1)

            def exps(a, t, n, par):
                act.wait_ge(bias_up.sem, bias_up.of(n, par + 1))
                act.wait_ge(t_made.sem, t_made.of(n - 1, 2 * par + 2))
                for half in range(2):
                    act.activation(ints[par][:, half, :], p_s[half][:, :], ACT.Exp, bias=nb[:, par:par + 1],
                                   scale=sq[:, bass.ds(t, 1), bass.ds(2 * a + par, 1)].rearrange("p t h -> p (t h)"),
                                   accum_out=esum[:, bass.ds(a, 1), bass.ds(t, 1), par, half:half + 1].rearrange("p a t o -> p (a t o)")
                                   ).then_inc(e_up.sem, 1)

            def emit(now, before):
                for here, last in halves(now, before):
                    if last:
                        leave(*last)
                    if here:
                        exps(*here)

            walk(act, emit)

        @block.vector
        def _(dve):
            for c in (max_up, top_up, bias_up, t_dve, o_read):
                c.open(dve)

            def row_max(a, t, n, par):
                for half in range(2):
                    dve.wait_ge(s_made.sem, s_made.of(n, 2 * par + half + 1))
                    dve.tensor_reduce(hmax[:, par, half:half + 1], p_s[half][:, :], AX.X, ALU.max).then_inc(max_up.sem, 1)
                dve.wait_ge(max_up.sem, max_up.of(n, 2 * par + 2))
                dve.tensor_scalar(top[:, par:par + 1], hmax[:, par, 0:1], hmax[:, par, 1:2],
                                  sq[:, bass.ds(t, 1), bass.ds(2 * a + par, 1)].rearrange("p t h -> p (t h)"),
                                  ALU.max, ALU.mult).then_inc(top_up.sem, 1)
                dve.wait_ge(top_up.sem, top_up.of(n, par + 1))
                dve.wait_ge(e_up.sem, e_up.of(n - 1, 2 * par + 2))
                dve.tensor_scalar(nb[:, par:par + 1], top[:, par:par + 1], -1.0, LOG_AMAX, ALU.mult, ALU.add).then_inc(bias_up.sem, 1)

            def leave(a, t, n, par):
                dve.wait_ge(t_made.sem, t_made.of(n, 2 * par + 2))
                dve.wait_ge(o_made.sem, o_made.of(n - 1, par + 1))
                dve.tensor_copy(turned[par][:, 8:16, :].rearrange("p k n -> p (k n)"), p_t[1][:, :].bitcast(U16)).then_inc(t_dve.sem, 1)
                dve.wait_ge(o_made.sem, o_made.of(n, par + 1))
                dve.tensor_copy(att[:, bass.ds(t, 1), bass.ds(a * (2 * XD) + par * XD, XD)].rearrange("p t d -> p (t d)"),
                                p_o[par][:, 0:XD]).then_inc(o_read.sem, 1)

            def emit(now, before):
                for here, last in halves(now, before):
                    if here:
                        row_max(*here)
                    if last:
                        leave(*last)

            walk(dve, emit)


def x0_output(core, sv, att, esum):
    nc, A = core.nc, core.A
    with ExitStack() as ctx:
        def sb(name, shape, dt=F32):
            return ctx.enter_context(nc.sbuf_tensor("x3_" + name, shape, dt))

        def ps(name, shape, dt=F32):
            return ctx.enter_context(nc.psum_tensor("x3_" + name, shape, dt))

        sem = semaphores(nc, ctx)

        def count(name, per):
            return Count(sem("x3_" + name), per)

        wp = sb("wp", [P, KT, H])
        den, rden = sb("den", [P, XH]), sb("rden", [P, XH])
        o = sb("o", [P, H])
        oT = sb("oT", [P, KT, P])
        y, stats, mv, ln_r = sb("y", [P, H]), sb("stats", [P, 6]), sb("mv", [P, 2]), sb("ln_r", [P, 1])
        p_oT, p_y = ps("p_oT", [P, BANK]), ps("p_y", [P, BANK])
        loaded = sem("x3_loaded")
        steps = sem("x3_steps")
        o_up, turned, oT_up = count("o_up", 1), count("turned", 1), count("oT_up", 1)
        made, read = count("made", 1), count("read", 1)
        var_up, rooted, x_up = count("var_up", 1), count("rooted", 1), count("x_up", 1)
        block = ctx.enter_context(nc.Block())

        @block.sync
        def _(sp):
            sp.dma_start(wp[:, :, :], A["L0_xattn_Wp"].rearrange("(t p) n -> p t n", p=P)).then_inc(loaded, 16)
            sp.wait_ge(loaded, 16)

        @block.gpsimd
        def _(pool):
            rooted.open(pool)
            with pool.Fori(0, B) as b:
                pool.wait_ge(var_up.sem, var_up.of(b))
                pool.tensor_tensor(ln_r[:, :], mv[:, 1:2], core.neghalf[:, 0:1], ALU.pow).then_inc(rooted.sem, 1)

        @block.tensor
        def _(pe):
            turned.open(pe)
            made.open(pe)
            pe.wait_ge(loaded, 16)
            with pe.Fori(0, B) as b:
                pe.wait_ge(o_up.sem, o_up.of(b))
                pe.wait_ge(oT_up.sem, oT_up.of(b - 1))
                for t in range(KT):
                    mm = pe.transpose(p_oT[:, t * P:(t + 1) * P], o[:, t * P:(t + 1) * P], core.ident[:, :])
                mm.then_inc(turned.sem, 1)
                pe.wait_ge(oT_up.sem, oT_up.of(b))
                pe.wait_ge(read.sem, read.of(b - 1))
                pe.matmul(p_y[:, 0:H], core.ones[:, :], core.bias("L0_xattn_bp"), start=True, stop=False)
                for t in range(KT):
                    mm = pe.matmul(p_y[:, 0:H], oT[:, t, :], wp[:, t, :], start=False, stop=(t == KT - 1))
                mm.then_inc(made.sem, 1)

        @block.scalar
        def _(act):
            oT_up.open(act)
            with act.Fori(0, B) as b:
                act.wait_ge(turned.sem, turned.of(b))
                act.wait_ge(made.sem, made.of(b - 1))
                act.copy(oT[:, :, :].rearrange("p t n -> p (t n)"), p_oT[:, 0:H]).then_inc(oT_up.sem, 1)

        @block.vector
        def _(dve):
            for c in (o_up, read, var_up, x_up):
                c.open(dve)
            ch = Chain(dve, steps, 6)
            with dve.Fori(0, B) as b:
                ch.start(b)
                dve.wait_ge(turned.sem, turned.of(b - 1))
                ch.link(dve.tensor_reduce(den[:, :].rearrange("p (a c) -> p a c", c=2),
                                          esum[:, :, bass.ds(b, 1), :, :].rearrange("p a o c k -> p (a o) c k"), AX.X, ALU.add))
                ch.link(dve.reciprocal(rden[:, :], den[:, :]))
                ch.link(dve.tensor_tensor(o[:, :].rearrange("p (h d) -> p h d", d=XD),
                                          att[:, bass.ds(b, 1), :].rearrange("p o (h d) -> p (o h) d", d=XD),
                                          bcast(rden[:, :], [P, XH, XD]), ALU.mult))
                dve.tensor_tensor(o[:, :], o[:, :], sv[:, :], ALU.mult).then_inc(o_up.sem, 1)
                norm_steps(dve, ch, core, b, y, stats, mv, ln_r, made, p_y[:, 0:H], read, var_up, rooted, 1, x_up)
                ch.end()


def small_attention(core, tag, heads, wqkv, wo, causal, source=None, biases=None, norms=None, bias_o=None):
    nc, A = core.nc, core.A
    dk = H // heads
    per_tile = P // dk
    NG = heads // G
    inputs = 2 if source else 1
    with ExitStack() as ctx:
        def sb(name, shape, dt=F32):
            return ctx.enter_context(nc.sbuf_tensor(f"{tag}_{name}", shape, dt))

        def ps(name, shape, dt=F32):
            return ctx.enter_context(nc.psum_tensor(f"{tag}_{name}", shape, dt))

        named = semaphores(nc, ctx)

        def sem(name):
            return named(f"{tag}_{name}")

        def count(name, per):
            return Count(sem(name), per)

        w = sb("w", [P, KT, 3 * H])
        w_o = sb("w_o", [P, KT, H])
        owner = sb("owner", [P, per_tile])
        gains = sb("gains", [P, 2, H])
        xb, cb = sb("xb", [P, H]), sb("cb", [P, H])
        inT = sb("inT", [P, inputs * KT, P])
        qk = sb("qk", [P, 2, H])
        vaug = sb("vaug", [P, heads, dk + 1])
        sq, ssq, rstd = sb("sq", [P, 2, H]), sb("ssq", [P, 2]), sb("rstd", [P, 2])
        qkT = sb("qkT", [P, 2, KT, P])
        kz = sb("kz", [P, KT, per_tile, P])
        rmax = sb("rmax", [P, heads])
        e = [sb(f"e{i}", [P, G, P]) for i in range(2)]
        eT = [sb(f"eT{i}", [P, G, P]) for i in range(2)]
        rden = sb("rden", [P, heads])
        o = sb("o", [P, H])
        oT = sb("oT", [P, KT, P])
        y, stats, mv, ln_r = sb("y", [P, H]), sb("stats", [P, 6]), sb("mv", [P, 2]), sb("ln_r", [P, 1])
        p_in, p_qk, p_v, p_e, p_o, p_y = (ps(n, [P, BANK]) for n in ("p_in", "p_qk", "p_v", "p_e", "p_o", "p_y"))
        p_s = [ps(f"p_s{i}", [P, BANK]) for i in range(2)]

        loaded, ready, steps = sem("loaded"), sem("ready"), sem("steps")
        ctx_in = count("ctx_in", 16)
        tile_in = count("tile_in", 1)
        turned, turned_up = count("turned", 3), count("turned_up", 3)
        made, up = count("made", 2), count("up", 2)
        squares_up, roots = count("squares_up", 1), count("roots", 2)
        qk_up, kz_up = count("qk_up", 1), count("kz_up", 1)
        s_made, s_read, e_up = count("s_made", NG), count("s_read", NG), count("e_up", NG)
        e_turned, eT_up, o_part = count("e_turned", NG), count("eT_up", NG), count("o_part", NG)
        o_read, o_up = count("o_read", 1), count("o_up", 1)
        y_made, y_read, var_up, x_up = count("y_made", 1), count("y_read", 1), count("var_up", 1), count("x_up", 1)
        LOADS = 5 + 2 * bool(norms)
        STEPS = 6 + NG
        block = ctx.enter_context(nc.Block())

        @block.sync
        def _(sp):
            for j, name in enumerate(wqkv):
                sp.dma_start(w[:, :, j * H:(j + 1) * H], A[name].rearrange("(t p) n -> p t n", p=P)).then_inc(loaded, 16)
            sp.dma_start(w_o[:, :, :], A[wo].rearrange("(t p) n -> p t n", p=P)).then_inc(loaded, 16)
            sp.dma_start(owner[:, :], A[f"c_owner{dk}"]).then_inc(loaded, 16)
            for j, name in enumerate(norms or ()):
                sp.dma_start(gains[:, j, :], A[name].partition_broadcast(P)).then_inc(loaded, 16)
            if source:
                ctx_in.open(sp)
                with sp.Fori(0, B) as b:
                    sp.wait_ge(turned.sem, turned.of(b - 1, 1))
                    sp.dma_start(cb[:, :], A[source][bass.ds(b, 1), :, :].rearrange("o p h -> (o p) h")).then_inc(ctx_in.sem, 16)
                sp.wait_ge(ctx_in.sem, ctx_in.of(B - 1))
            sp.wait_ge(loaded, 16 * LOADS)

        @block.gpsimd
        def _(pool):
            for c in (tile_in, roots, kz_up):
                c.open(pool)
            pool.wait_ge(loaded, 16 * LOADS)
            with pool.Fori(0, B) as b:
                pool.wait_ge(turned.sem, turned.of(b - 1, 1))
                pool.tensor_copy(xb[:, :], core.x[:, bass.ds(b, 1), :].rearrange("p o h -> p (o h)")).then_inc(tile_in.sem, 1)
                if norms:
                    pool.wait_ge(squares_up.sem, squares_up.of(b))
                    pool.tensor_tensor(rstd[:, :], ssq[:, :], core.neghalf[:, 0:2], ALU.pow).then_inc(roots.sem, 1)
                pool.wait_ge(turned_up.sem, turned_up.of(b, 2))
                pool.wait_ge(s_made.sem, s_made.of(b - 1))
                for t in range(KT):
                    i = pool.tensor_tensor(kz[:, t, :, :], over_heads(qkT[:, 1, t, :], per_tile),
                                           bcast(owner[:, :], [P, per_tile, P]), ALU.mult)
                i.then_inc(kz_up.sem, 1)
                pool.wait_ge(var_up.sem, var_up.of(b))
                pool.tensor_tensor(ln_r[:, :], mv[:, 1:2], core.neghalf[:, 0:1], ALU.pow).then_inc(roots.sem, 1 if norms else 2)

        @block.tensor
        def _(pe):
            for c in (turned, made, s_made, e_turned, o_part, y_made):
                c.open(pe)
            pe.wait_ge(loaded, 16 * LOADS)
            with pe.Fori(0, B) as b:
                pe.wait_ge(tile_in.sem, tile_in.of(b))
                pe.wait_ge(turned_up.sem, turned_up.of(b - 1))
                if source:
                    pe.wait_ge(ctx_in.sem, ctx_in.of(b))
                for i, src in enumerate((xb, cb)[:inputs]):
                    for t in range(KT):
                        mm = pe.transpose(p_in[:, (i * KT + t) * P:(i * KT + t + 1) * P], src[:, t * P:(t + 1) * P], core.ident[:, :])
                mm.then_inc(turned.sem, 1)
                pe.wait_ge(turned_up.sem, turned_up.of(b, 1))

                def project(out, i, first, last=True):
                    at = KT * (inputs - 1) * (i > 0)
                    if biases:
                        pe.matmul(out, core.ones[:, :], core.bias(biases[i]), start=first, stop=False)
                    for t in range(KT):
                        mm = pe.matmul(out, inT[:, at + t, :], w[:, t, i * H:(i + 1) * H],
                                       start=first and not biases and t == 0, stop=last and t == KT - 1)
                    return mm

                pe.wait_ge(up.sem, up.of(b - 1))
                project(p_qk[:, 0:H], 0, True, last=False)
                project(p_qk[:, H:2 * H], 1, False).then_inc(made.sem, 1)
                project(p_v[:, 0:H], 2, True).then_inc(made.sem, 1)
                pe.wait_ge(qk_up.sem, qk_up.of(b))
                for j in range(2):
                    for t in range(KT):
                        mm = pe.transpose(p_in[:, (j * KT + t) * P:(j * KT + t + 1) * P], qk[:, j, t * P:(t + 1) * P], core.ident[:, :])
                mm.then_inc(turned.sem, 1)

                def scores(g):
                    if g == 0:
                        pe.wait_ge(kz_up.sem, kz_up.of(b))
                    pe.wait_ge(s_read.sem, s_read.of(b, g - 1) if g >= 2 else s_read.of(b - 1))
                    if causal:
                        pe.matmul(p_s[g % 2][:, :], core.identb[:, :], core.causal[:, :, :].rearrange("p g k -> p (g k)"),
                                  start=True, stop=False)
                    t, lo = g * G // per_tile, g * G % per_tile
                    pe.matmul(p_s[g % 2][:, :], qkT[:, 0, t, :], kz[:, t, lo:lo + G, :].rearrange("p g k -> p (g k)"),
                              start=not causal, stop=True).then_inc(s_made.sem, 1)

                def attend(g):
                    pe.wait_ge(e_up.sem, e_up.of(b, g + 1))
                    pe.wait_ge(eT_up.sem, eT_up.of(b, g))
                    for h in range(G):
                        mm = pe.transpose(p_e[:, h * P:(h + 1) * P], e[g % 2][:, h, :], core.ident[:, :])
                    mm.then_inc(e_turned.sem, 1)

                def values(g):
                    pe.wait_ge(eT_up.sem, eT_up.of(b, g + 1))
                    if g == 0:
                        pe.wait_ge(o_read.sem, o_read.of(b - 1))
                        pe.wait_ge(up.sem, up.of(b))
                    for h in range(G):
                        n = g * G + h
                        mm = pe.matmul(p_o[:, n * (dk + 1):(n + 1) * (dk + 1)], eT[g % 2][:, h, :], vaug[:, n, :],
                                       start=(n == 0), stop=(n == heads - 1))
                    mm.then_inc(o_part.sem, 1)

                scores(0)
                scores(1)
                for g in range(NG):
                    attend(g)
                    if g + 2 < NG:
                        scores(g + 2)
                    values(g)
                pe.wait_ge(o_up.sem, o_up.of(b))
                for t in range(KT):
                    mm = pe.transpose(p_in[:, t * P:(t + 1) * P], o[:, t * P:(t + 1) * P], core.ident[:, :])
                mm.then_inc(turned.sem, 1)
                pe.wait_ge(turned_up.sem, turned_up.of(b, 3))
                pe.wait_ge(y_read.sem, y_read.of(b - 1))
                if bias_o:
                    pe.matmul(p_y[:, 0:H], core.ones[:, :], core.bias(bias_o), start=True, stop=False)
                for t in range(KT):
                    mm = pe.matmul(p_y[:, 0:H], oT[:, t, :], w_o[:, t, :], start=(not bias_o and t == 0), stop=(t == KT - 1))
                mm.then_inc(y_made.sem, 1)

        @block.scalar
        def _(act):
            for c in (turned_up, up, e_up, eT_up):
                c.open(act)
            act.wait_ge(ready, 1)
            with act.Fori(0, B) as b:
                act.wait_ge(turned.sem, turned.of(b, 1))
                act.wait_ge(made.sem, made.of(b - 1))
                n = inputs * H
                act.copy(inT[:, :, :].rearrange("p t n -> p (t n)"), p_in[:, 0:n]).then_inc(turned_up.sem, 1)
                act.wait_ge(made.sem, made.of(b, 1))
                act.wait_ge(turned.sem, turned.of(b - 1, 2))
                act.copy(qk[:, :, :].rearrange("p j n -> p (j n)"), p_qk[:, :]).then_inc(up.sem, 1)
                act.wait_ge(made.sem, made.of(b, 2))
                act.wait_ge(o_part.sem, o_part.of(b - 1))
                act.copy(vaug[:, :, 0:dk], p_v[:, 0:H].rearrange("p (h d) -> p h d", d=dk)).then_inc(up.sem, 1)
                act.wait_ge(turned.sem, turned.of(b, 2))
                act.wait_ge(s_made.sem, s_made.of(b - 1))
                act.wait_ge(kz_up.sem, kz_up.of(b - 1))
                act.copy(qkT[:, :, :, :].rearrange("p j t n -> p (j t n)"), p_in[:, :]).then_inc(turned_up.sem, 1)

                def exps(g):
                    act.wait_ge(s_read.sem, s_read.of(b, g + 1))
                    ef = e[g % 2][:, :, :].rearrange("p g k -> p (g k)")
                    act.activation(ef, ef, ACT.Exp, scale=float(dk) ** -0.5).then_inc(e_up.sem, 1)

                def leave(g):
                    act.wait_ge(e_turned.sem, e_turned.of(b, g + 1))
                    act.wait_ge(o_part.sem, o_part.of(b, g - 1) if g >= 2 else o_part.of(b - 1))
                    act.copy(eT[g % 2][:, :, :].rearrange("p g k -> p (g k)"), p_e[:, :]).then_inc(eT_up.sem, 1)

                exps(0)
                for g in range(NG):
                    if g + 1 < NG:
                        exps(g + 1)
                    leave(g)
                act.wait_ge(turned.sem, turned.of(b, 3))
                act.wait_ge(y_made.sem, y_made.of(b - 1))
                act.copy(oT[:, :, :].rearrange("p t n -> p (t n)"), p_in[:, 0:H]).then_inc(turned_up.sem, 1)

        @block.vector
        def _(dve):
            for c in (squares_up, qk_up, s_read, o_read, o_up, y_read, var_up, x_up):
                c.open(dve)
            dve.memset(vaug[:, :, dk:dk + 1], 1.0).then_inc(ready, 1)
            dve.wait_ge(loaded, 16 * LOADS)
            ch = Chain(dve, steps, STEPS + 2 * bool(norms))
            with dve.Fori(0, B) as b:
                ch.start(b)
                dve.wait_ge(up.sem, up.of(b, 1))
                if norms:
                    ch.link(dve.tensor_tensor(sq[:, :, :], qk[:, :, :], qk[:, :, :], ALU.mult))
                    dve.wait_ge(roots.sem, roots.of(b - 1, 1))
                    ch.link(dve.tensor_reduce(ssq[:, :], sq[:, :, :], AX.X, ALU.add))
                    dve.tensor_scalar(ssq[:, :], ssq[:, :], 1.0 / H, RMS_EPS, ALU.mult, ALU.add).then_inc(squares_up.sem, 1)
                    dve.wait_ge(roots.sem, roots.of(b, 1))
                    for j in range(2):
                        i = dve.scalar_tensor_tensor(out=qk[:, j, :], in0=qk[:, j, :], scalar=rstd[:, j:j + 1],
                                                     in1=gains[:, j, :], op0=ALU.mult, op1=ALU.mult)
                    i.then_inc(qk_up.sem, 1)
                else:
                    dve.sem_inc(qk_up.sem, 1)

                def shift(g):
                    dve.wait_ge(s_made.sem, s_made.of(b, g + 1))
                    dve.wait_ge(e_turned.sem, e_turned.of(b, g - 1) if g >= 2 else e_turned.of(b - 1))
                    s3 = p_s[g % 2][:, :].rearrange("p (h k) -> p h k", h=G)
                    top = rmax[:, g * G:(g + 1) * G]
                    ch.link(dve.tensor_reduce(top, s3, AX.X, ALU.max))
                    dve.tensor_tensor(e[g % 2][:, :, :], s3, bcast(top, [P, G, P]), ALU.subtract).then_inc(s_read.sem, 1)

                for g in range(NG):
                    shift(g)
                dve.wait_ge(o_part.sem, o_part.of(b))
                o3 = p_o[:, 0:heads * (dk + 1)].rearrange("p (h d) -> p h d", d=dk + 1)
                ch.link(dve.reciprocal(rden[:, :].unsqueeze(2), o3[:, :, dk:dk + 1]))
                dve.tensor_tensor(o[:, :].rearrange("p (h d) -> p h d", d=dk), o3[:, :, 0:dk],
                                  bcast(rden[:, :], [P, heads, dk]), ALU.mult).then_inc(o_read.sem, 1)
                dve.wait_ge(o_read.sem, o_read.of(b))
                dve.sem_inc(o_up.sem, 1)
                norm_steps(dve, ch, core, b, y, stats, mv, ln_r, y_made, p_y[:, 0:H], y_read, var_up, roots, 2, x_up)
                while ch.n < ch.per:
                    ch.settle()
                ch.end()


def l1_self_attention(core):
    small_attention(core, "s1", 32, ("L1_attn_Wq", "L1_attn_Wk", "L1_attn_Wv"), "L1_attn_Wo", causal=True)


def l1_cross_attention(core):
    small_attention(core, "c1", 16, ("L1_xattn_Wq", "L1_xattn_Wk_img", "L1_xattn_Wv_img"), "L1_xattn_Wo", causal=False,
                    source="ctx_2048", biases=("L1_xattn_bq", "L1_xattn_bk_img", "L1_xattn_bv_img"),
                    norms=("L1_xattn_gq", "L1_xattn_gk_img"), bias_o="L1_xattn_bo")


EXPERTS, CHOICES = 16, 6
EI, SI = 176, 352
GROUP = 4
NT = GROUP * P


def feed_forward(core, tag, width, loads, experts):
    nc, A = core.nc, core.A
    tiles = -(-width // P)
    with ExitStack() as ctx:
        def sb(name, shape, dt=F32):
            return ctx.enter_context(nc.sbuf_tensor(f"{tag}_{name}", shape, dt))

        def ps(name, shape, dt=F32):
            return ctx.enter_context(nc.psum_tensor(f"{tag}_{name}", shape, dt))

        named = semaphores(nc, ctx)

        def sem(name):
            return named(f"{tag}_{name}")

        def count(name, per):
            return Count(sem(name), per)

        wg, wu = sb("wg", [P, KT, width]), sb("wu", [P, KT, width])
        wd = sb("wd", [P, tiles, H])
        x4 = sb("x4", [P, GROUP, H])
        xT = sb("xT", [P, KT, NT])
        act_g = [sb(f"act_g{i}", [P, NT]) for i in range(2)]
        h = [sb(f"h{i}", [P, NT]) for i in range(2)]
        y = sb("y", [P, GROUP, H])
        stats, mv, ln_r = sb("stats", [P, GROUP, 6]), sb("mv", [P, GROUP, 2]), sb("ln_r", [P, GROUP])
        p_g = [ps(f"p_g{i}", [P, BANK]) for i in range(2)]
        p_u = [ps(f"p_u{i}", [P, BANK]) for i in range(2)]
        p_c = [ps(f"p_c{i}", [P, BANK]) for i in range(2)]
        p_y = [ps(f"p_y{i}", [P, BANK]) for i in range(2)]
        if experts:
            w_r = sb("w_r", [P, KT, EXPERTS])
            spread = sb("spread", [64, tiles, P], BF16)
            spread_f = sb("spread_f", [64, P])
            rstat = sb("rstat", [P, 3, GROUP])
            logit = sb("logit", [P, GROUP, EXPERTS])
            prob = sb("prob", [P, GROUP, EXPERTS + 2])
            repl = sb("repl", [P, GROUP, EXPERTS + 2])
            best = sb("best", [P, GROUP, 8])
            comb = sb("comb", [P, GROUP, EXPERTS])
            parts = sb("parts", [P, GROUP, 4, EXPERTS], BF16)
            combT = sb("combT", [64, NT], BF16)

        loaded, steps, ready = sem("loaded"), sem("steps"), sem("ready")
        tile_in = count("tile_in", 1)
        turned, xT_up = count("turned", 1), count("xT_up", 1)
        gate_made, up_made = count("gate_made", tiles), count("up_made", tiles)
        gate_up, h_up = count("gate_up", tiles), count("h_up", tiles)
        down = count("down", tiles)
        y_read, var_up, rooted, x_up = count("y_read", 1), count("var_up", 1), count("rooted", 1), count("x_up", 1)
        if experts:
            r_made, r_in, r_exp = count("r_made", 2), count("r_in", 1), count("r_exp", 1)
            parts_up, combT_up, c_made = count("parts_up", 1), count("combT_up", 1), count("c_made", tiles)
            h_raw = count("h_raw", tiles)
            spread_in = sem("spread_in")
        LOADS = len(list(loads(A, wg, wu, wd))) + bool(experts)
        STEPS = 3 + (13 if experts else 0)
        block = ctx.enter_context(nc.Block())

        @block.sync
        def _(sp):
            n = 0
            for dst, src in loads(A, wg, wu, wd):
                sp.dma_start(dst, src).then_inc(loaded, 16)
                n += 1
            if experts:
                sp.dma_start(w_r[:, :, :], A["L1_ffn_gate_w"].rearrange("(t p) n -> p t n", p=P)).then_inc(loaded, 16)
                for t in range(tiles):
                    if t:
                        sp.wait_ge(ready, t)
                    sp.dma_start(spread_f[:, :], A["c_spread"][t]).then_inc(spread_in, 16)
                sp.wait_ge(spread_in, 16 * tiles)
            sp.wait_ge(loaded, 16 * LOADS)

        @block.gpsimd
        def _(pool):
            for c in (tile_in, rooted):
                c.open(pool)
            with pool.Fori(0, B // GROUP) as b:
                pool.wait_ge(y_read.sem, y_read.of(b - 1))
                pool.tensor_copy(x4[:, :, :], core.x[:, bass.ds(b * GROUP, GROUP), :]).then_inc(tile_in.sem, 1)
                pool.wait_ge(var_up.sem, var_up.of(b))
                pool.tensor_tensor(ln_r[:, :], mv[:, :, 1], core.neghalf[:, 0:GROUP], ALU.pow).then_inc(rooted.sem, 1)

        @block.tensor
        def _(pe):
            for c in (turned, gate_made, up_made, down) + ((r_made, c_made) if experts else ()):
                c.open(pe)
            pe.wait_ge(loaded, 16 * LOADS)
            with pe.Fori(0, B // GROUP) as b:
                pe.wait_ge(tile_in.sem, tile_in.of(b))
                pe.wait_ge(gate_up.sem, gate_up.of(b - 1))
                for t in range(KT):
                    for j in range(GROUP):
                        mm = pe.transpose(p_g[t][:, j * P:(j + 1) * P], x4[:, j, t * P:(t + 1) * P], core.ident[:, :])
                mm.then_inc(turned.sem, 1)
                pe.wait_ge(xT_up.sem, xT_up.of(b))

                def tile_rows(n):
                    return min(P, width - n * P)

                def gate_and_up(n):
                    m = tile_rows(n)
                    for bank, w, c, freed in ((p_g, wg, gate_made, gate_up), (p_u, wu, up_made, h_raw if experts else h_up)):
                        pe.wait_ge(freed.sem, freed.of(b, n - 1) if n >= 2 else freed.of(b - 1))
                        for t in range(KT):
                            mm = pe.matmul(bank[n % 2][0:m, :], w[:, t, n * P:n * P + m], xT[:, t, :],
                                           start=(t == 0), stop=(t == KT - 1))
                        mm.then_inc(c.sem, 1)

                def weights(n):
                    m = tile_rows(n)
                    pe.wait_ge(h_up.sem, h_up.of(b, n - 1) if n >= 2 else h_up.of(b - 1))
                    pe.matmul(p_c[n % 2][0:m, :], spread[:, n, 0:m], combT[:, :], start=True, stop=True).then_inc(c_made.sem, 1)

                def project(n):
                    m = tile_rows(n)
                    pe.wait_ge(h_up.sem, h_up.of(b, n + 1))
                    if n == 0:
                        pe.wait_ge(y_read.sem, y_read.of(b - 1))
                    for j in range(GROUP):
                        mm = pe.matmul(p_y[j // 2][:, (j % 2) * H:(j % 2 + 1) * H], h[n % 2][0:m, j * P:(j + 1) * P],
                                       wd[0:m, n, :], start=(n == 0 and j % 2 == 0), stop=(n == tiles - 1 and j % 2 == 1))
                    mm.then_inc(down.sem, 1)

                if experts:
                    pe.wait_ge(h_up.sem, h_up.of(b - 1))
                    for j in range(GROUP):
                        for t in range(KT):
                            mm = pe.matmul(p_c[0][:, j * EXPERTS:(j + 1) * EXPERTS], xT[:, t, j * P:(j + 1) * P], w_r[:, t, :],
                                           start=(j == 0 and t == 0), stop=(j == GROUP - 1 and t == KT - 1))
                    mm.then_inc(r_made.sem, 1)
                gate_and_up(0)
                gate_and_up(1)
                if experts:
                    pe.wait_ge(ready, tiles)
                    pe.wait_ge(parts_up.sem, parts_up.of(b))
                    for j in range(GROUP):
                        mm = pe.transpose(p_c[1][0:64, 0:NT // 2].bitcast(BF16)[:, j * P:(j + 1) * P],
                                          parts[:, j, :, :].rearrange("p a e -> p (a e)"), core.identb[:, :])
                    mm.then_inc(r_made.sem, 1)
                    pe.wait_ge(combT_up.sem, combT_up.of(b))
                    weights(0)
                for n in range(tiles):
                    if experts and n + 1 < tiles:
                        weights(n + 1)
                    if n + 2 < tiles:
                        gate_and_up(n + 2)
                    project(n)

        @block.scalar
        def _(act):
            for c in (xT_up, gate_up) + ((r_exp, combT_up) if experts else ()):
                c.open(act)
            with act.Fori(0, B // GROUP) as b:
                act.wait_ge(turned.sem, turned.of(b))
                act.wait_ge(up_made.sem, up_made.of(b - 1))
                for t in range(KT):
                    i = act.copy(xT[:, t, :], p_g[t][:, :])
                i.then_inc(xT_up.sem, 1)
                if experts:
                    act.wait_ge(r_in.sem, r_in.of(b))
                    act.activation(prob[:, :, 0:EXPERTS], logit[:, :, :], ACT.Exp).then_inc(r_exp.sem, 1)
                    act.wait_ge(r_made.sem, r_made.of(b, 2))
                    act.wait_ge(c_made.sem, c_made.of(b - 1))
                    act.copy(combT[:, :], p_c[1][0:64, 0:NT // 2].bitcast(BF16)).then_inc(combT_up.sem, 1)
                for n in range(tiles):
                    m = min(P, width - n * P)
                    act.wait_ge(gate_made.sem, gate_made.of(b, n + 1))
                    freed = h_raw if experts else h_up
                    act.wait_ge(freed.sem, freed.of(b, n - 1) if n >= 2 else freed.of(b - 1))
                    act.activation(act_g[n % 2][0:m, :], p_g[n % 2][0:m, :], ACT.Silu).then_inc(gate_up.sem, 1)

        @block.vector
        def _(dve):
            for c in (h_up, y_read, var_up, x_up) + ((r_in, parts_up, h_raw) if experts else ()):
                c.open(dve)
            if experts:
                dve.memset(prob[:, :, EXPERTS:], 2.0)
                dve.memset(parts[:, :, 3, :], 0.0).then_inc(steps, 1)
                dve.wait_ge(steps, 1)
                dve.memset(parts[:, :, 3, 0:1], 1.0).then_inc(steps, 1)
                for t in range(tiles):
                    dve.wait_ge(spread_in, 16 * (t + 1))
                    dve.tensor_copy(spread[:, t, :], spread_f[:, :]).then_inc(ready, 1)
            ch = Chain(dve, steps, STEPS, base=2 if experts else 0)
            with dve.Fori(0, B // GROUP) as b:
                ch.start(b)
                if experts:
                    dve.wait_ge(r_made.sem, r_made.of(b, 1))
                    r3 = p_c[0][:, 0:GROUP * EXPERTS].rearrange("p (g e) -> p g e", e=EXPERTS)
                    pr = prob[:, :, 0:EXPERTS]
                    ch.link(dve.tensor_reduce(rstat[:, 0, :], r3, AX.X, ALU.max))
                    dve.tensor_tensor(logit[:, :, :], r3, bcast(rstat[:, 0, :], [P, GROUP, EXPERTS]), ALU.subtract).then_inc(r_in.sem, 1)
                    dve.wait_ge(r_exp.sem, r_exp.of(b))
                    ch.link(dve.tensor_reduce(rstat[:, 1, :], pr, AX.X, ALU.add))
                    ch.link(dve.reciprocal(rstat[:, 2, :], rstat[:, 1, :]))
                    ch.link(dve.tensor_tensor(pr, pr, bcast(rstat[:, 2, :], [P, GROUP, EXPERTS]), ALU.mult))
                    ch.settle()
                    for j in range(GROUP):
                        i = dve.max(best[:, j, :], prob[:, j, :])
                    ch.link(i)
                    ch.settle()
                    for j in range(GROUP):
                        i = dve.match_replace(repl[:, j, :], best[:, j, :], prob[:, j, :], CHOSEN)
                    ch.link(i)
                    ch.link(dve.scalar_tensor_tensor(out=comb[:, :, :], in0=repl[:, :, 0:EXPERTS], scalar=CHOSEN, in1=pr,
                                                     op0=ALU.is_ge, op1=ALU.mult))
                    dve.wait_ge(r_made.sem, r_made.of(b - 1))
                    for j in range(3):
                        i = dve.tensor_copy(parts[:, :, j, :], comb[:, :, :])
                        if j < 2:
                            ch.link(i)
                            ch.link(dve.tensor_tensor(comb[:, :, :], comb[:, :, :], parts[:, :, j, :], ALU.subtract))
                        else:
                            i.then_inc(parts_up.sem, 1)
                for n in range(tiles):
                    m = min(P, width - n * P)
                    dve.wait_ge(up_made.sem, up_made.of(b, n + 1))
                    dve.wait_ge(gate_up.sem, gate_up.of(b, n + 1))
                    dve.wait_ge(down.sem, down.of(b, n - 1) if n >= 2 else down.of(b - 1))
                    i = dve.tensor_tensor(h[n % 2][0:m, :], act_g[n % 2][0:m, :], p_u[n % 2][0:m, :], ALU.mult)
                    if experts:
                        i.then_inc(h_raw.sem, 1)
                        dve.wait_ge(h_raw.sem, h_raw.of(b, n + 1))
                        dve.wait_ge(c_made.sem, c_made.of(b, n + 1))
                        i = dve.tensor_tensor(h[n % 2][0:m, :], h[n % 2][0:m, :], p_c[n % 2][0:m, :], ALU.mult)
                    i.then_inc(h_up.sem, 1)
                dve.wait_ge(down.sem, down.of(b))
                for i in range(2):
                    ins = dve.tensor_tensor(y[:, 2 * i:2 * i + 2, :].rearrange("p g h -> p (g h)"), p_y[i][:, :],
                                            x4[:, 2 * i:2 * i + 2, :].rearrange("p g h -> p (g h)"), ALU.add)
                ins.then_inc(y_read.sem, 1)
                dve.wait_ge(y_read.sem, y_read.of(b))
                for j in range(GROUP):
                    ins = dve.bn_stats(stats[:, j, :], y[:, j, :])
                ch.link(ins)
                ch.settle()
                for j in range(GROUP):
                    ins = dve.bn_aggr(mv[:, j, :], stats[:, j, :])
                ch.link(ins)
                dve.tensor_scalar(mv[:, :, 1], mv[:, :, 1], LN_EPS, None, ALU.add).then_inc(var_up.sem, 1)
                dve.wait_ge(rooted.sem, rooted.of(b))
                for j in range(GROUP):
                    ins = dve.tensor_scalar(core.x[:, bass.ds(b * GROUP + j, 1), :].rearrange("p o h -> p (o h)"), y[:, j, :],
                                            mv[:, j, 0:1], ln_r[:, j:j + 1], ALU.subtract, ALU.mult)
                ins.then_inc(x_up.sem, 1)
                dve.wait_ge(x_up.sem, x_up.of(b))
                ch.end()


def l0_feed_forward(core):
    inter = 1024

    def loads(A, wg, wu, wd):
        w = A["L0_ffn_w_gate_up"].rearrange("(t p) n -> p t n", p=P)
        yield wg[:, :, :], w[:, :, 0:inter]
        yield wu[:, :, :], w[:, :, inter:]
        yield wd[:, :, :], A["L0_ffn_w_down"].rearrange("(k p) n -> p k n", p=P)

    feed_forward(core, "f0", inter, loads, experts=False)


def l1_feed_forward(core):
    wide = EXPERTS * EI

    def loads(A, wg, wu, wd):
        for t in range(KT):
            rows = slice(t * P, (t + 1) * P)
            for j, dst in enumerate((wg, wu)):
                yield (dst[:, t, 0:wide].rearrange("p (e i) -> p e i", i=EI),
                       A["L1_ffn_w1"][rows, :, j * EI:(j + 1) * EI])
                yield dst[:, t, wide:], A["L1_ffn_shared_w1"][rows, j * SI:(j + 1) * SI]
        yield (wd[:, 0:wide // P, :],
               A["L1_ffn_w2"].rearrange("e i h -> (e i) h").rearrange("(k p) h -> p k h", p=P))
        whole = SI // P
        yield (wd[:, wide // P:wide // P + whole, :],
               A["L1_ffn_shared_w2"][0:whole * P, :].rearrange("(k p) h -> p k h", p=P))
        yield wd[0:SI - whole * P, wide // P + whole, :], A["L1_ffn_shared_w2"][whole * P:, :]

    feed_forward(core, "f1", wide + SI, loads, experts=True)


def constants():
    pos = np.arange(P)
    half = ROPE // 2
    inv = (1.0 / np.power(np.float32(10000.0), np.arange(half, dtype=np.float32) * np.float32(2.0 / ROPE))).astype(np.float32)

    def rope(at):
        ang = at.astype(np.float32)[:, None] * inv[None, :]
        cos, sin = np.cos(ang), np.sin(ang)
        return (np.concatenate([cos, cos, np.ones((len(at), D - ROPE))], axis=1).astype(np.float32),
                np.concatenate([-sin, sin], axis=1).astype(np.float32))

    c = {}
    c["c_ident"] = np.eye(P, dtype=np.float32)
    c["c_causal"] = np.where(pos[None, :] <= pos[:, None], 0, NEG).astype(np.float32)
    c["c_cos"], c["c_sin"] = rope(pos)
    ends = np.arange(1, NC + 1) * RATIO - 1
    c["c_cos_c"], c["c_sin_c"] = rope(ends[pos % NC])
    c["c_cmask"] = np.where(ends[None, :] <= pos[:, None], 0, NEG).astype(np.float32)
    c["c_member"] = (pos[:, None] // RATIO == np.arange(NC)[None, :]).astype(np.float32)
    for dk in (8, 16):
        c[f"c_owner{dk}"] = (pos[:, None] // dk == np.arange(P // dk)[None, :]).astype(np.float32)
    wide = EXPERTS * EI
    row = np.arange(-(-(wide + SI) // P) * P)
    owner = np.where(row < wide, row // EI, 3 * EXPERTS)
    spread = np.zeros((64, len(row)), np.float32)
    for j in range(3):
        spread += np.arange(64)[:, None] == np.where(row < wide, owner + j * EXPERTS, -1)[None, :]
    spread[3 * EXPERTS, :] = row >= wide
    c["c_spread"] = np.ascontiguousarray(spread.reshape(64, -1, P).transpose(1, 0, 2))
    return c


LAYERS = [l0_cross_attention, l0_feed_forward, l1_self_attention, l1_cross_attention, l1_feed_forward]


def program(nc, A, out, stop=6, start=0):
    with ExitStack() as ctx:
        core = Core(nc, ctx, A, out)
        setup(core)
        if start < 1:
            with ExitStack() as own:
                wcol = own.enter_context(nc.sbuf_tensor("token_weights", [P, B], F32))
                l0_token_weights(core, wcol)
                l0_attention(core, wcol)
        for n, layer in enumerate(LAYERS, 2):
            if start < n <= stop:
                layer(core)
        store(core)


def store(core):
    nc = core.nc
    with ExitStack() as ctx:
        stored = semaphores(nc, ctx)("stored")
        block = ctx.enter_context(nc.Block())

        @block.sync
        def _(sp):
            sp.dma_start(core.out.rearrange("b p h -> p b h"), core.x[:, :, :]).then_inc(stored, 16)
            sp.wait_ge(stored, 16)


UNUSED = ("L1_xattn_context_lens", "L1_xattn_Wk", "L1_xattn_bk", "L1_xattn_gk", "L1_xattn_Wv", "L1_xattn_bv")
TRANSPOSED = ("L0_ffn_w_gate_up", "L0_ffn_w_down", "L1_attn_Wq", "L1_attn_Wk", "L1_attn_Wv", "L1_attn_Wo",
              "L1_ffn_gate_w", "L1_ffn_shared_w1", "L1_ffn_shared_w2")
OUT = ((B, P, H), "float32")


def kernel(**inputs):
    import numpy as _np
    import concourse.bacc as _bacc
    from concourse import mybir as _mybir
    from concourse.bass_utils import run_bass_kernel_spmd as _run

    given = {}
    for name, a in inputs.items():
        if name in UNUSED:
            continue
        if name in TRANSPOSED:
            a = _np.asarray(a).T
        elif name == "L1_ffn_w1":
            a = _np.asarray(a).transpose(2, 0, 1)
        elif name == "L1_ffn_w2":
            a = _np.asarray(a).transpose(0, 2, 1)
        given[name] = _np.ascontiguousarray(a)
    given.update(constants())
    nc = _bacc.Bacc("TRN2", target_bir_lowering=False, num_devices=1)
    arrays, A = {}, {}
    for name, a in given.items():
        arrays[f"in_{name}_dram"] = a
        A[name] = nc.dram_tensor(f"in_{name}_dram", a.shape, _mybir.dt.from_np(a.dtype), kind="ExternalInput").ap()
    out = nc.dram_tensor("out_0_dram", OUT[0], _mybir.dt.from_np(_np.dtype(OUT[1])), kind="ExternalOutput").ap()
    program(nc, A, out)
    r = _run(nc, [arrays], core_ids=[0])
    return r.results[0]["out_0_dram"]
```

```python
from contextlib import ExitStack

import numpy as np

import concourse.bass as bass
from concourse import mybir

F32 = mybir.dt.float32
BF16 = mybir.dt.bfloat16
U16 = mybir.dt.uint16
ALU = mybir.AluOpType
ACT = mybir.ActivationFunctionType
AX = mybir.AxisListType

P = 128
B = 16
H = 256
KT = H // P
BANK = 512
NEG = -1e30
LN_EPS = 1e-5
RMS_EPS = 1e-6

BIASES = [("L0_attn_bq", 2048), ("L0_attn_blk", 2048), ("L0_attn_blv", 2048), ("L0_attn_bk", 128),
          ("L0_attn_bv", 128), ("L0_attn_bo", 256), ("L0_xattn_bq", 256), ("L0_xattn_bkv", 512),
          ("L0_xattn_bp", 256), ("L1_xattn_bq", 256), ("L1_xattn_bk_img", 256), ("L1_xattn_bv_img", 256),
          ("L1_xattn_bo", 256)]
BIAS_AT = {}
for _name, _n in BIASES:
    BIAS_AT[_name] = sum(n for _, n in BIASES[:len(BIAS_AT)])
BIAS_LEN = sum(n for _, n in BIASES)


class Count:

    def __init__(self, sem, per):
        self.sem, self.per = sem, per

    def open(self, eng):
        eng.sem_inc(self.sem, self.per)

    def of(self, b, k=None):
        return self.per * b + (self.per + (self.per if k is None else k))


class Chain:

    def __init__(self, eng, sem, per, base=0):
        self.eng, self.sem, self.per, self.base, self.n = eng, sem, per, base, 0

    def start(self, b):
        self.b, self.n = b, 0

    def mark(self, ins):
        self.n += 1
        ins.then_inc(self.sem, 1)
        return self.n

    def wait(self, n=None):
        self.eng.wait_ge(self.sem, self.per * self.b + (self.base + (self.n if n is None else n)))

    def link(self, ins):
        self.mark(ins)
        self.wait()

    def settle(self):
        self.n += 1
        self.eng.sem_inc(self.sem, 1)

    def end(self):
        assert self.n == self.per, f"{self.n} links in a pass, {self.per} counted"


def pipeline(eng, order, pieces, passes):
    depth = max(lag for _, lag in order)

    def emit(i, there):
        for name, lag in order:
            if name in pieces and there(lag):
                pieces[name](i - lag)

    for i in range(depth):
        emit(i, lambda lag, i=i: lag <= i)
    with eng.Fori(depth, passes) as i:
        emit(i, lambda lag: True)
    for i in range(passes, passes + depth):
        emit(i, lambda lag, i=i: i - lag < passes)


def semaphores(nc, ctx):
    held = []

    def clear():
        nc.clear_and_free_semaphores(held)
        nc.all_engine_barrier()

    def sem(name):
        held.append(nc.alloc_semaphore(name))
        return held[-1]

    ctx.callback(clear)
    return sem


def bcast(ap, shape):
    return ap.unsqueeze(2).to_broadcast(shape)


def over_heads(ap, heads):
    return ap.unsqueeze(1).to_broadcast([ap.shape[0], heads, ap.shape[1]])


class Core:

    def __init__(self, nc, ctx, A, out):
        self.nc, self.A, self.out = nc, A, out

        def sb(name, shape, dt=F32):
            return ctx.enter_context(nc.sbuf_tensor(name, shape, dt))

        self.x = sb("x_res", [P, B, H])
        self.ident = sb("ident", [P, P])
        self.identb = sb("identb", [P, P], BF16)
        self.causal = sb("causal", [P, 4, P], BF16)
        self.bias_rows = sb("bias_rows", [3, BIAS_LEN], BF16)
        self.ones = sb("ones", [3, P], BF16)
        self.neghalf = sb("neghalf", [P, 32])

    def bias(self, name, lo=0, n=None):
        at = BIAS_AT[name] + lo
        return self.bias_rows[:, at:at + (dict(BIASES)[name] - lo if n is None else n)]


def setup(core):
    nc, A = core.nc, core.A
    rows = BIAS_LEN // P
    with ExitStack() as ctx:
        def sb(name, shape, dt=F32):
            return ctx.enter_context(nc.sbuf_tensor(name, shape, dt))

        causal_f = sb("causal_f", [P, P])
        whole = sb("bias_whole", [rows, P])
        rest = sb("bias_rest", [rows, 2, P])
        parts = sb("bias_parts", [rows, 3, P], BF16)
        sem = semaphores(nc, ctx)
        loaded, bias_in, made, spread = (sem("setup_" + n) for n in ("loaded", "bias_in", "made", "spread"))
        block = ctx.enter_context(nc.Block())

        @block.sync
        def _(sp):
            for name, n in BIASES:
                at = BIAS_AT[name] // P
                sp.dma_start(whole[at:at + n // P, :], A[name].rearrange("(a p) -> a p", p=P)).then_inc(bias_in, 16)
            sp.dma_start(core.ident[:, :], A["c_ident"]).then_inc(loaded, 16)
            sp.dma_start(causal_f[:, :], A["c_causal"]).then_inc(loaded, 16)
            sp.dma_start(core.x[:, :, :], A["x"].rearrange("b p h -> p b h")).then_inc(loaded, 16)
            sp.wait_ge(made, 5)
            for j in range(3):
                sp.dma_start(core.bias_rows[j:j + 1, :].rearrange("o (a p) -> o a p", p=P),
                             parts[:, j, :]).then_inc(spread, 16)
            sp.wait_ge(spread, 48)
            sp.wait_ge(loaded, 48)

        @block.vector
        def _(dve):
            dve.wait_ge(bias_in, 16 * len(BIASES))
            dve.tensor_copy(parts[:, 0, :], whole[:, :]).then_inc(made, 1)
            dve.wait_ge(made, 1)
            dve.tensor_tensor(rest[:, 0, :], whole[:, :], parts[:, 0, :], ALU.subtract).then_inc(made, 1)
            dve.wait_ge(made, 2)
            dve.tensor_copy(parts[:, 1, :], rest[:, 0, :]).then_inc(made, 1)
            dve.wait_ge(made, 3)
            dve.tensor_tensor(rest[:, 1, :], rest[:, 0, :], parts[:, 1, :], ALU.subtract).then_inc(made, 1)
            dve.wait_ge(made, 4)
            dve.tensor_copy(parts[:, 2, :], rest[:, 1, :]).then_inc(made, 1)
            dve.wait_ge(loaded, 48)
            dve.tensor_copy(core.identb[:, :], core.ident[:, :])
            for j in range(4):
                dve.tensor_copy(core.causal[:, j, :], causal_f[:, :])
            dve.memset(core.ones[:, :], 1.0)
            dve.memset(core.neghalf[:, :], -0.5)


NH, D = 16, 128
RATIO, NC = 4, 32
ROPE = D // 2
G = 4
CHOSEN = 3e38


def l0_attention(core, wcol):
    nc, A = core.nc, core.A
    NG = NH // G
    with ExitStack() as ctx:
        def sb(name, shape, dt=F32):
            return ctx.enter_context(nc.sbuf_tensor(name, shape, dt))

        def ps(name, shape, dt=F32):
            return ctx.enter_context(nc.psum_tensor(name, shape, dt))

        named = semaphores(nc, ctx)

        def sem(name):
            return named("a0_" + name)

        def count(name, per):
            return Count(sem(name), per)

        w_qkv = [sb(f"a0_w{n}", [P, KT, NH * D]) for n in "qkv"]
        w_o = sb("a0_wo", [P, NH, H])
        w_c = sb("a0_wc", [P, KT, 2 * D])
        cq, ck_tab, cc = (sb(n, [P, D]) for n in ("a0_cos_q", "a0_cos_k", "a0_cos_c"))
        sq_tab, sk_tab, sc_tab = (sb(n, [P, ROPE]) for n in ("a0_sin_q", "a0_sin_k", "a0_sin_c"))
        wn = sb("a0_norm_w", [P, 2, D])
        cmask_f = sb("a0_cmask_f", [P, NC])
        cmask = sb("a0_cmask", [P, NH, NC], BF16)
        member = sb("a0_member", [P, NC])

        xb = sb("a0_xb", [P, H])
        xT = sb("a0_xT", [P, KT, P])
        raw = [sb(f"a0_raw{n}", [P, NH * D]) for n in "qkv"]
        rot = [sb(f"a0_rot{n}", [P, NH * D]) for n in "qk"]
        sq = sb("a0_sq", [P, NH * D])
        half = sb("a0_half", [P, NH * ROPE])
        ssq = sb("a0_ssq", [P, 2 * NH])
        rstd = sb("a0_rstd", [P, 2 * NH])
        qT = sb("a0_qT", [P, NH, P])
        kT = sb("a0_kT", [P, NH, P])
        wsel = sb("a0_wsel", [P, NC])
        entT = sb("a0_entT", [P, KT, 4, NC])
        ckr = sb("a0_ckr", [P, D])
        cv = sb("a0_cv", [P, G, D])
        crot = sb("a0_crot", [P, D])
        chalf = sb("a0_chalf", [P, ROPE])
        csq = sb("a0_csq", [P, D])
        cst = sb("a0_cst", [P, 3])
        ckT = sb("a0_ckT", [P, P])
        scm = sb("a0_scm", [P, NH, NC])
        top = sb("a0_top", [P, NH, 8])
        repl = sb("a0_repl", [P, NH, NC])
        tmax = sb("a0_tmax", [P, NH])
        es = sb("a0_es", [P, NH, NC])
        tsum = sb("a0_tsum", [P, NH])
        psT = sb("a0_psT", [P, NG, P])
        rqs = sb("a0_rqs", [P, NH])
        lmax = sb("a0_lmax", [P, NH])
        nbias = sb("a0_nbias", [P, NH])
        lsum = sb("a0_lsum", [P, NH])
        lrec = sb("a0_lrec", [P, NH])
        prob = [sb(f"a0_prob{i}", [P, G, P]) for i in range(2)]
        pT = [sb(f"a0_pT{i}", [P, G, P]) for i in range(2)]
        cT = [sb(f"a0_cT{i}", [P, G, P]) for i in range(2)]
        y = sb("a0_y", [P, H])
        stats = sb("a0_stats", [P, 6])
        mv = sb("a0_mv", [P, 2])
        ln_r = sb("a0_ln_r", [P, 1])

        proj = [ps(f"a0_p_proj{i}", [P, BANK]) for i in range(2)]
        work = [ps(f"a0_p_work{i}", [P, BANK]) for i in range(2)]
        p_pT = ps("a0_p_pT", [P, BANK])
        p_cT = ps("a0_p_cT", [P, BANK])
        p_c = ps("a0_p_c", [P, BANK])
        p_o = ps("a0_p_o", [P, BANK])

        loaded, tables = sem("loaded"), sem("tables")
        LOADS, TABLES = 16, 11
        comp_steps, rot_steps, sparse_steps, local_steps, tail_steps = (
            sem(n) for n in ("comp_steps", "rot_steps", "sparse_steps", "local_steps", "tail_steps"))
        tile_in = count("tile_in", 1)
        PROJ = 14
        Q_AT, K_AT, C_AT, V_AT = 1, 5, 9, 10
        proj_made, proj_read = count("proj_made", PROJ), count("proj_read", PROJ)
        work_made, work_read = count("work_made", 3 * NG), count("work_read", 2 * NG)
        squared, summed, rotated = count("squared", 2), count("summed", 2), count("rotated", 2)
        root_h, k_normed, rqs_up = count("root_heads", 2), count("k_normed", 1), count("rqs_up", 1)
        wsel_up, c_sum, root_c, crot_up = (count(n, 1) for n in ("wsel_up", "c_sum", "root_c", "crot_up"))
        c_made = count("c_made", 4)
        c_read = count("c_read", 3)
        s_arg, s_exp, s_prob = (count("sparse_" + n, 1) for n in ("arg", "exp", "prob"))
        bias_up, l_exp, l_prob = (count(n, NG) for n in ("bias_up", "local_exp", "local_prob"))
        pT_made, pT_read = count("pT_made", NG), count("pT_read", NG)
        cT_made, cT_read = count("cT_made", NG), count("cT_read", NG)
        o_made, o_read = count("o_made", 1), count("o_read", 1)
        var_up, root_l, x_up = count("var_up", 1), count("root_l", 1), count("x_up", 1)

        def before(c, b, k, n):
            return c.of(b, k - n) if k > n else c.of(b - 1, c.per + k - n)

        order = [("turn_q", 1), ("sparse", 1), ("turn_k", 1), ("in", 0), ("s0", 1), ("s1", 1), ("norm1", 2),
                 ("q", 0), ("sparse_exp", 1), ("sparse_prob", 1), ("rot_q", 0), ("norm2", 2), ("e0", 1), ("k", 0),
                 ("e1", 1), ("turn_sparse", 1), ("m0", 1), ("sum_q", 0), ("top2", 1), ("entries", 0), ("m1", 1),
                 ("even2", 1), ("top3", 1), ("rot_k", 0), ("m2", 1), ("m3", 1), ("sum_k", 0), ("out", 1),
                 ("k_norm", 0), ("comp_kv", 0), ("v", 0), ("comp_key", 0)]

        block = ctx.enter_context(nc.Block())

        @block.sync
        def _(sp):
            for w, name in zip(w_qkv, ("L0_attn_Wq", "L0_attn_Wlk", "L0_attn_Wlv")):
                sp.dma_start(w[:, :, :], A[name].rearrange("(t p) n -> p t n", p=P)).then_inc(loaded, 16)
            sp.dma_start(w_o[:, :, :], A["L0_attn_Wo"].rearrange("(h p) n -> p h n", p=P)).then_inc(loaded, 16)
            for j, name in enumerate(("L0_attn_Wk", "L0_attn_Wv")):
                sp.dma_start(w_c[:, :, j * D:(j + 1) * D],
                             A[name].rearrange("(t p) n -> p t n", p=P)).then_inc(loaded, 16)
            for j, name in enumerate(("L0_attn_qn_w", "L0_attn_kn_w")):
                sp.dma_start(wn[:, j, :], A[name].partition_broadcast(P)).then_inc(loaded, 16)
            for t, name in ((cq, "c_cos"), (ck_tab, "c_cos"), (cc, "c_cos_c"), (sq_tab, "c_sin"),
                            (sk_tab, "c_sin"), (sc_tab, "c_sin_c"), (cmask_f, "c_cmask"), (member, "c_member")):
                sp.dma_start(t[:, :], A[name]).then_inc(loaded, 16)
            sp.wait_ge(loaded, 16 * LOADS)

        @block.gpsimd
        def _(pool):
            for c in (tile_in, squared, root_h, k_normed, root_c, root_l):
                c.open(pool)

            def tile_copy(b):
                pool.wait_ge(proj_made.sem, proj_made.of(b - 1, 1))
                pool.wait_ge(c_made.sem, c_made.of(b - 1, 1))
                pool.tensor_copy(xb[:, :], core.x[:, bass.ds(b, 1), :].rearrange("p o h -> p (o h)")).then_inc(tile_in.sem, 1)

            def square(j):
                def run(b):
                    pool.wait_ge(proj_read.sem, proj_read.of(b, (Q_AT, K_AT)[j] + 4))
                    pool.wait_ge(summed.sem, before(summed, b, j + 1, 1))
                    pool.tensor_tensor(sq[:, :], raw[j][:, :], raw[j][:, :], ALU.mult).then_inc(squared.sem, 1)
                return run

            def root_queries(b):
                pool.wait_ge(summed.sem, summed.of(b, 1))
                pool.wait_ge(rqs_up.sem, rqs_up.of(b - 1))
                pool.tensor_tensor(rstd[:, 0:NH], ssq[:, 0:NH], core.neghalf[:, 0:NH], ALU.pow).then_inc(root_h.sem, 1)

            def norm_keys(b):
                pool.wait_ge(summed.sem, summed.of(b, 2))
                pool.wait_ge(k_normed.sem, k_normed.of(b - 1))
                pool.tensor_tensor(rstd[:, NH:], ssq[:, NH:], core.neghalf[:, 0:NH], ALU.pow).then_inc(root_h.sem, 1)
                pool.wait_ge(root_h.sem, root_h.of(b, 2))
                pool.wait_ge(rotated.sem, rotated.of(b, 2))
                kr = rot[1][:, :].rearrange("p (h d) -> p h d", h=NH)
                pool.tensor_tensor(kr, kr, bcast(rstd[:, NH:], [P, NH, D]), ALU.mult).then_inc(k_normed.sem, 1)

            def root_compressed(b):
                pool.wait_ge(c_sum.sem, c_sum.of(b))
                pool.wait_ge(crot_up.sem, crot_up.of(b - 1))
                pool.tensor_tensor(cst[:, 2:3], cst[:, 1:2], core.neghalf[:, 0:1], ALU.pow).then_inc(root_c.sem, 1)

            def root_layer(b):
                pool.wait_ge(var_up.sem, var_up.of(b))
                pool.wait_ge(x_up.sem, x_up.of(b - 1))
                pool.tensor_tensor(ln_r[:, :], mv[:, 1:2], core.neghalf[:, 0:1], ALU.pow).then_inc(root_l.sem, 1)

            pipeline(pool, order, {"in": tile_copy, "q": square(0), "k": square(1), "norm1": root_layer,
                                   "sum_q": root_queries, "k_norm": norm_keys, "comp_kv": root_compressed}, B)

        @block.tensor
        def _(pe):
            for c in (work_made, proj_made, c_made, pT_made, cT_made, o_made):
                c.open(pe)
            pe.wait_ge(loaded, 16 * LOADS)
            pe.wait_ge(tables, TABLES)

            def turn_in(b):
                pe.wait_ge(tile_in.sem, tile_in.of(b))
                pe.wait_ge(proj_read.sem, before(proj_read, b, 1, 2))
                for t in range(KT):
                    mm = pe.transpose(proj[0][:, t * P:(t + 1) * P], xb[:, t * P:(t + 1) * P], core.ident[:, :])
                mm.then_inc(proj_made.sem, 1)

            def entries(b):
                pe.wait_ge(wsel_up.sem, wsel_up.of(b))
                pe.wait_ge(c_read.sem, c_read.of(b - 1))
                for t in range(KT):
                    mm = pe.matmul(p_c[:, t * NC:(t + 1) * NC], xb[:, t * P:(t + 1) * P], wsel[:, :],
                                   start=True, stop=True)
                mm.then_inc(c_made.sem, 1)

            def project(i, at):
                def run(b):
                    if i == 0:
                        pe.wait_ge(proj_read.sem, proj_read.of(b, 1))
                    name = ("L0_attn_bq", "L0_attn_blk", "L0_attn_blv")[i]
                    for c in range(NG):
                        n = at + c
                        bank = proj[n % 2]
                        pe.wait_ge(proj_read.sem, before(proj_read, b, n + 1, 2))
                        pe.matmul(bank[:, :], core.ones[:, :], core.bias(name, c * BANK, BANK), start=True, stop=False)
                        for t in range(KT):
                            mm = pe.matmul(bank[:, :], xT[:, t, :], w_qkv[i][:, t, c * BANK:(c + 1) * BANK],
                                           start=False, stop=(t == KT - 1))
                        mm.then_inc(proj_made.sem, 1)
                return run

            def compressed_kv(b):
                bank = proj[C_AT % 2]
                pe.wait_ge(c_read.sem, c_read.of(b, 1))
                pe.wait_ge(proj_read.sem, before(proj_read, b, C_AT + 1, 2))
                pe.matmul(bank[:, 0:2 * D], core.ones[:, :],
                          core.bias_rows[:, BIAS_AT["L0_attn_bk"]:BIAS_AT["L0_attn_bk"] + 2 * D], start=True, stop=False)
                for t in range(KT):
                    mm = pe.matmul(bank[:, 0:2 * D], entT[:, t, :, :].rearrange("p a c -> p (a c)"), w_c[:, t, :],
                                   start=False, stop=(t == KT - 1))
                mm.then_inc(proj_made.sem, 1)

            def compressed_key(b):
                pe.wait_ge(crot_up.sem, crot_up.of(b))
                pe.transpose(p_c[:, 0:P], crot[:, :], core.ident[:, :]).then_inc(c_made.sem, 1)

            def turn_heads(j):
                def run(b):
                    if j == 0:
                        pe.wait_ge(rotated.sem, rotated.of(b, 1))
                        pe.wait_ge(l_exp.sem, l_exp.of(b - 1))
                    else:
                        pe.wait_ge(k_normed.sem, k_normed.of(b))
                    for g in range(NG):
                        n = j * NG + g
                        if n >= 2:
                            pe.wait_ge(work_read.sem, work_read.of(b, n - 1))
                        for h in range(G):
                            at = (g * G + h) * D
                            mm = pe.transpose(work[n % 2][:, h * P:(h + 1) * P], rot[j][:, at:at + D], core.ident[:, :])
                        mm.then_inc(work_made.sem, 1)
                return run

            def sparse_scores(b):
                pe.wait_ge(work_read.sem, work_read.of(b, NG))
                pe.wait_ge(c_read.sem, c_read.of(b, 2))
                pe.matmul(p_c[:, :], core.identb[:, :], cmask[:, :, :].rearrange("p h c -> p (h c)"),
                          start=True, stop=False)
                for h in range(NH):
                    mm = pe.matmul(p_c[:, h * NC:(h + 1) * NC], qT[:, h, :], ckT[:, 0:NC],
                                   start=False, stop=(h == NH - 1))
                mm.then_inc(c_made.sem, 1)

            def scores(g):
                def run(b):
                    if g == 0:
                        pe.wait_ge(work_read.sem, work_read.of(b))
                    if g >= 2:
                        pe.wait_ge(l_exp.sem, l_exp.of(b, g - 1))
                    bank = work[g % 2]
                    pe.matmul(bank[:, :], core.identb[:, :], core.causal[:, :, :].rearrange("p g k -> p (g k)"),
                              start=True, stop=False)
                    for h in range(G):
                        mm = pe.matmul(bank[:, h * P:(h + 1) * P], qT[:, g * G + h, :], kT[:, g * G + h, :],
                                       start=False, stop=(h == G - 1))
                    mm.then_inc(work_made.sem, 1)
                return run

            def turn_sparse(b):
                pe.wait_ge(s_prob.sem, s_prob.of(b))
                for g in range(NG):
                    mm = pe.transpose(p_c[:, g * P:(g + 1) * P],
                                      es[:, g * G:(g + 1) * G, :].rearrange("p h c -> p (h c)"), core.ident[:, :])
                mm.then_inc(c_made.sem, 1)

            def output(b, g):
                pe.wait_ge(cT_read.sem, cT_read.of(b, g + 1))
                if g == 0:
                    pe.wait_ge(o_read.sem, o_read.of(b - 1))
                    pe.matmul(p_o[:, 0:H], core.ones[:, :], core.bias("L0_attn_bo"), start=True, stop=False)
                for h in range(G):
                    mm = pe.matmul(p_o[:, 0:H], cT[g % 2][:, h, :], w_o[:, g * G + h, :],
                                   start=False, stop=(g == NG - 1 and h == G - 1))
                if g == NG - 1:
                    mm.then_inc(o_made.sem, 1)

            def group(g):
                def run(b):
                    pe.wait_ge(l_prob.sem, l_prob.of(b, g + 1))
                    pe.wait_ge(pT_read.sem, pT_read.of(b, g))
                    for h in range(G):
                        mm = pe.transpose(p_pT[:, h * P:(h + 1) * P], prob[g % 2][:, h, :], core.ident[:, :])
                    mm.then_inc(pT_made.sem, 1)
                    if g + 2 < NG:
                        scores(g + 2)(b)
                    if g >= 1:
                        output(b, g - 1)
                    pe.wait_ge(pT_read.sem, pT_read.of(b, g + 1))
                    pe.wait_ge(cT_read.sem, cT_read.of(b, g))
                    if g == 0:
                        pe.wait_ge(proj_read.sem, proj_read.of(b))
                        pe.wait_ge(c_read.sem, c_read.of(b))
                    for h in range(G):
                        o = p_cT[:, h * P:(h + 1) * P]
                        at = (g * G + h) * D
                        pe.matmul(o, raw[2][:, at:at + D], pT[g % 2][:, h, :], start=(h == 0), stop=False)
                        mm = pe.matmul(o, cv[:, h, :], psT[:, g, :], start=False, stop=(h == G - 1))
                    mm.then_inc(cT_made.sem, 1)
                return run

            def last_output(b):
                output(b, NG - 1)

            pieces = {"turn_q": turn_heads(0), "sparse": sparse_scores, "turn_k": turn_heads(1), "in": turn_in,
                      "s0": scores(0), "s1": scores(1), "q": project(0, Q_AT), "k": project(1, K_AT),
                      "turn_sparse": turn_sparse, "entries": entries, "out": last_output,
                      "comp_kv": compressed_kv, "v": project(2, V_AT), "comp_key": compressed_key}
            pieces.update({f"m{g}": group(g) for g in range(NG)})
            pipeline(pe, order, pieces, B)

        @block.scalar
        def _(act):
            for c in (work_read, proj_read, c_read, s_exp, l_exp, pT_read, cT_read):
                c.open(act)
            act.wait_ge(tables, TABLES)

            def inputs_up(b):
                act.wait_ge(proj_made.sem, proj_made.of(b, 1))
                act.copy(xT[:, :, :].rearrange("p t n -> p (t n)"), proj[0][:, 0:KT * P]).then_inc(proj_read.sem, 1)

            def entries_up(b):
                act.wait_ge(c_made.sem, c_made.of(b, 1))
                act.wait_ge(proj_made.sem, proj_made.of(b - 1))
                for j in range(4):
                    i = act.copy(entT[:, :, j, :], p_c[:, 0:KT * NC].rearrange("p (t c) -> p t c", t=KT))
                i.then_inc(c_read.sem, 1)

            def projected(i, at):
                def run(b):
                    if i < 2:
                        act.wait_ge(rotated.sem, rotated.of(b - 1, i + 1))
                        act.wait_ge(squared.sem, squared.of(b - 1, i + 1))
                    else:
                        act.wait_ge(cT_made.sem, cT_made.of(b - 1))
                    for c in range(NG):
                        act.wait_ge(proj_made.sem, proj_made.of(b, at + c + 1))
                        act.copy(raw[i][:, c * BANK:(c + 1) * BANK], proj[(at + c) % 2][:, :]).then_inc(proj_read.sem, 1)
                return run

            def compressed_up(b):
                act.wait_ge(proj_made.sem, proj_made.of(b, C_AT + 1))
                act.wait_ge(cT_made.sem, cT_made.of(b - 1))
                act.wait_ge(crot_up.sem, crot_up.of(b - 1))
                bank = proj[C_AT % 2]
                act.copy(ckr[:, :], bank[:, 0:D])
                for h in range(G):
                    q = slice(NC * h, NC * (h + 1))
                    last = act.copy(cv[q, h, :], bank[q, D:2 * D])
                last.then_inc(proj_read.sem, 1)

            def compressed_key_up(b):
                act.wait_ge(c_made.sem, c_made.of(b, 2))
                act.copy(ckT[:, :], p_c[:, 0:P]).then_inc(c_read.sem, 1)

            def heads_up(j):
                def run(b):
                    for g in range(NG):
                        n = j * NG + g
                        act.wait_ge(work_made.sem, work_made.of(b, n + 1))
                        dst = (qT, kT)[j][:, g * G:(g + 1) * G, :]
                        act.copy(dst.rearrange("p h t -> p (h t)"), work[n % 2][:, :]).then_inc(work_read.sem, 1)
                return run

            def sparse_exp(b):
                act.wait_ge(s_arg.sem, s_arg.of(b))
                act.wait_ge(c_made.sem, c_made.of(b - 1))
                act.activation(es[:, :, :], scm[:, :, :], ACT.Exp).then_inc(s_exp.sem, 1)

            def exps(g):
                def run(b):
                    act.wait_ge(bias_up.sem, bias_up.of(b, g + 1))
                    act.wait_ge(l_prob.sem, l_prob.of(b, g - 1) if g >= 2 else l_prob.of(b - 1, NG - 1 + g))
                    act.wait_ge(pT_made.sem, pT_made.of(b, g - 1) if g >= 2 else pT_made.of(b - 1, NG - 1 + g))
                    for h in range(G):
                        n = g * G + h
                        i = act.activation(prob[g % 2][:, h, :], work[g % 2][:, h * P:(h + 1) * P], ACT.Exp,
                                           bias=nbias[:, n:n + 1], scale=rqs[:, n:n + 1],
                                           accum_out=lsum[:, n:n + 1])
                    i.then_inc(l_exp.sem, 1)
                return run

            def sparse_up(b):
                act.wait_ge(c_made.sem, c_made.of(b, 4))
                act.wait_ge(cT_made.sem, cT_made.of(b - 1))
                act.copy(psT[:, :, :].rearrange("p g t -> p (g t)"), p_c[:, :]).then_inc(c_read.sem, 1)

            def group(g):
                def run(b):
                    act.wait_ge(pT_made.sem, pT_made.of(b, g + 1))
                    act.wait_ge(cT_made.sem, cT_made.of(b, g - 1) if g >= 2 else cT_made.of(b - 1, NG - 1 + g))
                    act.copy(pT[g % 2][:, :, :].rearrange("p g t -> p (g t)"), p_pT[:, :]).then_inc(pT_read.sem, 1)
                    if g + 2 < NG:
                        exps(g + 2)(b)
                    act.wait_ge(cT_made.sem, cT_made.of(b, g + 1))
                    if g == 0:
                        act.wait_ge(o_made.sem, o_made.of(b - 1))
                    act.copy(cT[g % 2][:, :, :].rearrange("p g t -> p (g t)"), p_cT[:, :]).then_inc(cT_read.sem, 1)
                return run

            pieces = {"turn_q": heads_up(0), "turn_k": heads_up(1), "in": inputs_up, "q": projected(0, Q_AT),
                      "k": projected(1, K_AT), "sparse_exp": sparse_exp, "e0": exps(0), "e1": exps(1),
                      "turn_sparse": sparse_up, "entries": entries_up, "comp_kv": compressed_up,
                      "v": projected(2, V_AT), "comp_key": compressed_key_up}
            pieces.update({f"m{g}": group(g) for g in range(NG)})
            pipeline(act, order, pieces, B)

        @block.vector
        def _(dve):
            for c in (rotated, summed, wsel_up, c_sum, crot_up, rqs_up, s_arg, s_prob, bias_up, l_prob, o_read,
                      var_up, x_up):
                c.open(dve)
            dve.wait_ge(loaded, 16 * LOADS)
            for j, (cos, sin) in enumerate(((cq, sq_tab), (ck_tab, sk_tab), (cc, sc_tab))):
                w = wn[:, min(j, 1), :]
                dve.tensor_tensor(cos[:, :], cos[:, :], w, ALU.mult).then_inc(tables, 1)
                for lo, hi in ((0, ROPE // 2), (ROPE // 2, 0)):
                    dve.tensor_tensor(sin[:, lo:lo + ROPE // 2], sin[:, lo:lo + ROPE // 2],
                                      w[:, hi:hi + ROPE // 2], ALU.mult).then_inc(tables, 1)
            dve.memset(cv[:, :, :], 0.0).then_inc(tables, 1)
            dve.tensor_copy(cmask[:, :, :], over_heads(cmask_f[:, :], NH)).then_inc(tables, 1)
            dve.wait_ge(tables, TABLES)
            comp, turned, sparse, local, tail = (
                Chain(dve, s, n) for s, n in ((comp_steps, 5), (rot_steps, 8), (sparse_steps, 41),
                                              (local_steps, 2 * NG), (tail_steps, 3)))

            def rotate(ch, dst, hbuf, src, cos, sin, heads):
                d3 = dst.rearrange("p (h d) -> p h d", h=heads)
                s3 = src.rearrange("p (h d) -> p h d", h=heads)
                h3 = hbuf.rearrange("p (h d) -> p h d", h=heads)
                ch.mark(dve.tensor_tensor(d3, s3, over_heads(cos[:, :], heads), ALU.mult))
                for lo, hi in ((0, ROPE // 2), (ROPE // 2, 0)):
                    ch.mark(dve.tensor_tensor(h3[:, :, lo:lo + ROPE // 2], s3[:, :, hi:hi + ROPE // 2],
                                              over_heads(sin[:, lo:lo + ROPE // 2], heads), ALU.mult))
                ch.wait()
                return dve.tensor_tensor(d3[:, :, 0:ROPE], d3[:, :, 0:ROPE], h3, ALU.add)

            def token_weights(b):
                dve.wait_ge(c_made.sem, c_made.of(b - 1, 1))
                dve.tensor_scalar(wsel[:, :], member[:, :], wcol[:, bass.ds(b, 1)], None, ALU.mult).then_inc(wsel_up.sem, 1)

            def compressed_keys(b):
                comp.start(b)
                dve.wait_ge(proj_read.sem, proj_read.of(b, C_AT + 1))
                dve.wait_ge(c_made.sem, c_made.of(b - 1, 2))
                dve.wait_ge(root_c.sem, root_c.of(b - 1))
                comp.link(dve.tensor_tensor_reduce(out=csq[:, :], in0=ckr[:, :], in1=ckr[:, :], scale=1.0, scalar=0.0,
                                                   op0=ALU.mult, op1=ALU.add, accum_out=cst[:, 0:1]))
                dve.tensor_scalar(cst[:, 1:2], cst[:, 0:1], 1.0 / D, RMS_EPS, ALU.mult, ALU.add).then_inc(c_sum.sem, 1)
                comp.link(rotate(comp, crot[:, :], chalf[:, :], ckr[:, :], cc, sc_tab, 1))
                dve.wait_ge(root_c.sem, root_c.of(b))
                dve.tensor_scalar(crot[:, :], crot[:, :], cst[:, 2:3], None, ALU.mult).then_inc(crot_up.sem, 1)
                dve.wait_ge(crot_up.sem, crot_up.of(b))
                comp.end()

            def turn(j):
                cos, sin = ((cq, sq_tab), (ck_tab, sk_tab))[j]

                def run(b):
                    turned.b, turned.n = b, 4 * j
                    dve.wait_ge(work_made.sem, work_made.of(b - 1, NG * (j + 1)))
                    dve.wait_ge(proj_read.sem, proj_read.of(b, (Q_AT, K_AT)[j] + 4))
                    dve.wait_ge(rotated.sem, before(rotated, b, j + 1, 1))
                    rotate(turned, rot[j][:, :], half[:, :], raw[j][:, :], cos, sin, NH).then_inc(rotated.sem, 1)
                return run

            def sums(j):
                def run(b):
                    turned.b, turned.n = b, 4 * j + 3
                    dve.wait_ge(squared.sem, squared.of(b, j + 1))
                    dve.wait_ge(root_h.sem, root_h.of(b - 1, j + 1))
                    hs = ssq[:, j * NH:(j + 1) * NH]
                    turned.link(dve.tensor_reduce(hs, sq[:, :].rearrange("p (h d) -> p h d", h=NH), AX.X, ALU.add))
                    dve.tensor_scalar(hs, hs, 1.0 / D, RMS_EPS, ALU.mult, ALU.add).then_inc(summed.sem, 1)
                return run

            def largest(b):
                sparse.start(b)
                dve.wait_ge(root_h.sem, root_h.of(b, 1))
                dve.wait_ge(l_exp.sem, l_exp.of(b - 1))
                dve.tensor_scalar(rqs[:, :], rstd[:, 0:NH], float(D) ** -0.5, None, ALU.mult).then_inc(rqs_up.sem, 1)
                dve.wait_ge(c_made.sem, c_made.of(b, 3))
                dve.wait_ge(s_exp.sem, s_exp.of(b - 1))
                sparse.link(dve.tensor_copy(scm[:, :, :].rearrange("p h c -> p (h c)"), p_c[:, :]))
                sparse.settle()
                for h in range(NH):
                    sparse.mark(dve.max(top[:, h, :], scm[:, h, :]))
                sparse.wait()
                sparse.settle()
                for h in range(NH):
                    sparse.mark(dve.match_replace(repl[:, h, :], top[:, h, :], scm[:, h, :], CHOSEN))
                sparse.link(dve.tensor_scalar(tmax[:, :], top[:, :, 0], NEG / 2, None, ALU.max))
                sparse.link(dve.tensor_tensor(scm[:, :, :], scm[:, :, :], bcast(tmax[:, :], [P, NH, NC]), ALU.subtract))
                dve.wait_ge(rqs_up.sem, rqs_up.of(b))
                dve.tensor_tensor(scm[:, :, :], scm[:, :, :], bcast(rqs[:, :], [P, NH, NC]), ALU.mult).then_inc(s_arg.sem, 1)

            def sparse_prob(b):
                dve.wait_ge(s_exp.sem, s_exp.of(b))
                sparse.link(dve.scalar_tensor_tensor(out=es[:, :, :].rearrange("p h c -> p (h c)"),
                                                     in0=repl[:, :, :].rearrange("p h c -> p (h c)"), scalar=CHOSEN,
                                                     in1=es[:, :, :].rearrange("p h c -> p (h c)"),
                                                     op0=ALU.is_ge, op1=ALU.mult))
                sparse.link(dve.tensor_reduce(tsum[:, :], es[:, :, :], AX.X, ALU.add))
                sparse.link(dve.tensor_scalar(tsum[:, :], tsum[:, :], 1e-9, None, ALU.max))
                sparse.link(dve.reciprocal(tmax[:, :], tsum[:, :]))
                dve.scalar_tensor_tensor(out=es[:, :, :], in0=es[:, :, :], scalar=0.5,
                                         in1=bcast(tmax[:, :], [P, NH, NC]), op0=ALU.mult,
                                         op1=ALU.mult).then_inc(s_prob.sem, 1)
                sparse.end()

            def row_max(g):
                def run(b):
                    local.b, local.n = b, (0, 1, 3, 6)[g]
                    dve.wait_ge(work_made.sem, work_made.of(b, 2 * NG + g + 1))
                    hs = slice(g * G, (g + 1) * G)
                    local.link(dve.tensor_reduce(lmax[:, hs], work[g % 2][:, :].rearrange("p (h k) -> p h k", h=G),
                                                 AX.X, ALU.max))
                    dve.scalar_tensor_tensor(out=nbias[:, hs], in0=lmax[:, hs], scalar=-1.0, in1=rqs[:, hs],
                                             op0=ALU.mult, op1=ALU.mult).then_inc(bias_up.sem, 1)
                return run

            def group(g):
                def run(b):
                    local.b, local.n = b, (2, 4, 5, 7)[g]
                    hs = slice(g * G, (g + 1) * G)
                    dve.wait_ge(l_exp.sem, l_exp.of(b, g + 1))
                    local.link(dve.reciprocal(lrec[:, hs], lsum[:, hs]))
                    dve.scalar_tensor_tensor(out=prob[g % 2][:, :, :], in0=prob[g % 2][:, :, :], scalar=0.5,
                                             in1=bcast(lrec[:, hs], [P, G, P]), op0=ALU.mult,
                                             op1=ALU.mult).then_inc(l_prob.sem, 1)
                return run

            def statistics(b):
                tail.start(b)
                xt = core.x[:, bass.ds(b, 1), :].rearrange("p o h -> p (o h)")
                dve.wait_ge(o_made.sem, o_made.of(b))
                dve.tensor_tensor(y[:, :], p_o[:, 0:H], xt, ALU.add).then_inc(o_read.sem, 1)
                dve.wait_ge(o_read.sem, o_read.of(b))
                tail.link(dve.bn_stats(stats[:, :], y[:, :]))
                tail.settle()
                tail.link(dve.bn_aggr(mv[:, :], stats[:, :]))
                dve.tensor_scalar(mv[:, 1:2], mv[:, 1:2], LN_EPS, None, ALU.add).then_inc(var_up.sem, 1)
                tail.end()

            def layer_norm(b):
                xt = core.x[:, bass.ds(b, 1), :].rearrange("p o h -> p (o h)")
                dve.wait_ge(root_l.sem, root_l.of(b))
                dve.tensor_scalar(xt, y[:, :], mv[:, 0:1], ln_r[:, 0:1], ALU.subtract, ALU.mult).then_inc(x_up.sem, 1)

            pieces = {"sparse": largest, "s0": row_max(0), "s1": row_max(1), "norm1": statistics, "rot_q": turn(0),
                      "sum_q": sums(0), "norm2": layer_norm, "sparse_prob": sparse_prob, "in": token_weights,
                      "top2": row_max(2), "top3": row_max(3), "m0": group(0), "m1": group(1), "even2": group(2),
                      "m3": group(3), "rot_k": turn(1), "sum_k": sums(1), "comp_kv": compressed_keys}
            pipeline(dve, order, pieces, B)


def l0_token_weights(core, wcol):
    nc, A = core.nc, core.A
    with ExitStack() as ctx:
        def sb(name, shape, dt=F32):
            return ctx.enter_context(nc.sbuf_tensor(name, shape, dt))

        wcmp = sb("w0_wcmp", [P, H])
        bcmp = sb("w0_bcmp", [P, 1])
        prod = sb("w0_prod", [P, B, H])
        logit = sb("w0_logit", [P, B])
        shifted = sb("w0_shifted", [B, P])
        grown = sb("w0_grown", [B, P])
        stat = sb("w0_stat", [B, 3, NC])
        turned = ctx.enter_context(nc.psum_tensor("w0_turned", [B, P], F32))
        back = ctx.enter_context(nc.psum_tensor("w0_back", [P, B], F32))
        sem = semaphores(nc, ctx)
        loaded, steps, turns, exped = (sem("w0_" + n)
                                       for n in ("loaded", "steps", "turns", "exped"))
        block = ctx.enter_context(nc.Block())

        @block.sync
        def _(sp):
            sp.dma_start(wcmp[:, :], A["L0_attn_Wcmp"].rearrange("h o -> (h o)").partition_broadcast(P)).then_inc(loaded, 16)
            sp.dma_start(bcmp[:, :], A["L0_attn_bcmp"].partition_broadcast(P)).then_inc(loaded, 16)
            sp.wait_ge(loaded, 32)

        @block.vector
        def _(dve):
            ch = Chain(dve, steps, 9)
            ch.start(0)
            dve.wait_ge(loaded, 32)
            ch.link(dve.tensor_tensor(prod[:, :, :], core.x[:, :, :], over_heads(wcmp[:, :], B), ALU.mult))
            ch.link(dve.tensor_reduce(logit[:, :], prod[:, :, :], AX.X, ALU.add))
            ch.link(dve.tensor_scalar(logit[:, :], logit[:, :], bcmp[:, 0:1], None, ALU.add))
            dve.wait_ge(turns, 1)
            logits = turned[:, :].rearrange("b (c r) -> b c r", r=RATIO)
            ch.link(dve.tensor_reduce(stat[:, 0, :], logits, AX.X, ALU.max))
            ch.link(dve.tensor_tensor(shifted[:, :].rearrange("b (c r) -> b c r", r=RATIO), logits,
                                      bcast(stat[:, 0, :], [B, NC, RATIO]), ALU.subtract))
            dve.wait_ge(exped, 1)
            g3 = grown[:, :].rearrange("b (c r) -> b c r", r=RATIO)
            ch.link(dve.tensor_reduce(stat[:, 1, :], g3, AX.X, ALU.add))
            ch.link(dve.reciprocal(stat[:, 2, :], stat[:, 1, :]))
            ch.link(dve.tensor_tensor(g3, g3, bcast(stat[:, 2, :], [B, NC, RATIO]), ALU.mult))
            dve.wait_ge(turns, 2)
            ch.link(dve.tensor_copy(wcol[:, :], back[:, :]))
            ch.end()

        @block.scalar
        def _(act):
            act.wait_ge(steps, 5)
            act.activation(grown[:, :], shifted[:, :], ACT.Exp).then_inc(exped, 1)

        @block.tensor
        def _(pe):
            pe.wait_ge(steps, 3)
            pe.transpose(turned[:, :], logit[:, :], core.ident[:, :]).then_inc(turns, 1)
            pe.wait_ge(steps, 8)
            pe.transpose(back[:, :], grown[:, :], core.ident[0:B, 0:B]).then_inc(turns, 1)


XH, XD = 16, 16
PAIRS = XH // 2
ROUND = 1.5 * 2.0 ** 23
QMAX = 127.0
AMAX = 255.0
FLOOR = 1e-8


def norm_steps(dve, ch, core, b, y, stats, mv, ln_r, made, p_y, read, var_up, rooted, root_k, x_up):
    xt = core.x[:, bass.ds(b, 1), :].rearrange("p o h -> p (o h)")
    dve.wait_ge(made.sem, made.of(b))
    dve.tensor_tensor(y[:, :], p_y, xt, ALU.add).then_inc(read.sem, 1)
    dve.wait_ge(read.sem, read.of(b))
    ch.link(dve.bn_stats(stats[:, :], y[:, :]))
    ch.settle()
    ch.link(dve.bn_aggr(mv[:, :], stats[:, :]))
    dve.tensor_scalar(mv[:, 1:2], mv[:, 1:2], LN_EPS, None, ALU.add).then_inc(var_up.sem, 1)
    dve.wait_ge(rooted.sem, rooted.of(b, root_k))
    dve.tensor_scalar(xt, y[:, :], mv[:, 0:1], ln_r[:, 0:1], ALU.subtract, ALU.mult).then_inc(x_up.sem, 1)
    dve.wait_ge(x_up.sem, x_up.of(b))


def l0_cross_attention(core):
    nc = core.nc
    with ExitStack() as ctx:
        def sb(name, shape, dt=F32):
            return ctx.enter_context(nc.sbuf_tensor("x0_" + name, shape, dt))

        qz = sb("qz", [P, 2, PAIRS, B, P], BF16)
        kT = sb("kT", [P, PAIRS, B * P], BF16)
        vi = sb("vi", [P, B, H], BF16)
        sv = sb("sv", [P, H])
        sq = sb("sq", [P, B, XH])
        att = sb("att", [P, B, H])
        esum = sb("esum", [P, PAIRS, B, 2, 2])
        x0_operands(core, qz, kT, vi, sv, sq, att)
        x0_attend(core, qz, kT, vi, sq, att, esum)
        x0_output(core, sv, att, esum)


def x0_operands(core, qz, kT, vi, sv, sq, vraw):
    nc, A = core.nc, core.A
    with ExitStack() as ctx:
        def sb(name, shape, dt=F32):
            return ctx.enter_context(nc.sbuf_tensor("x1_" + name, shape, dt))

        def ps(name, shape, dt=F32):
            return ctx.enter_context(nc.psum_tensor("x1_" + name, shape, dt))

        named = semaphores(nc, ctx)

        def sem(name):
            return named("x1_" + name)

        def count(name, per):
            return Count(sem(name), per)

        wq = sb("wq", [P, KT, H])
        wkv = sb("wkv", [P, KT, 2 * H])
        xb, cb = sb("xb", [P, H]), sb("cb", [P, H])
        inT = sb("inT", [P, 2 * KT, P])
        kq = sb("kq", [P, 2, H])
        amax, scl, rec = (sb(n, [P, 2 * XH]) for n in ("amax", "scl", "rec"))
        kval = sb("kval", [P, H])
        krep = sb("krep", [P, XH, 4, XD], BF16)
        qrep = sb("qrep", [P, XH, 4, XD], BF16)
        cmax = sb("cmax", [P, H])
        vstat = sb("vstat", [P, 2, KT])
        svcol = sb("svcol", [P, KT, P])
        rsv = sb("rsv", [P, H])
        p_in, p_kv, p_q = (ps(n, [P, BANK]) for n in ("p_in", "p_kv", "p_q"))
        p_kT, p_qT = (ps(n, [P, 2 * BANK], BF16) for n in ("p_kT", "p_qT"))
        p_v = ps("p_v", [P, BANK])

        loaded, zeroed = sem("loaded"), sem("zeroed")
        ctx_in = count("ctx_in", 16)
        tile_in = count("tile_in", 1)
        turned, in_up = count("turned", 1), count("in_up", 1)
        made, read = count("made", 2), count("read", 2)
        reps = count("reps", 1)
        rep_made, rep_read = count("rep_made", 1), count("rep_read", 2)
        steps = sem("steps")
        v_steps, v_turn = sem("v_steps"), sem("v_turn")
        DVE_STEPS = 12
        block = ctx.enter_context(nc.Block())

        @block.sync
        def _(sp):
            ctx_in.open(sp)
            sp.dma_start(wq[:, :, :], A["L0_xattn_Wq"].rearrange("(t p) n -> p t n", p=P)).then_inc(loaded, 16)
            sp.dma_start(wkv[:, :, :], A["L0_xattn_Wkv"].rearrange("(t p) n -> p t n", p=P)).then_inc(loaded, 16)
            with sp.Fori(0, B) as b:
                sp.wait_ge(turned.sem, turned.of(b - 1))
                sp.dma_start(cb[:, :], A["ctx_2048"][bass.ds(b, 1), :, :].rearrange("o p h -> (o p) h")).then_inc(ctx_in.sem, 16)
            sp.wait_ge(ctx_in.sem, ctx_in.of(B - 1))
            sp.wait_ge(loaded, 32)

        @block.gpsimd
        def _(pool):
            tile_in.open(pool)
            pool.memset(qz[XD * 4:P, 0, :, :, :].rearrange("p a b t -> p (a b t)"), 0.0).then_inc(zeroed, 1)
            pool.wait_ge(zeroed, 1)
            pool.memset(qz[0:XD * 4, 1, :, :, :].rearrange("p a b t -> p (a b t)"), 0.0).then_inc(zeroed, 1)
            pool.wait_ge(zeroed, 2)
            with pool.Fori(0, B) as b:
                pool.wait_ge(turned.sem, turned.of(b - 1))
                pool.tensor_copy(xb[:, :], core.x[:, bass.ds(b, 1), :].rearrange("p o h -> p (o h)")).then_inc(tile_in.sem, 1)

        @block.tensor
        def _(pe):
            for c in (turned, made, rep_made):
                c.open(pe)
            pe.wait_ge(loaded, 32)
            with pe.Fori(0, B) as b:
                pe.wait_ge(tile_in.sem, tile_in.of(b))
                pe.wait_ge(ctx_in.sem, ctx_in.of(b))
                pe.wait_ge(in_up.sem, in_up.of(b - 1))
                for t in range(KT):
                    pe.transpose(p_in[:, t * P:(t + 1) * P], xb[:, t * P:(t + 1) * P], core.ident[:, :])
                for t in range(KT):
                    mm = pe.transpose(p_in[:, (KT + t) * P:(KT + t + 1) * P], cb[:, t * P:(t + 1) * P], core.ident[:, :])
                mm.then_inc(turned.sem, 1)
                pe.wait_ge(in_up.sem, in_up.of(b))
                for j, (bank, w, name, n) in enumerate(((p_kv, wkv, "L0_xattn_bkv", 2 * H), (p_q, wq, "L0_xattn_bq", H))):
                    pe.wait_ge(read.sem, read.of(b - 1, j + 1))
                    pe.matmul(bank[:, 0:n], core.ones[:, :], core.bias(name), start=True, stop=False)
                    for t in range(KT):
                        mm = pe.matmul(bank[:, 0:n], inT[:, (1 - j) * KT + t, :], w[:, t, :],
                                       start=False, stop=(t == KT - 1))
                    mm.then_inc(made.sem, 1)
                pe.wait_ge(reps.sem, reps.of(b))
                pe.wait_ge(rep_read.sem, rep_read.of(b - 1))
                for bank, src in ((p_kT, krep), (p_qT, qrep)):
                    for h in range(PAIRS):
                        mm = pe.transpose(bank[:, h * P:(h + 1) * P],
                                          src[:, 2 * h:2 * h + 2, :, :].rearrange("p a c d -> p (a c d)"), core.identb[:, :])
                mm.then_inc(rep_made.sem, 1)
            pe.wait_ge(v_steps, 1)
            for t in range(KT):
                mm = pe.transpose(p_v[:, t * P:(t + 1) * P], cmax[:, t * P:(t + 1) * P], core.ident[:, :])
            mm.then_inc(v_turn, 1)
            pe.wait_ge(v_steps, 4)
            for t in range(KT):
                mm = pe.matmul(p_v[:, t * P:(t + 1) * P], svcol[:, t, :], core.ident[:, :], start=True, stop=True)
            mm.then_inc(v_turn, 1)

        @block.scalar
        def _(act):
            for c in (in_up, read, rep_read):
                c.open(act)
            act.wait_ge(zeroed, 2)
            with act.Fori(0, B) as b:
                act.wait_ge(turned.sem, turned.of(b))
                act.wait_ge(made.sem, made.of(b - 1))
                act.copy(inT[:, :, :].rearrange("p t n -> p (t n)"), p_in[:, :]).then_inc(in_up.sem, 1)
                act.wait_ge(made.sem, made.of(b, 1))
                act.wait_ge(reps.sem, reps.of(b - 1))
                act.copy(kq[:, 0, :], p_kv[:, 0:H])
                act.copy(vraw[:, bass.ds(b, 1), :].rearrange("p o h -> p (o h)"), p_kv[:, H:2 * H]).then_inc(read.sem, 1)
                act.wait_ge(made.sem, made.of(b, 2))
                act.mul(kq[:, 1, :], p_q[:, 0:H], float(XD) ** -0.5).then_inc(read.sem, 1)
                act.wait_ge(rep_made.sem, rep_made.of(b))
                for par in range(2):
                    r = slice(64 * par, 64 * par + 64)
                    i = act.copy(qz[r, par, :, bass.ds(b, 1), :].rearrange("p a o t -> p a (o t)"),
                                 p_qT[r, :].rearrange("p (a t) -> p a t", a=PAIRS))
                i.then_inc(rep_read.sem, 1)
                act.copy(kT[:, :, bass.ds(b * P, P)], p_kT[:, :].rearrange("p (a t) -> p a t", a=PAIRS)).then_inc(rep_read.sem, 1)
            act.wait_ge(rep_read.sem, rep_read.of(B - 1))

        @block.vector
        def _(dve):
            reps.open(dve)
            dve.memset(krep[:, :, 3, :], 0.0)
            dve.memset(qrep[:, :, 3, :], 0.0)
            ch = Chain(dve, steps, DVE_STEPS)
            kq3 = kq[:, :, :].rearrange("p j (h d) -> p (j h) d", d=XD)
            kv3 = kval[:, :].rearrange("p (h d) -> p h d", d=XD)
            with dve.Fori(0, B) as b:
                ch.start(b)
                dve.wait_ge(read.sem, read.of(b))
                ch.link(dve.tensor_reduce(amax[:, :], kq3, AX.X, ALU.max, apply_absolute_value=True))
                ch.link(dve.tensor_scalar(scl[:, :], amax[:, :], 1.0 / QMAX, FLOOR, ALU.mult, ALU.max))
                ch.mark(dve.reciprocal(rec[:, :], scl[:, :]))
                ch.link(dve.tensor_copy(sq[:, bass.ds(b, 1), :].rearrange("p o h -> p (o h)"), scl[:, XH:]))
                ch.link(dve.tensor_tensor(kq3, kq3, bcast(rec[:, :], [P, 2 * XH, XD]), ALU.mult))
                ch.link(dve.tensor_scalar(kq[:, :, :], kq[:, :, :], ROUND, ROUND, ALU.add, ALU.subtract))
                dve.wait_ge(rep_made.sem, rep_made.of(b - 1))
                ch.mark(dve.tensor_tensor(kv3, kq3[:, 0:XH, :], bcast(scl[:, 0:XH], [P, XH, XD]), ALU.mult))
                ch.mark(dve.tensor_copy(qrep[:, :, 0:3, :],
                                        kq3[:, XH:, :].unsqueeze(2).to_broadcast([P, XH, 3, XD])))
                ch.wait()
                for j in range(3):
                    i = dve.tensor_copy(krep[:, :, j, :], kv3)
                    if j < 2:
                        ch.link(i)
                        i = dve.tensor_tensor(kv3, kv3, krep[:, :, j, :], ALU.subtract)
                        ch.link(i)
                    else:
                        i.then_inc(reps.sem, 1)
                ch.end()
            dve.wait_ge(read.sem, read.of(B - 1))
            dve.tensor_reduce(cmax[:, :], vraw[:, :, :].rearrange("p b h -> p h b"), AX.X, ALU.max,
                              apply_absolute_value=True).then_inc(v_steps, 1)
            dve.wait_ge(v_turn, 1)
            dve.tensor_reduce(vstat[:, 0, :], p_v[:, 0:H].rearrange("p (t n) -> p t n", t=KT), AX.X, ALU.max).then_inc(v_steps, 1)
            dve.wait_ge(v_steps, 2)
            dve.tensor_scalar(vstat[:, 1, :], vstat[:, 0, :], 1.0 / QMAX, FLOOR, ALU.mult, ALU.max).then_inc(v_steps, 1)
            dve.wait_ge(v_steps, 3)
            dve.tensor_copy(svcol[:, :, :], bcast(vstat[:, 1, :], [P, KT, P])).then_inc(v_steps, 1)
            dve.wait_ge(v_turn, 2)
            dve.tensor_copy(sv[:, :], p_v[:, 0:H]).then_inc(v_steps, 1)
            dve.wait_ge(v_steps, 5)
            dve.reciprocal(rsv[:, :], sv[:, :]).then_inc(v_steps, 1)
            dve.wait_ge(v_steps, 6)
            dve.tensor_tensor(vraw[:, :, :], vraw[:, :, :], over_heads(rsv[:, :], B), ALU.mult).then_inc(v_steps, 1)
            dve.wait_ge(v_steps, 7)
            dve.tensor_scalar(vi[:, :, :], vraw[:, :, :], ROUND, ROUND, ALU.add, ALU.subtract).then_inc(v_steps, 1)
            dve.wait_ge(v_steps, 8)


def x0_attend(core, qz, kT, vi, sq, att, esum):
    nc = core.nc
    HALF = B * P // 2
    LOG_AMAX = float(np.log(AMAX))
    with ExitStack() as ctx:
        def sb(name, shape, dt=F32):
            return ctx.enter_context(nc.sbuf_tensor("x2_" + name, shape, dt))

        def ps(name, shape, dt=F32):
            return ctx.enter_context(nc.psum_tensor("x2_" + name, shape, dt))

        sem = semaphores(nc, ctx)

        def count(name, per):
            return Count(sem("x2_" + name), per)

        ints = [sb(f"ints{i}", [P, 2, HALF], U16) for i in range(2)]
        turned = [sb(f"turned{i}", [P, B, P], BF16) for i in range(2)]
        hmax = sb("hmax", [P, 2, 2])
        top = sb("top", [P, 2])
        nb = sb("nb", [P, 2])
        p_s = [[ps("p_s00", [P, HALF]), ps("p_s10", [P, HALF])], [ps("p_s1", [P, HALF])] * 2]
        p_t = ps("p_t", [P, HALF], BF16)
        p_o = ps("p_o", [P, BANK])

        s_made = count("s_made", 4)
        max_up = count("max_up", 4)
        top_up = count("top_up", 2)
        bias_up = count("bias_up", 2)
        e_up = count("e_up", 4)
        t_made = count("t_made", 4)
        t_act = count("t_act", 2)
        t_dve = count("t_dve", 2)
        o_made = count("o_made", 2)
        o_read = count("o_read", 2)
        block = ctx.enter_context(nc.Block())

        def walk(eng, emit):
            emit((0, 0, 0), None)
            with eng.Fori(1, B) as t:
                emit((0, t, t), (0, t - 1, t - 1))
            with eng.Fori(1, PAIRS) as a:
                emit((a, 0, a * B), (a - 1, B - 1, a * B - 1))
                with eng.Fori(1, B) as t:
                    emit((a, t, a * B + t), (a, t - 1, a * B + t - 1))
            emit(None, (PAIRS - 1, B - 1, PAIRS * B - 1))

        def steps(now, before):
            zero, one = now and (*now, 0), now and (*now, 1)
            yield zero, before and (*before, 1), before and (*before, 0)
            yield one, zero, before and (*before, 1)

        @block.tensor
        def _(pe):
            for c in (s_made, t_made, o_made):
                c.open(pe)

            def scores(a, t, n, par, half):
                if half:
                    pe.wait_ge(e_up.sem, e_up.of(n, 1) if par else e_up.of(n - 1, 3))
                else:
                    pe.wait_ge(e_up.sem, e_up.of(n - 1, 2 * par + 2))
                for c in range(2):
                    mm = pe.matmul(p_s[half][par][:, c * BANK:(c + 1) * BANK],
                                   qz[:, par, bass.ds(a, 1), bass.ds(t, 1), :].rearrange("p a t n -> p (a t n)"),
                                   kT[:, bass.ds(a, 1), half * HALF + c * BANK:half * HALF + (c + 1) * BANK].rearrange("p a n -> p (a n)"),
                                   start=True, stop=True)
                mm.then_inc(s_made.sem, 1)

            def turn(a, t, n, par, half):
                if half:
                    pe.wait_ge(e_up.sem, e_up.of(n, 2 * par + 1))
                    pe.wait_ge(t_dve.sem, t_dve.of(n, 1) if par else t_dve.of(n - 1))
                else:
                    pe.wait_ge(e_up.sem, e_up.of(n, 2 * par + 2))
                    pe.wait_ge(t_act.sem, t_act.of(n, par + 1))
                for c in range(8):
                    mm = pe.transpose(p_t[:, c * P:(c + 1) * P],
                                      ints[par][:, half, c * P:(c + 1) * P].bitcast(BF16), core.identb[:, :])
                mm.then_inc(t_made.sem, 1)

            def values(a, t, n, par):
                pe.wait_ge(o_read.sem, o_read.of(n, 1) if par else o_read.of(n - 1))
                pe.wait_ge(t_act.sem, t_act.of(n, par + 1))
                pe.wait_ge(t_dve.sem, t_dve.of(n, par + 1))
                for k in range(B):
                    mm = pe.matmul(p_o[:, 0:XD], turned[par][:, k, :],
                                   vi[:, k, bass.ds(a * (2 * XD) + par * XD, XD)], start=(k == 0), stop=(k == B - 1))
                mm.then_inc(o_made.sem, 1)

            def emit(now, before):
                for here, last, earlier in steps(now, before):
                    if here:
                        scores(*here, 0)
                        scores(*here, 1)
                    if last:
                        turn(*last, 1)
                    if earlier:
                        values(*earlier)
                    if last:
                        turn(*last, 0)

            walk(pe, emit)

        @block.scalar
        def _(act):
            for c in (e_up, t_act):
                c.open(act)

            def leave(a, t, n, par):
                act.wait_ge(t_made.sem, t_made.of(n, 2 * par + 1))
                act.wait_ge(o_made.sem, o_made.of(n - 1, par + 1))
                act.copy(turned[par][:, 8:16, :].rearrange("p k n -> p (k n)"), p_t[:, :].bitcast(U16)).then_inc(t_act.sem, 1)

            def exps(a, t, n, par):
                act.wait_ge(bias_up.sem, bias_up.of(n, par + 1))
                act.wait_ge(t_made.sem, t_made.of(n - 1, 2 * par + 2))
                for half in (1, 0):
                    act.activation(ints[par][:, half, :], p_s[half][par][:, :], ACT.Exp, bias=nb[:, par:par + 1],
                                   scale=sq[:, bass.ds(t, 1), bass.ds(2 * a + par, 1)].rearrange("p t h -> p (t h)"),
                                   accum_out=esum[:, bass.ds(a, 1), bass.ds(t, 1), par, half:half + 1].rearrange("p a t o -> p (a t o)")
                                   ).then_inc(e_up.sem, 1)

            def emit(now, before):
                for here, last, _ in steps(now, before):
                    if last:
                        leave(*last)
                    if here:
                        exps(*here)

            walk(act, emit)

        @block.vector
        def _(dve):
            for c in (max_up, top_up, bias_up, t_dve, o_read):
                c.open(dve)

            def row_max(a, t, n, par):
                for half in range(2):
                    dve.wait_ge(s_made.sem, s_made.of(n, 2 * par + half + 1))
                    dve.tensor_reduce(hmax[:, par, half:half + 1], p_s[half][par][:, :], AX.X, ALU.max).then_inc(max_up.sem, 1)
                dve.wait_ge(max_up.sem, max_up.of(n, 2 * par + 2))
                dve.tensor_scalar(top[:, par:par + 1], hmax[:, par, 0:1], hmax[:, par, 1:2],
                                  sq[:, bass.ds(t, 1), bass.ds(2 * a + par, 1)].rearrange("p t h -> p (t h)"),
                                  ALU.max, ALU.mult).then_inc(top_up.sem, 1)
                dve.wait_ge(top_up.sem, top_up.of(n, par + 1))
                dve.wait_ge(e_up.sem, e_up.of(n - 1, 2 * par + 2))
                dve.tensor_scalar(nb[:, par:par + 1], top[:, par:par + 1], -1.0, LOG_AMAX, ALU.mult, ALU.add).then_inc(bias_up.sem, 1)

            def leave(a, t, n, par):
                dve.wait_ge(t_made.sem, t_made.of(n, 2 * par + 2))
                dve.wait_ge(o_made.sem, o_made.of(n - 1, par + 1))
                dve.tensor_copy(turned[par][:, 0:8, :].rearrange("p k n -> p (k n)"), p_t[:, :].bitcast(U16)).then_inc(t_dve.sem, 1)

            def keep(a, t, n, par):
                dve.wait_ge(o_made.sem, o_made.of(n, par + 1))
                dve.tensor_copy(att[:, bass.ds(t, 1), bass.ds(a * (2 * XD) + par * XD, XD)].rearrange("p t d -> p (t d)"),
                                p_o[:, 0:XD]).then_inc(o_read.sem, 1)

            def emit(now, before):
                for here, last, earlier in steps(now, before):
                    if here:
                        row_max(*here)
                    if last:
                        leave(*last)
                    if earlier:
                        keep(*earlier)

            walk(dve, emit)


def x0_output(core, sv, att, esum):
    nc, A = core.nc, core.A
    with ExitStack() as ctx:
        def sb(name, shape, dt=F32):
            return ctx.enter_context(nc.sbuf_tensor("x3_" + name, shape, dt))

        def ps(name, shape, dt=F32):
            return ctx.enter_context(nc.psum_tensor("x3_" + name, shape, dt))

        sem = semaphores(nc, ctx)

        def count(name, per):
            return Count(sem("x3_" + name), per)

        wp = sb("wp", [P, KT, H])
        den, rden = sb("den", [P, XH]), sb("rden", [P, XH])
        o = sb("o", [P, H])
        oT = sb("oT", [P, KT, P])
        y, stats, mv, ln_r = sb("y", [P, H]), sb("stats", [P, 6]), sb("mv", [P, 2]), sb("ln_r", [P, 1])
        p_oT, p_y = ps("p_oT", [P, BANK]), ps("p_y", [P, BANK])
        loaded = sem("x3_loaded")
        steps = sem("x3_steps")
        o_up, turned, oT_up = count("o_up", 1), count("turned", 1), count("oT_up", 1)
        made, read = count("made", 1), count("read", 1)
        var_up, rooted, x_up = count("var_up", 1), count("rooted", 1), count("x_up", 1)
        block = ctx.enter_context(nc.Block())

        @block.sync
        def _(sp):
            sp.dma_start(wp[:, :, :], A["L0_xattn_Wp"].rearrange("(t p) n -> p t n", p=P)).then_inc(loaded, 16)
            sp.wait_ge(loaded, 16)

        @block.gpsimd
        def _(pool):
            rooted.open(pool)
            with pool.Fori(0, B) as b:
                pool.wait_ge(var_up.sem, var_up.of(b))
                pool.tensor_tensor(ln_r[:, :], mv[:, 1:2], core.neghalf[:, 0:1], ALU.pow).then_inc(rooted.sem, 1)

        @block.tensor
        def _(pe):
            turned.open(pe)
            made.open(pe)
            pe.wait_ge(loaded, 16)
            with pe.Fori(0, B) as b:
                pe.wait_ge(o_up.sem, o_up.of(b))
                pe.wait_ge(oT_up.sem, oT_up.of(b - 1))
                for t in range(KT):
                    mm = pe.transpose(p_oT[:, t * P:(t + 1) * P], o[:, t * P:(t + 1) * P], core.ident[:, :])
                mm.then_inc(turned.sem, 1)
                pe.wait_ge(oT_up.sem, oT_up.of(b))
                pe.wait_ge(read.sem, read.of(b - 1))
                pe.matmul(p_y[:, 0:H], core.ones[:, :], core.bias("L0_xattn_bp"), start=True, stop=False)
                for t in range(KT):
                    mm = pe.matmul(p_y[:, 0:H], oT[:, t, :], wp[:, t, :], start=False, stop=(t == KT - 1))
                mm.then_inc(made.sem, 1)

        @block.scalar
        def _(act):
            oT_up.open(act)
            with act.Fori(0, B) as b:
                act.wait_ge(turned.sem, turned.of(b))
                act.wait_ge(made.sem, made.of(b - 1))
                act.copy(oT[:, :, :].rearrange("p t n -> p (t n)"), p_oT[:, 0:H]).then_inc(oT_up.sem, 1)

        @block.vector
        def _(dve):
            for c in (o_up, read, var_up, x_up):
                c.open(dve)
            ch = Chain(dve, steps, 6)
            with dve.Fori(0, B) as b:
                ch.start(b)
                dve.wait_ge(turned.sem, turned.of(b - 1))
                ch.link(dve.tensor_reduce(den[:, :].rearrange("p (a c) -> p a c", c=2),
                                          esum[:, :, bass.ds(b, 1), :, :].rearrange("p a o c k -> p (a o) c k"), AX.X, ALU.add))
                ch.link(dve.reciprocal(rden[:, :], den[:, :]))
                ch.link(dve.tensor_tensor(o[:, :].rearrange("p (h d) -> p h d", d=XD),
                                          att[:, bass.ds(b, 1), :].rearrange("p o (h d) -> p (o h) d", d=XD),
                                          bcast(rden[:, :], [P, XH, XD]), ALU.mult))
                dve.tensor_tensor(o[:, :], o[:, :], sv[:, :], ALU.mult).then_inc(o_up.sem, 1)
                norm_steps(dve, ch, core, b, y, stats, mv, ln_r, made, p_y[:, 0:H], read, var_up, rooted, 1, x_up)
                ch.end()


def small_attention(core, tag, heads, wqkv, wo, causal, source=None, biases=None, norms=None, bias_o=None):
    nc, A = core.nc, core.A
    dk = H // heads
    per_tile = P // dk
    NG = heads // G
    inputs = 2 if source else 1
    with ExitStack() as ctx:
        def sb(name, shape, dt=F32):
            return ctx.enter_context(nc.sbuf_tensor(f"{tag}_{name}", shape, dt))

        def ps(name, shape, dt=F32):
            return ctx.enter_context(nc.psum_tensor(f"{tag}_{name}", shape, dt))

        named = semaphores(nc, ctx)

        def sem(name):
            return named(f"{tag}_{name}")

        def count(name, per):
            return Count(sem(name), per)

        w = sb("w", [P, KT, 3 * H])
        w_o = sb("w_o", [P, KT, H])
        owner = sb("owner", [P, per_tile])
        gains = sb("gains", [P, 2, H])
        xb, cb = sb("xb", [P, H]), sb("cb", [P, H])
        inT = sb("inT", [P, inputs * KT, P])
        qk = sb("qk", [P, 2, H])
        vaug = sb("vaug", [P, heads, dk + 1])
        sq, ssq, rstd = sb("sq", [P, 2, H]), sb("ssq", [P, 2]), sb("rstd", [P, 2])
        qkT = sb("qkT", [P, 2, KT, P])
        kz = sb("kz", [P, KT, per_tile, P])
        rmax = sb("rmax", [P, heads])
        e = [sb(f"e{i}", [P, G, P]) for i in range(2)]
        eT = [sb(f"eT{i}", [P, G, P]) for i in range(2)]
        rden = sb("rden", [P, heads])
        o = sb("o", [P, H])
        oT = sb("oT", [P, KT, P])
        y, stats, mv, ln_r = sb("y", [P, H]), sb("stats", [P, 6]), sb("mv", [P, 2]), sb("ln_r", [P, 1])
        p_in, p_qk, p_v, p_e, p_o, p_y = (ps(n, [P, BANK]) for n in ("p_in", "p_qk", "p_v", "p_e", "p_o", "p_y"))
        p_s = [ps(f"p_s{i}", [P, BANK]) for i in range(2)]

        loaded, ready = sem("loaded"), sem("ready")
        front_steps, mid_steps, tail_steps = sem("front_steps"), sem("mid_steps"), sem("tail_steps")
        ctx_in = count("ctx_in", 16)
        tile_in = count("tile_in", 1)
        in_turned, in_up = count("in_turned", 1), count("in_up", 1)
        qk_turned, qkT_up = count("qk_turned", 1), count("qkT_up", KT)
        o_turned, oT_up = count("o_turned", 1), count("oT_up", 1)
        made, up = count("made", 2), count("up", 2)
        squares_up, qk_root, qk_up, kz_up = count("squares_up", 1), count("qk_root", 1), count("qk_up", 1), count("kz_up", KT)
        s_made, s_read, e_up = count("s_made", NG), count("s_read", NG), count("e_up", NG)
        e_turned, eT_up, o_part = count("e_turned", NG), count("eT_up", NG), count("o_part", NG)
        o_up = count("o_up", 1)
        y_made, y_read, var_up = count("y_made", 1), count("y_read", 1), count("var_up", 1)
        ln_root, x_up = count("ln_root", 1), count("x_up", 1)
        LOADS = 5 + 2 * bool(norms)
        half = NG // 2
        block = ctx.enter_context(nc.Block())

        order = [(f"m{g}", 1) for g in range(NG)]

        def after(g, *names):
            at = order.index((f"m{g}", 1)) + 1
            while at < len(order) and order[at][0][0] != "m":
                at += 1
            order[at:at] = names

        after(0, ("t_out", 2), ("f_in", 0))
        after(1, ("t_turn", 2), ("f_project", 0))
        after(NG // 2, ("f_norm", 0), ("t_project", 2))
        after(NG // 2, ("f_turn", 0), ("f_cols0", 0), ("t_norm", 2))
        after(NG - 2, ("f_cols1", 0), ("s0", 0))
        after(NG - 1, ("s1", 0), ("f_values", 0))
        order.insert(order.index((f"m{NG - 1}", 1)), ("e0", 0))

        @block.sync
        def _(sp):
            for j, name in enumerate(wqkv):
                sp.dma_start(w[:, :, j * H:(j + 1) * H], A[name].rearrange("(t p) n -> p t n", p=P)).then_inc(loaded, 16)
            sp.dma_start(w_o[:, :, :], A[wo].rearrange("(t p) n -> p t n", p=P)).then_inc(loaded, 16)
            sp.dma_start(owner[:, :], A[f"c_owner{dk}"]).then_inc(loaded, 16)
            for j, name in enumerate(norms or ()):
                sp.dma_start(gains[:, j, :], A[name].partition_broadcast(P)).then_inc(loaded, 16)
            if source:
                ctx_in.open(sp)
                with sp.Fori(0, B) as b:
                    sp.wait_ge(in_turned.sem, in_turned.of(b - 1))
                    sp.dma_start(cb[:, :], A[source][bass.ds(b, 1), :, :].rearrange("o p h -> (o p) h")).then_inc(ctx_in.sem, 16)
                sp.wait_ge(ctx_in.sem, ctx_in.of(B - 1))
            sp.wait_ge(loaded, 16 * LOADS)

        @block.gpsimd
        def _(pool):
            for c in (tile_in, qk_root, kz_up, ln_root):
                c.open(pool)
            pool.wait_ge(loaded, 16 * LOADS)

            def tile_copy(b):
                pool.wait_ge(in_turned.sem, in_turned.of(b - 1))
                pool.tensor_copy(xb[:, :], core.x[:, bass.ds(b, 1), :].rearrange("p o h -> p (o h)")).then_inc(tile_in.sem, 1)

            def norm(b):
                pool.wait_ge(squares_up.sem, squares_up.of(b))
                pool.tensor_tensor(rstd[:, :], ssq[:, :], core.neghalf[:, 0:2], ALU.pow).then_inc(qk_root.sem, 1)

            def spread_keys(t):
                def run(b):
                    pool.wait_ge(qkT_up.sem, qkT_up.of(b, t + 1))
                    pool.wait_ge(s_made.sem, s_made.of(b - 1, (t + 1) * half))
                    pool.tensor_tensor(kz[:, t, :, :], over_heads(qkT[:, 1, t, :], per_tile),
                                       bcast(owner[:, :], [P, per_tile, P]), ALU.mult).then_inc(kz_up.sem, 1)
                return run

            def root(b):
                pool.wait_ge(var_up.sem, var_up.of(b))
                pool.tensor_tensor(ln_r[:, :], mv[:, 1:2], core.neghalf[:, 0:1], ALU.pow).then_inc(ln_root.sem, 1)

            pieces = {"f_in": tile_copy, "f_cols0": spread_keys(0), "f_cols1": spread_keys(1), "t_norm": root}
            if norms:
                pieces["f_norm"] = norm
            pipeline(pool, order, pieces, B)

        @block.tensor
        def _(pe):
            for c in (in_turned, qk_turned, o_turned, made, s_made, e_turned, o_part, y_made):
                c.open(pe)
            pe.wait_ge(loaded, 16 * LOADS)

            def turn_in(b):
                pe.wait_ge(tile_in.sem, tile_in.of(b))
                pe.wait_ge(qkT_up.sem, qkT_up.of(b - 1))
                if source:
                    pe.wait_ge(ctx_in.sem, ctx_in.of(b))
                for i, src in enumerate((xb, cb)[:inputs]):
                    for t in range(KT):
                        mm = pe.transpose(p_in[:, (i * KT + t) * P:(i * KT + t + 1) * P], src[:, t * P:(t + 1) * P], core.ident[:, :])
                mm.then_inc(in_turned.sem, 1)

            def project(b):
                pe.wait_ge(in_up.sem, in_up.of(b))

                def one(out, i, first, last=True):
                    at = KT * (inputs - 1) * (i > 0)
                    if biases:
                        pe.matmul(out, core.ones[:, :], core.bias(biases[i]), start=first, stop=False)
                    for t in range(KT):
                        mm = pe.matmul(out, inT[:, at + t, :], w[:, t, i * H:(i + 1) * H],
                                       start=first and not biases and t == 0, stop=last and t == KT - 1)
                    return mm

                pe.wait_ge(up.sem, up.of(b - 1))
                one(p_qk[:, 0:H], 0, True, last=False)
                one(p_qk[:, H:2 * H], 1, False).then_inc(made.sem, 1)
                one(p_v[:, 0:H], 2, True).then_inc(made.sem, 1)

            def turn_qk(b):
                pe.wait_ge(qk_up.sem, qk_up.of(b))
                for j in range(2):
                    for t in range(KT):
                        mm = pe.transpose(p_in[:, (j * KT + t) * P:(j * KT + t + 1) * P], qk[:, j, t * P:(t + 1) * P], core.ident[:, :])
                mm.then_inc(qk_turned.sem, 1)

            def scores(g):
                def run(b):
                    t, lo = g // half, g * G % per_tile
                    pe.wait_ge(kz_up.sem, kz_up.of(b, t + 1))
                    pe.wait_ge(s_read.sem, s_read.of(b, g - 1) if g >= 2 else s_read.of(b - 1, NG - 1 + g))
                    if causal:
                        pe.matmul(p_s[g % 2][:, :], core.identb[:, :], core.causal[:, :, :].rearrange("p g k -> p (g k)"),
                                  start=True, stop=False)
                    pe.matmul(p_s[g % 2][:, :], qkT[:, 0, t, :], kz[:, t, lo:lo + G, :].rearrange("p g k -> p (g k)"),
                              start=not causal, stop=True).then_inc(s_made.sem, 1)
                return run

            def group(g):
                def run(b):
                    pe.wait_ge(e_up.sem, e_up.of(b, g + 1))
                    pe.wait_ge(eT_up.sem, eT_up.of(b, g))
                    for h in range(G):
                        mm = pe.transpose(p_e[:, h * P:(h + 1) * P], e[g % 2][:, h, :], core.ident[:, :])
                    mm.then_inc(e_turned.sem, 1)
                    if g + 2 < NG:
                        scores(g + 2)(b)
                    pe.wait_ge(eT_up.sem, eT_up.of(b, g + 1))
                    if g == 0:
                        pe.wait_ge(o_up.sem, o_up.of(b - 1))
                        pe.wait_ge(up.sem, up.of(b))
                    for h in range(G):
                        n = g * G + h
                        mm = pe.matmul(p_o[:, n * (dk + 1):(n + 1) * (dk + 1)], eT[g % 2][:, h, :], vaug[:, n, :],
                                       start=(n == 0), stop=(n == heads - 1))
                    mm.then_inc(o_part.sem, 1)
                return run

            def turn_out(b):
                pe.wait_ge(o_up.sem, o_up.of(b))
                pe.wait_ge(y_read.sem, y_read.of(b - 1))
                for t in range(KT):
                    mm = pe.transpose(p_y[:, H + t * P:H + (t + 1) * P], o[:, t * P:(t + 1) * P], core.ident[:, :])
                mm.then_inc(o_turned.sem, 1)

            def output(b):
                pe.wait_ge(oT_up.sem, oT_up.of(b))
                if bias_o:
                    pe.matmul(p_y[:, 0:H], core.ones[:, :], core.bias(bias_o), start=True, stop=False)
                for t in range(KT):
                    mm = pe.matmul(p_y[:, 0:H], oT[:, t, :], w_o[:, t, :], start=(not bias_o and t == 0), stop=(t == KT - 1))
                mm.then_inc(y_made.sem, 1)

            pieces = {"f_in": turn_in, "f_project": project, "f_turn": turn_qk, "s0": scores(0), "s1": scores(1),
                      "t_turn": turn_out, "t_project": output}
            pieces.update({f"m{g}": group(g) for g in range(NG)})
            pipeline(pe, order, pieces, B)

        @block.scalar
        def _(act):
            for c in (in_up, qkT_up, oT_up, up, e_up, eT_up):
                c.open(act)
            act.wait_ge(ready, 1)

            def inputs_up(b):
                act.wait_ge(in_turned.sem, in_turned.of(b))
                act.wait_ge(made.sem, made.of(b - 1))
                act.copy(inT[:, :, :].rearrange("p t n -> p (t n)"), p_in[:, 0:inputs * H]).then_inc(in_up.sem, 1)

            def queries_up(b):
                act.wait_ge(made.sem, made.of(b, 1))
                act.wait_ge(qk_turned.sem, qk_turned.of(b - 1))
                act.copy(qk[:, :, :].rearrange("p j n -> p (j n)"), p_qk[:, :]).then_inc(up.sem, 1)

            def values_up(b):
                act.wait_ge(made.sem, made.of(b, 2))
                act.wait_ge(o_part.sem, o_part.of(b - 1))
                act.copy(vaug[:, :, 0:dk], p_v[:, 0:H].rearrange("p (h d) -> p h d", d=dk)).then_inc(up.sem, 1)

            def columns(t):
                def run(b):
                    act.wait_ge(qk_turned.sem, qk_turned.of(b))
                    act.wait_ge(s_made.sem, s_made.of(b - 1, (t + 1) * half))
                    act.wait_ge(kz_up.sem, kz_up.of(b - 1, t + 1))
                    act.copy(qkT[:, :, t, :], p_in[:, :].rearrange("p (j t n) -> p j t n", j=2, t=KT)[:, :, t, :]).then_inc(qkT_up.sem, 1)
                return run

            def exps(g):
                def run(b):
                    act.wait_ge(s_read.sem, s_read.of(b, g + 1))
                    ef = e[g % 2][:, :, :].rearrange("p g k -> p (g k)")
                    act.activation(ef, ef, ACT.Exp, scale=float(dk) ** -0.5).then_inc(e_up.sem, 1)
                return run

            def group(g):
                def run(b):
                    if g + 1 < NG:
                        exps(g + 1)(b)
                    act.wait_ge(e_turned.sem, e_turned.of(b, g + 1))
                    act.wait_ge(o_part.sem, o_part.of(b, g - 1) if g >= 2 else o_part.of(b - 1, NG - 1 + g))
                    act.copy(eT[g % 2][:, :, :].rearrange("p g k -> p (g k)"), p_e[:, :]).then_inc(eT_up.sem, 1)
                return run

            def output_up(b):
                act.wait_ge(o_turned.sem, o_turned.of(b))
                act.wait_ge(y_made.sem, y_made.of(b - 1))
                act.copy(oT[:, :, :].rearrange("p t n -> p (t n)"), p_y[:, H:2 * H]).then_inc(oT_up.sem, 1)

            pieces = {"f_in": inputs_up, "f_project": queries_up, "f_values": values_up, "f_cols0": columns(0),
                      "f_cols1": columns(1), "e0": exps(0), "t_turn": output_up}
            pieces.update({f"m{g}": group(g) for g in range(NG)})
            pipeline(act, order, pieces, B)

        @block.vector
        def _(dve):
            for c in (squares_up, qk_up, s_read, o_up, y_read, var_up, x_up):
                c.open(dve)
            dve.memset(vaug[:, :, dk:dk + 1], 1.0).then_inc(ready, 1)
            dve.wait_ge(loaded, 16 * LOADS)
            front = Chain(dve, front_steps, 2)
            mid = Chain(dve, mid_steps, NG)
            tail = Chain(dve, tail_steps, 4)

            def sums(b):
                front.start(b)
                dve.wait_ge(up.sem, up.of(b, 1))
                front.link(dve.tensor_tensor(sq[:, :, :], qk[:, :, :], qk[:, :, :], ALU.mult))
                dve.wait_ge(qk_root.sem, qk_root.of(b - 1))
                front.link(dve.tensor_reduce(ssq[:, :], sq[:, :, :], AX.X, ALU.add))
                dve.tensor_scalar(ssq[:, :], ssq[:, :], 1.0 / H, RMS_EPS, ALU.mult, ALU.add).then_inc(squares_up.sem, 1)
                front.end()

            def norm(b):
                dve.wait_ge(qk_root.sem, qk_root.of(b))
                for j in range(2):
                    i = dve.scalar_tensor_tensor(out=qk[:, j, :], in0=qk[:, j, :], scalar=rstd[:, j:j + 1],
                                                 in1=gains[:, j, :], op0=ALU.mult, op1=ALU.mult)
                i.then_inc(qk_up.sem, 1)

            def no_norm(b):
                dve.wait_ge(up.sem, up.of(b, 1))
                dve.sem_inc(qk_up.sem, 1)

            def shift(g):
                def run(b):
                    if g == 0:
                        mid.start(b)
                    dve.wait_ge(s_made.sem, s_made.of(b, g + 1))
                    dve.wait_ge(e_turned.sem, e_turned.of(b, g - 1) if g >= 2 else e_turned.of(b - 1, NG - 1 + g))
                    s3 = p_s[g % 2][:, :].rearrange("p (h k) -> p h k", h=G)
                    top = rmax[:, g * G:(g + 1) * G]
                    mid.b, mid.n = b, g
                    mid.link(dve.tensor_reduce(top, s3, AX.X, ALU.max))
                    dve.tensor_tensor(e[g % 2][:, :, :], s3, bcast(top, [P, G, P]), ALU.subtract).then_inc(s_read.sem, 1)
                return run

            def output(b):
                tail.start(b)
                dve.wait_ge(o_part.sem, o_part.of(b))
                dve.wait_ge(o_turned.sem, o_turned.of(b - 1))
                o3 = p_o[:, 0:heads * (dk + 1)].rearrange("p (h d) -> p h d", d=dk + 1)
                tail.link(dve.reciprocal(rden[:, :].unsqueeze(2), o3[:, :, dk:dk + 1]))
                dve.tensor_tensor(o[:, :].rearrange("p (h d) -> p h d", d=dk), o3[:, :, 0:dk],
                                  bcast(rden[:, :], [P, heads, dk]), ALU.mult).then_inc(o_up.sem, 1)

            def layer_norm(b):
                tail.b, tail.n = b, 1
                norm_steps(dve, tail, core, b, y, stats, mv, ln_r, y_made, p_y[:, 0:H], y_read, var_up, ln_root, 1, x_up)
                tail.end()

            pieces = {"f_project": sums if norms else no_norm, "s0": shift(0), "s1": shift(1),
                      "t_out": output, "t_norm": layer_norm}
            if norms:
                pieces["f_norm"] = norm
            pieces.update({f"m{g}": shift(g + 2) for g in range(NG - 2)})
            pipeline(dve, order, pieces, B)


def l1_self_attention(core):
    small_attention(core, "s1", 32, ("L1_attn_Wq", "L1_attn_Wk", "L1_attn_Wv"), "L1_attn_Wo", causal=True)


def l1_cross_attention(core):
    small_attention(core, "c1", 16, ("L1_xattn_Wq", "L1_xattn_Wk_img", "L1_xattn_Wv_img"), "L1_xattn_Wo", causal=False,
                    source="ctx_2048", biases=("L1_xattn_bq", "L1_xattn_bk_img", "L1_xattn_bv_img"),
                    norms=("L1_xattn_gq", "L1_xattn_gk_img"), bias_o="L1_xattn_bo")


EXPERTS, CHOICES = 16, 6
EI, SI = 176, 352
GROUP = 4
NT = GROUP * P


def feed_forward(core, tag, width, loads, experts):
    nc, A = core.nc, core.A
    tiles = -(-width // P)
    with ExitStack() as ctx:
        def sb(name, shape, dt=F32):
            return ctx.enter_context(nc.sbuf_tensor(f"{tag}_{name}", shape, dt))

        def ps(name, shape, dt=F32):
            return ctx.enter_context(nc.psum_tensor(f"{tag}_{name}", shape, dt))

        named = semaphores(nc, ctx)

        def sem(name):
            return named(f"{tag}_{name}")

        def count(name, per):
            return Count(sem(name), per)

        wg, wu = sb("wg", [P, KT, width]), sb("wu", [P, KT, width])
        wd = sb("wd", [P, tiles, H])
        x4 = sb("x4", [P, GROUP, H])
        xT = sb("xT", [P, KT, NT])
        act_g = [sb(f"act_g{i}", [P, NT]) for i in range(2)]
        h = [sb(f"h{i}", [P, NT]) for i in range(2)]
        y = sb("y", [P, GROUP, H])
        stats, mv, ln_r = sb("stats", [P, GROUP, 6]), sb("mv", [P, GROUP, 2]), sb("ln_r", [P, GROUP])
        p_g = [ps(f"p_g{i}", [P, BANK]) for i in range(2)]
        p_u = [ps(f"p_u{i}", [P, BANK]) for i in range(2)]
        p_c = [ps(f"p_c{i}", [P, BANK]) for i in range(2)]
        p_y = [ps(f"p_y{i}", [P, BANK]) for i in range(2)]
        if experts:
            w_r = sb("w_r", [P, KT, EXPERTS])
            spread = sb("spread", [64, tiles, P], BF16)
            spread_f = sb("spread_f", [64, P])
            rstat = sb("rstat", [P, 3, GROUP])
            logit = sb("logit", [P, GROUP, EXPERTS])
            prob = sb("prob", [P, GROUP, EXPERTS + 2])
            repl = sb("repl", [P, GROUP, EXPERTS + 2])
            best = sb("best", [P, GROUP, 8])
            comb = sb("comb", [P, GROUP, EXPERTS])
            parts = sb("parts", [P, GROUP, 4, EXPERTS], BF16)
            combT = sb("combT", [64, NT], BF16)

        loaded, steps, ready = sem("loaded"), sem("steps"), sem("ready")
        tile_in = count("tile_in", 1)
        turned, xT_up = count("turned", 1), count("xT_up", 1)
        gate_made, up_made = count("gate_made", tiles), count("up_made", tiles)
        gate_up, h_up = count("gate_up", tiles), count("h_up", tiles)
        down = count("down", tiles)
        y_read, var_up, rooted, x_up = count("y_read", 1), count("var_up", 1), count("rooted", 1), count("x_up", 1)
        if experts:
            r_made, r_in, r_exp = count("r_made", 2), count("r_in", 1), count("r_exp", 1)
            parts_up, combT_up, c_made = count("parts_up", 1), count("combT_up", 1), count("c_made", tiles)
            h_raw = count("h_raw", tiles)
            spread_in = sem("spread_in")
        LOADS = len(list(loads(A, wg, wu, wd))) + bool(experts)
        STEPS = 3 + (13 if experts else 0)
        block = ctx.enter_context(nc.Block())

        @block.sync
        def _(sp):
            n = 0
            for dst, src in loads(A, wg, wu, wd):
                sp.dma_start(dst, src).then_inc(loaded, 16)
                n += 1
            if experts:
                sp.dma_start(w_r[:, :, :], A["L1_ffn_gate_w"].rearrange("(t p) n -> p t n", p=P)).then_inc(loaded, 16)
                for t in range(tiles):
                    if t:
                        sp.wait_ge(ready, t)
                    sp.dma_start(spread_f[:, :], A["c_spread"][t]).then_inc(spread_in, 16)
                sp.wait_ge(spread_in, 16 * tiles)
            sp.wait_ge(loaded, 16 * LOADS)

        @block.gpsimd
        def _(pool):
            for c in (tile_in, rooted):
                c.open(pool)
            with pool.Fori(0, B // GROUP) as b:
                pool.wait_ge(y_read.sem, y_read.of(b - 1))
                pool.tensor_copy(x4[:, :, :], core.x[:, bass.ds(b * GROUP, GROUP), :]).then_inc(tile_in.sem, 1)
                pool.wait_ge(var_up.sem, var_up.of(b))
                pool.tensor_tensor(ln_r[:, :], mv[:, :, 1], core.neghalf[:, 0:GROUP], ALU.pow).then_inc(rooted.sem, 1)

        @block.tensor
        def _(pe):
            for c in (turned, gate_made, up_made, down) + ((r_made, c_made) if experts else ()):
                c.open(pe)
            pe.wait_ge(loaded, 16 * LOADS)
            with pe.Fori(0, B // GROUP) as b:
                pe.wait_ge(tile_in.sem, tile_in.of(b))
                pe.wait_ge(gate_up.sem, gate_up.of(b - 1))
                for t in range(KT):
                    for j in range(GROUP):
                        mm = pe.transpose(p_g[t][:, j * P:(j + 1) * P], x4[:, j, t * P:(t + 1) * P], core.ident[:, :])
                mm.then_inc(turned.sem, 1)
                pe.wait_ge(xT_up.sem, xT_up.of(b))

                def tile_rows(n):
                    return min(P, width - n * P)

                def gate_and_up(n):
                    m = tile_rows(n)
                    for bank, w, c, freed in ((p_g, wg, gate_made, gate_up), (p_u, wu, up_made, h_raw if experts else h_up)):
                        pe.wait_ge(freed.sem, freed.of(b, n - 1) if n >= 2 else freed.of(b - 1))
                        for t in range(KT):
                            mm = pe.matmul(bank[n % 2][0:m, :], w[:, t, n * P:n * P + m], xT[:, t, :],
                                           start=(t == 0), stop=(t == KT - 1))
                        mm.then_inc(c.sem, 1)

                def weights(n):
                    m = tile_rows(n)
                    pe.wait_ge(h_up.sem, h_up.of(b, n - 1) if n >= 2 else h_up.of(b - 1))
                    pe.matmul(p_c[n % 2][0:m, :], spread[:, n, 0:m], combT[:, :], start=True, stop=True).then_inc(c_made.sem, 1)

                def project(n):
                    m = tile_rows(n)
                    pe.wait_ge(h_up.sem, h_up.of(b, n + 1))
                    if n == 0:
                        pe.wait_ge(y_read.sem, y_read.of(b - 1))
                    for j in range(GROUP):
                        mm = pe.matmul(p_y[j // 2][:, (j % 2) * H:(j % 2 + 1) * H], h[n % 2][0:m, j * P:(j + 1) * P],
                                       wd[0:m, n, :], start=(n == 0 and j % 2 == 0), stop=(n == tiles - 1 and j % 2 == 1))
                    mm.then_inc(down.sem, 1)

                if experts:
                    pe.wait_ge(h_up.sem, h_up.of(b - 1))
                    for j in range(GROUP):
                        for t in range(KT):
                            mm = pe.matmul(p_c[0][:, j * EXPERTS:(j + 1) * EXPERTS], xT[:, t, j * P:(j + 1) * P], w_r[:, t, :],
                                           start=(j == 0 and t == 0), stop=(j == GROUP - 1 and t == KT - 1))
                    mm.then_inc(r_made.sem, 1)
                gate_and_up(0)
                gate_and_up(1)
                if experts:
                    pe.wait_ge(ready, tiles)
                    pe.wait_ge(parts_up.sem, parts_up.of(b))
                    for j in range(GROUP):
                        mm = pe.transpose(p_c[1][0:64, 0:NT // 2].bitcast(BF16)[:, j * P:(j + 1) * P],
                                          parts[:, j, :, :].rearrange("p a e -> p (a e)"), core.identb[:, :])
                    mm.then_inc(r_made.sem, 1)
                    pe.wait_ge(combT_up.sem, combT_up.of(b))
                    weights(0)
                for n in range(tiles):
                    if experts and n + 1 < tiles:
                        weights(n + 1)
                    if n + 2 < tiles:
                        gate_and_up(n + 2)
                    project(n)

        @block.scalar
        def _(act):
            for c in (xT_up, gate_up) + ((r_exp, combT_up) if experts else ()):
                c.open(act)
            with act.Fori(0, B // GROUP) as b:
                act.wait_ge(turned.sem, turned.of(b))
                act.wait_ge(up_made.sem, up_made.of(b - 1))
                for t in range(KT):
                    i = act.copy(xT[:, t, :], p_g[t][:, :])
                i.then_inc(xT_up.sem, 1)
                if experts:
                    act.wait_ge(r_in.sem, r_in.of(b))
                    act.activation(prob[:, :, 0:EXPERTS], logit[:, :, :], ACT.Exp).then_inc(r_exp.sem, 1)
                    act.wait_ge(r_made.sem, r_made.of(b, 2))
                    act.wait_ge(c_made.sem, c_made.of(b - 1))
                    act.copy(combT[:, :], p_c[1][0:64, 0:NT // 2].bitcast(BF16)).then_inc(combT_up.sem, 1)
                for n in range(tiles):
                    m = min(P, width - n * P)
                    act.wait_ge(gate_made.sem, gate_made.of(b, n + 1))
                    freed = h_raw if experts else h_up
                    act.wait_ge(freed.sem, freed.of(b, n - 1) if n >= 2 else freed.of(b - 1))
                    act.activation(act_g[n % 2][0:m, :], p_g[n % 2][0:m, :], ACT.Silu).then_inc(gate_up.sem, 1)

        @block.vector
        def _(dve):
            for c in (h_up, y_read, var_up, x_up) + ((r_in, parts_up, h_raw) if experts else ()):
                c.open(dve)
            if experts:
                dve.memset(prob[:, :, EXPERTS:], 2.0)
                dve.memset(parts[:, :, 3, :], 0.0).then_inc(steps, 1)
                dve.wait_ge(steps, 1)
                dve.memset(parts[:, :, 3, 0:1], 1.0).then_inc(steps, 1)
                for t in range(tiles):
                    dve.wait_ge(spread_in, 16 * (t + 1))
                    dve.tensor_copy(spread[:, t, :], spread_f[:, :]).then_inc(ready, 1)
            ch = Chain(dve, steps, STEPS, base=2 if experts else 0)
            with dve.Fori(0, B // GROUP) as b:
                ch.start(b)
                if experts:
                    dve.wait_ge(r_made.sem, r_made.of(b, 1))
                    r3 = p_c[0][:, 0:GROUP * EXPERTS].rearrange("p (g e) -> p g e", e=EXPERTS)
                    pr = prob[:, :, 0:EXPERTS]
                    ch.link(dve.tensor_reduce(rstat[:, 0, :], r3, AX.X, ALU.max))
                    dve.tensor_tensor(logit[:, :, :], r3, bcast(rstat[:, 0, :], [P, GROUP, EXPERTS]), ALU.subtract).then_inc(r_in.sem, 1)
                    dve.wait_ge(r_exp.sem, r_exp.of(b))
                    ch.link(dve.tensor_reduce(rstat[:, 1, :], pr, AX.X, ALU.add))
                    ch.link(dve.reciprocal(rstat[:, 2, :], rstat[:, 1, :]))
                    ch.link(dve.tensor_tensor(pr, pr, bcast(rstat[:, 2, :], [P, GROUP, EXPERTS]), ALU.mult))
                    ch.settle()
                    for j in range(GROUP):
                        i = dve.max(best[:, j, :], prob[:, j, :])
                    ch.link(i)
                    ch.settle()
                    for j in range(GROUP):
                        i = dve.match_replace(repl[:, j, :], best[:, j, :], prob[:, j, :], CHOSEN)
                    ch.link(i)
                    ch.link(dve.scalar_tensor_tensor(out=comb[:, :, :], in0=repl[:, :, 0:EXPERTS], scalar=CHOSEN, in1=pr,
                                                     op0=ALU.is_ge, op1=ALU.mult))
                    dve.wait_ge(r_made.sem, r_made.of(b - 1))
                    for j in range(3):
                        i = dve.tensor_copy(parts[:, :, j, :], comb[:, :, :])
                        if j < 2:
                            ch.link(i)
                            ch.link(dve.tensor_tensor(comb[:, :, :], comb[:, :, :], parts[:, :, j, :], ALU.subtract))
                        else:
                            i.then_inc(parts_up.sem, 1)
                for n in range(tiles):
                    m = min(P, width - n * P)
                    dve.wait_ge(up_made.sem, up_made.of(b, n + 1))
                    dve.wait_ge(gate_up.sem, gate_up.of(b, n + 1))
                    dve.wait_ge(down.sem, down.of(b, n - 1) if n >= 2 else down.of(b - 1))
                    i = dve.tensor_tensor(h[n % 2][0:m, :], act_g[n % 2][0:m, :], p_u[n % 2][0:m, :], ALU.mult)
                    if experts:
                        i.then_inc(h_raw.sem, 1)
                        dve.wait_ge(h_raw.sem, h_raw.of(b, n + 1))
                        dve.wait_ge(c_made.sem, c_made.of(b, n + 1))
                        i = dve.tensor_tensor(h[n % 2][0:m, :], h[n % 2][0:m, :], p_c[n % 2][0:m, :], ALU.mult)
                    i.then_inc(h_up.sem, 1)
                dve.wait_ge(down.sem, down.of(b))
                for i in range(2):
                    ins = dve.tensor_tensor(y[:, 2 * i:2 * i + 2, :].rearrange("p g h -> p (g h)"), p_y[i][:, :],
                                            x4[:, 2 * i:2 * i + 2, :].rearrange("p g h -> p (g h)"), ALU.add)
                ins.then_inc(y_read.sem, 1)
                dve.wait_ge(y_read.sem, y_read.of(b))
                for j in range(GROUP):
                    ins = dve.bn_stats(stats[:, j, :], y[:, j, :])
                ch.link(ins)
                ch.settle()
                for j in range(GROUP):
                    ins = dve.bn_aggr(mv[:, j, :], stats[:, j, :])
                ch.link(ins)
                dve.tensor_scalar(mv[:, :, 1], mv[:, :, 1], LN_EPS, None, ALU.add).then_inc(var_up.sem, 1)
                dve.wait_ge(rooted.sem, rooted.of(b))
                for j in range(GROUP):
                    ins = dve.tensor_scalar(core.x[:, bass.ds(b * GROUP + j, 1), :].rearrange("p o h -> p (o h)"), y[:, j, :],
                                            mv[:, j, 0:1], ln_r[:, j:j + 1], ALU.subtract, ALU.mult)
                ins.then_inc(x_up.sem, 1)
                dve.wait_ge(x_up.sem, x_up.of(b))
                ch.end()


def l0_feed_forward(core):
    inter = 1024

    def loads(A, wg, wu, wd):
        w = A["L0_ffn_w_gate_up"].rearrange("(t p) n -> p t n", p=P)
        yield wg[:, :, :], w[:, :, 0:inter]
        yield wu[:, :, :], w[:, :, inter:]
        yield wd[:, :, :], A["L0_ffn_w_down"].rearrange("(k p) n -> p k n", p=P)

    feed_forward(core, "f0", inter, loads, experts=False)


def l1_feed_forward(core):
    wide = EXPERTS * EI

    def loads(A, wg, wu, wd):
        for t in range(KT):
            rows = slice(t * P, (t + 1) * P)
            for j, dst in enumerate((wg, wu)):
                yield (dst[:, t, 0:wide].rearrange("p (e i) -> p e i", i=EI),
                       A["L1_ffn_w1"][rows, :, j * EI:(j + 1) * EI])
                yield dst[:, t, wide:], A["L1_ffn_shared_w1"][rows, j * SI:(j + 1) * SI]
        yield (wd[:, 0:wide // P, :],
               A["L1_ffn_w2"].rearrange("e i h -> (e i) h").rearrange("(k p) h -> p k h", p=P))
        whole = SI // P
        yield (wd[:, wide // P:wide // P + whole, :],
               A["L1_ffn_shared_w2"][0:whole * P, :].rearrange("(k p) h -> p k h", p=P))
        yield wd[0:SI - whole * P, wide // P + whole, :], A["L1_ffn_shared_w2"][whole * P:, :]

    feed_forward(core, "f1", wide + SI, loads, experts=True)


def constants():
    pos = np.arange(P)
    half = ROPE // 2
    inv = (1.0 / np.power(np.float32(10000.0), np.arange(half, dtype=np.float32) * np.float32(2.0 / ROPE))).astype(np.float32)

    def rope(at):
        ang = at.astype(np.float32)[:, None] * inv[None, :]
        cos, sin = np.cos(ang), np.sin(ang)
        return (np.concatenate([cos, cos, np.ones((len(at), D - ROPE))], axis=1).astype(np.float32),
                np.concatenate([-sin, sin], axis=1).astype(np.float32))

    c = {}
    c["c_ident"] = np.eye(P, dtype=np.float32)
    c["c_causal"] = np.where(pos[None, :] <= pos[:, None], 0, NEG).astype(np.float32)
    c["c_cos"], c["c_sin"] = rope(pos)
    ends = np.arange(1, NC + 1) * RATIO - 1
    c["c_cos_c"], c["c_sin_c"] = rope(ends[pos % NC])
    c["c_cmask"] = np.where(ends[None, :] <= pos[:, None], 0, NEG).astype(np.float32)
    c["c_member"] = (pos[:, None] // RATIO == np.arange(NC)[None, :]).astype(np.float32)
    for dk in (8, 16):
        c[f"c_owner{dk}"] = (pos[:, None] // dk == np.arange(P // dk)[None, :]).astype(np.float32)
    wide = EXPERTS * EI
    row = np.arange(-(-(wide + SI) // P) * P)
    owner = np.where(row < wide, row // EI, 3 * EXPERTS)
    spread = np.zeros((64, len(row)), np.float32)
    for j in range(3):
        spread += np.arange(64)[:, None] == np.where(row < wide, owner + j * EXPERTS, -1)[None, :]
    spread[3 * EXPERTS, :] = row >= wide
    c["c_spread"] = np.ascontiguousarray(spread.reshape(64, -1, P).transpose(1, 0, 2))
    return c


LAYERS = [l0_cross_attention, l0_feed_forward, l1_self_attention, l1_cross_attention, l1_feed_forward]


def program(nc, A, out, stop=6, start=0):
    with ExitStack() as ctx:
        core = Core(nc, ctx, A, out)
        setup(core)
        if start < 1:
            with ExitStack() as own:
                wcol = own.enter_context(nc.sbuf_tensor("token_weights", [P, B], F32))
                l0_token_weights(core, wcol)
                l0_attention(core, wcol)
        for n, layer in enumerate(LAYERS, 2):
            if start < n <= stop:
                layer(core)
        store(core)


def store(core):
    nc = core.nc
    with ExitStack() as ctx:
        stored = semaphores(nc, ctx)("stored")
        block = ctx.enter_context(nc.Block())

        @block.sync
        def _(sp):
            sp.dma_start(core.out.rearrange("b p h -> p b h"), core.x[:, :, :]).then_inc(stored, 16)
            sp.wait_ge(stored, 16)


UNUSED = ("L1_xattn_context_lens", "L1_xattn_Wk", "L1_xattn_bk", "L1_xattn_gk", "L1_xattn_Wv", "L1_xattn_bv")
TRANSPOSED = ("L0_ffn_w_gate_up", "L0_ffn_w_down", "L1_attn_Wq", "L1_attn_Wk", "L1_attn_Wv", "L1_attn_Wo",
              "L1_ffn_gate_w", "L1_ffn_shared_w1", "L1_ffn_shared_w2")
OUT = ((B, P, H), "float32")


def kernel(**inputs):
    import numpy as _np
    import concourse.bacc as _bacc
    from concourse import mybir as _mybir
    from concourse.bass_utils import run_bass_kernel_spmd as _run

    given = {}
    for name, a in inputs.items():
        if name in UNUSED:
            continue
        if name in TRANSPOSED:
            a = _np.asarray(a).T
        elif name == "L1_ffn_w1":
            a = _np.asarray(a).transpose(2, 0, 1)
        elif name == "L1_ffn_w2":
            a = _np.asarray(a).transpose(0, 2, 1)
        given[name] = _np.ascontiguousarray(a)
    given.update(constants())
    nc = _bacc.Bacc("TRN2", target_bir_lowering=False, num_devices=1)
    arrays, A = {}, {}
    for name, a in given.items():
        arrays[f"in_{name}_dram"] = a
        A[name] = nc.dram_tensor(f"in_{name}_dram", a.shape, _mybir.dt.from_np(a.dtype), kind="ExternalInput").ap()
    out = nc.dram_tensor("out_0_dram", OUT[0], _mybir.dt.from_np(_np.dtype(OUT[1])), kind="ExternalOutput").ap()
    program(nc, A, out)
    r = _run(nc, [arrays], core_ids=[0])
    return r.results[0]["out_0_dram"]
```

```python
from contextlib import ExitStack

import numpy as np

import concourse.bass as bass
from concourse import mybir

F32 = mybir.dt.float32
BF16 = mybir.dt.bfloat16
U16 = mybir.dt.uint16
ALU = mybir.AluOpType
ACT = mybir.ActivationFunctionType
AX = mybir.AxisListType

P = 128
B = 16
H = 256
KT = H // P
BANK = 512
NEG = -1e30
LN_EPS = 1e-5
RMS_EPS = 1e-6

BIASES = [("L0_attn_bq", 2048), ("L0_attn_blk", 2048), ("L0_attn_blv", 2048), ("L0_attn_bk", 128),
          ("L0_attn_bv", 128), ("L0_attn_bo", 256), ("L0_xattn_bq", 256), ("L0_xattn_bkv", 512),
          ("L0_xattn_bp", 256), ("L1_xattn_bq", 256), ("L1_xattn_bk_img", 256), ("L1_xattn_bv_img", 256),
          ("L1_xattn_bo", 256)]
BIAS_AT = {}
for _name, _n in BIASES:
    BIAS_AT[_name] = sum(n for _, n in BIASES[:len(BIAS_AT)])
BIAS_LEN = sum(n for _, n in BIASES)


class Count:

    def __init__(self, sem, per):
        self.sem, self.per = sem, per

    def open(self, eng):
        eng.sem_inc(self.sem, self.per)

    def of(self, b, k=None):
        return self.per * b + (self.per + (self.per if k is None else k))


class Chain:

    def __init__(self, eng, sem, per, base=0):
        self.eng, self.sem, self.per, self.base, self.n = eng, sem, per, base, 0

    def start(self, b):
        self.b, self.n = b, 0

    def mark(self, ins):
        self.n += 1
        ins.then_inc(self.sem, 1)
        return self.n

    def wait(self, n=None):
        self.eng.wait_ge(self.sem, self.per * self.b + (self.base + (self.n if n is None else n)))

    def link(self, ins):
        self.mark(ins)
        self.wait()

    def settle(self):
        self.n += 1
        self.eng.sem_inc(self.sem, 1)

    def end(self):
        assert self.n == self.per, f"{self.n} links in a pass, {self.per} counted"


def pipeline(eng, order, pieces, passes):
    depth = max(lag for _, lag in order)

    def emit(i, there):
        for name, lag in order:
            if name in pieces and there(lag):
                pieces[name](i - lag)

    for i in range(depth):
        emit(i, lambda lag, i=i: lag <= i)
    with eng.Fori(depth, passes) as i:
        emit(i, lambda lag: True)
    for i in range(passes, passes + depth):
        emit(i, lambda lag, i=i: i - lag < passes)


def semaphores(nc, ctx):
    held = []

    def clear():
        nc.clear_and_free_semaphores(held)
        nc.all_engine_barrier()

    def sem(name):
        held.append(nc.alloc_semaphore(name))
        return held[-1]

    ctx.callback(clear)
    return sem


def bcast(ap, shape):
    return ap.unsqueeze(2).to_broadcast(shape)


def over_heads(ap, heads):
    return ap.unsqueeze(1).to_broadcast([ap.shape[0], heads, ap.shape[1]])


class Core:

    def __init__(self, nc, ctx, A, out):
        self.nc, self.A, self.out = nc, A, out

        def sb(name, shape, dt=F32):
            return ctx.enter_context(nc.sbuf_tensor(name, shape, dt))

        self.x = sb("x_res", [P, B, H])
        self.ident = sb("ident", [P, P])
        self.identb = sb("identb", [P, P], BF16)
        self.causal = sb("causal", [P, 4, P], BF16)
        self.bias_rows = sb("bias_rows", [3, BIAS_LEN], BF16)
        self.ones = sb("ones", [3, P], BF16)
        self.neghalf = sb("neghalf", [P, 32])

    def bias(self, name, lo=0, n=None):
        at = BIAS_AT[name] + lo
        return self.bias_rows[:, at:at + (dict(BIASES)[name] - lo if n is None else n)]


def setup(core, ahead):
    nc, A = core.nc, core.A
    rows = BIAS_LEN // P
    with ExitStack() as ctx:
        def sb(name, shape, dt=F32):
            return ctx.enter_context(nc.sbuf_tensor(name, shape, dt))

        causal_f = sb("causal_f", [P, P])
        whole = sb("bias_whole", [rows, P])
        rest = sb("bias_rest", [rows, 2, P])
        parts = sb("bias_parts", [rows, 3, P], BF16)
        sem = semaphores(nc, ctx)
        loaded, bias_in, made, spread = (sem("setup_" + n) for n in ("loaded", "bias_in", "made", "spread"))
        block = ctx.enter_context(nc.Block())

        @block.sync
        def _(sp):
            for name, n in BIASES:
                at = BIAS_AT[name] // P
                sp.dma_start(whole[at:at + n // P, :], A[name].rearrange("(a p) -> a p", p=P)).then_inc(bias_in, 16)
            sp.dma_start(core.ident[:, :], A["c_ident"]).then_inc(loaded, 16)
            sp.dma_start(causal_f[:, :], A["c_causal"]).then_inc(loaded, 16)
            sp.dma_start(core.x[:, :, :], A["x"].rearrange("b p h -> p b h")).then_inc(loaded, 16)
            ahead.load_first(sp)
            sp.wait_ge(made, 5)
            for j in range(3):
                sp.dma_start(core.bias_rows[j:j + 1, :].rearrange("o (a p) -> o a p", p=P),
                             parts[:, j, :]).then_inc(spread, 16)
            sp.wait_ge(spread, 48)
            sp.wait_ge(loaded, 48)

        @block.scalar
        def _(act):
            act.wait_ge(bias_in, 16 * len(BIASES))
            act.wait_ge(loaded, 48)
            ahead.load(act)

        @block.vector
        def _(dve):
            dve.wait_ge(bias_in, 16 * len(BIASES))
            dve.tensor_copy(parts[:, 0, :], whole[:, :]).then_inc(made, 1)
            dve.wait_ge(made, 1)
            dve.tensor_tensor(rest[:, 0, :], whole[:, :], parts[:, 0, :], ALU.subtract).then_inc(made, 1)
            dve.wait_ge(made, 2)
            dve.tensor_copy(parts[:, 1, :], rest[:, 0, :]).then_inc(made, 1)
            dve.wait_ge(made, 3)
            dve.tensor_tensor(rest[:, 1, :], rest[:, 0, :], parts[:, 1, :], ALU.subtract).then_inc(made, 1)
            dve.wait_ge(made, 4)
            dve.tensor_copy(parts[:, 2, :], rest[:, 1, :]).then_inc(made, 1)
            dve.wait_ge(loaded, 48)
            dve.tensor_copy(core.identb[:, :], core.ident[:, :])
            for j in range(4):
                dve.tensor_copy(core.causal[:, j, :], causal_f[:, :])
            dve.memset(core.ones[:, :], 1.0)
            dve.memset(core.neghalf[:, :], -0.5)


NH, D = 16, 128
RATIO, NC = 4, 32
ROPE = D // 2
G = 4
CHOSEN = 3e38


class AttentionWeights:

    def __init__(self, core, ctx):
        nc, A = core.nc, core.A
        self.A = A

        def sb(name, shape):
            return ctx.enter_context(nc.sbuf_tensor(name, shape, F32))

        self.qkv = [sb(f"a0_w{n}", [P, KT, NH * D]) for n in "qkv"]
        self.o = sb("a0_wo", [P, NH, H])
        self.c = sb("a0_wc", [P, KT, 2 * D])
        self.cmp, self.cmp_bias = sb("w0_wcmp", [P, H]), sb("w0_bcmp", [P, 1])
        sem = semaphores(nc, ctx)
        self.loaded, self.cmp_in = sem("a0_weights_in"), sem("w0_weights_in")
        self.loads = [(w[:, :, :], A[name].rearrange("(t p) n -> p t n", p=P))
                      for w, name in zip(self.qkv, ("L0_attn_Wq", "L0_attn_Wlk", "L0_attn_Wlv"))]
        self.loads += [(self.c[:, :, j * D:(j + 1) * D], A[name].rearrange("(t p) n -> p t n", p=P))
                       for j, name in enumerate(("L0_attn_Wk", "L0_attn_Wv"))]
        self.loads.append((self.o[:, :, :], A["L0_attn_Wo"].rearrange("(h p) n -> p h n", p=P)))
        self.all_in = 16 * len(self.loads)

    def load_first(self, eng):
        eng.dma_start(self.cmp[:, :], self.A["L0_attn_Wcmp"].rearrange("h o -> (h o)").partition_broadcast(P)).then_inc(self.cmp_in, 16)
        eng.dma_start(self.cmp_bias[:, :], self.A["L0_attn_bcmp"].partition_broadcast(P)).then_inc(self.cmp_in, 16)

    def load(self, eng):
        for dst, src in self.loads:
            eng.dma_start(dst, src).then_inc(self.loaded, 16)


def l0_attention(core, wcol, weights):
    nc, A = core.nc, core.A
    NG = NH // G
    w_qkv, w_o, w_c = weights.qkv, weights.o, weights.c
    with ExitStack() as ctx:
        def sb(name, shape, dt=F32):
            return ctx.enter_context(nc.sbuf_tensor(name, shape, dt))

        def ps(name, shape, dt=F32):
            return ctx.enter_context(nc.psum_tensor(name, shape, dt))

        named = semaphores(nc, ctx)

        def sem(name):
            return named("a0_" + name)

        def count(name, per):
            return Count(sem(name), per)

        cq, ck_tab, cc = (sb(n, [P, D]) for n in ("a0_cos_q", "a0_cos_k", "a0_cos_c"))
        sq_tab, sk_tab, sc_tab = (sb(n, [P, ROPE]) for n in ("a0_sin_q", "a0_sin_k", "a0_sin_c"))
        wn = sb("a0_norm_w", [P, 2, D])
        cmask_f = sb("a0_cmask_f", [P, NC])
        cmask = sb("a0_cmask", [P, NH, NC], BF16)
        member = sb("a0_member", [P, NC])

        xb = sb("a0_xb", [P, H])
        xT = sb("a0_xT", [P, KT, P])
        raw = [sb(f"a0_raw{n}", [P, NH * D]) for n in "qkv"]
        rot = [sb(f"a0_rot{n}", [P, NH * D]) for n in "qk"]
        sq = sb("a0_sq", [P, NH * D])
        half = sb("a0_half", [P, NH * ROPE])
        ssq = sb("a0_ssq", [P, 2 * NH])
        rstd = sb("a0_rstd", [P, 2 * NH])
        qT = sb("a0_qT", [P, NH, P])
        kT = sb("a0_kT", [P, NH, P])
        wsel = sb("a0_wsel", [P, NC])
        entT = sb("a0_entT", [P, KT, 4, NC])
        ckr = sb("a0_ckr", [P, D])
        cv = sb("a0_cv", [P, G, D])
        crot = sb("a0_crot", [P, D])
        chalf = sb("a0_chalf", [P, ROPE])
        csq = sb("a0_csq", [P, D])
        cst = sb("a0_cst", [P, 3])
        ckT = sb("a0_ckT", [P, P])
        scm = sb("a0_scm", [P, NH, NC])
        top = sb("a0_top", [P, NH, 8])
        repl = sb("a0_repl", [P, NH, NC])
        tmax = sb("a0_tmax", [P, NH])
        es = sb("a0_es", [P, NH, NC])
        tsum = sb("a0_tsum", [P, NH])
        psT = sb("a0_psT", [P, NG, P])
        rqs = sb("a0_rqs", [P, NH])
        lmax = sb("a0_lmax", [P, NH])
        nbias = sb("a0_nbias", [P, NH])
        lsum = sb("a0_lsum", [P, NH])
        lrec = sb("a0_lrec", [P, NH])
        prob = [sb(f"a0_prob{i}", [P, G, P]) for i in range(2)]
        pT = [sb(f"a0_pT{i}", [P, G, P]) for i in range(2)]
        cT = [sb(f"a0_cT{i}", [P, G, P]) for i in range(2)]
        y = sb("a0_y", [P, H])
        stats = sb("a0_stats", [P, 6])
        mv = sb("a0_mv", [P, 2])
        ln_r = sb("a0_ln_r", [P, 1])

        proj = [ps(f"a0_p_proj{i}", [P, BANK]) for i in range(2)]
        work = [ps(f"a0_p_work{i}", [P, BANK]) for i in range(2)]
        p_pT = ps("a0_p_pT", [P, BANK])
        p_cT = ps("a0_p_cT", [P, BANK])
        p_c = ps("a0_p_c", [P, BANK])
        p_o = ps("a0_p_o", [P, BANK])

        loaded, tables = sem("loaded"), sem("tables")
        LOADS, TABLES = 10, 11
        comp_steps, rot_steps, sparse_steps, local_steps, tail_steps = (
            sem(n) for n in ("comp_steps", "rot_steps", "sparse_steps", "local_steps", "tail_steps"))
        tile_in = count("tile_in", 1)
        PROJ = 14
        Q_AT, K_AT, C_AT, V_AT = 1, 5, 9, 10
        proj_made, proj_read = count("proj_made", PROJ), count("proj_read", PROJ)
        work_made, work_read = count("work_made", 3 * NG), count("work_read", 2 * NG)
        squared, summed, rotated = count("squared", 2), count("summed", 2), count("rotated", 2)
        root_h, k_normed, rqs_up = count("root_heads", 2), count("k_normed", 1), count("rqs_up", 1)
        wsel_up, c_sum, root_c, crot_up = (count(n, 1) for n in ("wsel_up", "c_sum", "root_c", "crot_up"))
        c_made = count("c_made", 4)
        c_read = count("c_read", 3)
        s_arg, s_exp, s_prob = (count("sparse_" + n, 1) for n in ("arg", "exp", "prob"))
        bias_up, l_exp, l_prob = (count(n, NG) for n in ("bias_up", "local_exp", "local_prob"))
        pT_made, pT_read = count("pT_made", NG), count("pT_read", NG)
        cT_made, cT_read = count("cT_made", NG), count("cT_read", NG)
        o_made, o_read = count("o_made", 1), count("o_read", 1)
        var_up, root_l, x_up = count("var_up", 1), count("root_l", 1), count("x_up", 1)

        def before(c, b, k, n):
            return c.of(b, k - n) if k > n else c.of(b - 1, c.per + k - n)

        order = [("turn_q", 1), ("sparse", 1), ("turn_k", 1), ("in", 0), ("s0", 1), ("s1", 1), ("norm1", 2),
                 ("q", 0), ("sparse_exp", 1), ("sparse_prob", 1), ("rot_q", 0), ("norm2", 2), ("e0", 1), ("k", 0),
                 ("e1", 1), ("turn_sparse", 1), ("m0", 1), ("sum_q", 0), ("top2", 1), ("entries", 0), ("m1", 1),
                 ("even2", 1), ("top3", 1), ("rot_k", 0), ("m2", 1), ("m3", 1), ("sum_k", 0), ("out", 1),
                 ("k_norm", 0), ("comp_kv", 0), ("v", 0), ("comp_key", 0)]

        block = ctx.enter_context(nc.Block())

        @block.sync
        def _(sp):
            for j, name in enumerate(("L0_attn_qn_w", "L0_attn_kn_w")):
                sp.dma_start(wn[:, j, :], A[name].partition_broadcast(P)).then_inc(loaded, 16)
            for t, name in ((cq, "c_cos"), (ck_tab, "c_cos"), (cc, "c_cos_c"), (sq_tab, "c_sin"),
                            (sk_tab, "c_sin"), (sc_tab, "c_sin_c"), (cmask_f, "c_cmask"), (member, "c_member")):
                sp.dma_start(t[:, :], A[name]).then_inc(loaded, 16)
            sp.wait_ge(loaded, 16 * LOADS)
            sp.wait_ge(weights.loaded, weights.all_in)

        @block.gpsimd
        def _(pool):
            for c in (tile_in, squared, root_h, k_normed, root_c, root_l):
                c.open(pool)

            def tile_copy(b):
                pool.wait_ge(proj_made.sem, proj_made.of(b - 1, 1))
                pool.wait_ge(c_made.sem, c_made.of(b - 1, 1))
                pool.tensor_copy(xb[:, :], core.x[:, bass.ds(b, 1), :].rearrange("p o h -> p (o h)")).then_inc(tile_in.sem, 1)

            def square(j):
                def run(b):
                    pool.wait_ge(proj_read.sem, proj_read.of(b, (Q_AT, K_AT)[j] + 4))
                    pool.wait_ge(summed.sem, before(summed, b, j + 1, 1))
                    pool.tensor_tensor(sq[:, :], raw[j][:, :], raw[j][:, :], ALU.mult).then_inc(squared.sem, 1)
                return run

            def root_queries(b):
                pool.wait_ge(summed.sem, summed.of(b, 1))
                pool.wait_ge(rqs_up.sem, rqs_up.of(b - 1))
                pool.tensor_tensor(rstd[:, 0:NH], ssq[:, 0:NH], core.neghalf[:, 0:NH], ALU.pow).then_inc(root_h.sem, 1)

            def norm_keys(b):
                pool.wait_ge(summed.sem, summed.of(b, 2))
                pool.wait_ge(k_normed.sem, k_normed.of(b - 1))
                pool.tensor_tensor(rstd[:, NH:], ssq[:, NH:], core.neghalf[:, 0:NH], ALU.pow).then_inc(root_h.sem, 1)
                pool.wait_ge(root_h.sem, root_h.of(b, 2))
                pool.wait_ge(rotated.sem, rotated.of(b, 2))
                kr = rot[1][:, :].rearrange("p (h d) -> p h d", h=NH)
                pool.tensor_tensor(kr, kr, bcast(rstd[:, NH:], [P, NH, D]), ALU.mult).then_inc(k_normed.sem, 1)

            def root_compressed(b):
                pool.wait_ge(c_sum.sem, c_sum.of(b))
                pool.wait_ge(crot_up.sem, crot_up.of(b - 1))
                pool.tensor_tensor(cst[:, 2:3], cst[:, 1:2], core.neghalf[:, 0:1], ALU.pow).then_inc(root_c.sem, 1)

            def root_layer(b):
                pool.wait_ge(var_up.sem, var_up.of(b))
                pool.wait_ge(x_up.sem, x_up.of(b - 1))
                pool.tensor_tensor(ln_r[:, :], mv[:, 1:2], core.neghalf[:, 0:1], ALU.pow).then_inc(root_l.sem, 1)

            pipeline(pool, order, {"in": tile_copy, "q": square(0), "k": square(1), "norm1": root_layer,
                                   "sum_q": root_queries, "k_norm": norm_keys, "comp_kv": root_compressed}, B)

        @block.tensor
        def _(pe):
            for c in (work_made, proj_made, c_made, pT_made, cT_made, o_made):
                c.open(pe)
            pe.wait_ge(weights.loaded, weights.all_in)
            pe.wait_ge(tables, TABLES)

            def turn_in(b):
                pe.wait_ge(tile_in.sem, tile_in.of(b))
                pe.wait_ge(proj_read.sem, before(proj_read, b, 1, 2))
                for t in range(KT):
                    mm = pe.transpose(proj[0][:, t * P:(t + 1) * P], xb[:, t * P:(t + 1) * P], core.ident[:, :])
                mm.then_inc(proj_made.sem, 1)

            def entries(b):
                pe.wait_ge(wsel_up.sem, wsel_up.of(b))
                pe.wait_ge(c_read.sem, c_read.of(b - 1))
                for t in range(KT):
                    mm = pe.matmul(p_c[:, t * NC:(t + 1) * NC], xb[:, t * P:(t + 1) * P], wsel[:, :],
                                   start=True, stop=True)
                mm.then_inc(c_made.sem, 1)

            def project(i, at):
                def run(b):
                    if i == 0:
                        pe.wait_ge(proj_read.sem, proj_read.of(b, 1))
                    name = ("L0_attn_bq", "L0_attn_blk", "L0_attn_blv")[i]
                    for c in range(NG):
                        n = at + c
                        bank = proj[n % 2]
                        pe.wait_ge(proj_read.sem, before(proj_read, b, n + 1, 2))
                        pe.matmul(bank[:, :], core.ones[:, :], core.bias(name, c * BANK, BANK), start=True, stop=False)
                        for t in range(KT):
                            mm = pe.matmul(bank[:, :], xT[:, t, :], w_qkv[i][:, t, c * BANK:(c + 1) * BANK],
                                           start=False, stop=(t == KT - 1))
                        mm.then_inc(proj_made.sem, 1)
                return run

            def compressed_kv(b):
                bank = proj[C_AT % 2]
                pe.wait_ge(c_read.sem, c_read.of(b, 1))
                pe.wait_ge(proj_read.sem, before(proj_read, b, C_AT + 1, 2))
                pe.matmul(bank[:, 0:2 * D], core.ones[:, :],
                          core.bias_rows[:, BIAS_AT["L0_attn_bk"]:BIAS_AT["L0_attn_bk"] + 2 * D], start=True, stop=False)
                for t in range(KT):
                    mm = pe.matmul(bank[:, 0:2 * D], entT[:, t, :, :].rearrange("p a c -> p (a c)"), w_c[:, t, :],
                                   start=False, stop=(t == KT - 1))
                mm.then_inc(proj_made.sem, 1)

            def compressed_key(b):
                pe.wait_ge(crot_up.sem, crot_up.of(b))
                pe.transpose(p_c[:, 0:P], crot[:, :], core.ident[:, :]).then_inc(c_made.sem, 1)

            def turn_heads(j):
                def run(b):
                    if j == 0:
                        pe.wait_ge(rotated.sem, rotated.of(b, 1))
                        pe.wait_ge(l_exp.sem, l_exp.of(b - 1))
                    else:
                        pe.wait_ge(k_normed.sem, k_normed.of(b))
                    for g in range(NG):
                        n = j * NG + g
                        if n >= 2:
                            pe.wait_ge(work_read.sem, work_read.of(b, n - 1))
                        for h in range(G):
                            at = (g * G + h) * D
                            mm = pe.transpose(work[n % 2][:, h * P:(h + 1) * P], rot[j][:, at:at + D], core.ident[:, :])
                        mm.then_inc(work_made.sem, 1)
                return run

            def sparse_scores(b):
                pe.wait_ge(work_read.sem, work_read.of(b, NG))
                pe.wait_ge(c_read.sem, c_read.of(b, 2))
                pe.matmul(p_c[:, :], core.identb[:, :], cmask[:, :, :].rearrange("p h c -> p (h c)"),
                          start=True, stop=False)
                for h in range(NH):
                    mm = pe.matmul(p_c[:, h * NC:(h + 1) * NC], qT[:, h, :], ckT[:, 0:NC],
                                   start=False, stop=(h == NH - 1))
                mm.then_inc(c_made.sem, 1)

            def scores(g):
                def run(b):
                    if g == 0:
                        pe.wait_ge(work_read.sem, work_read.of(b))
                    if g >= 2:
                        pe.wait_ge(l_exp.sem, l_exp.of(b, g - 1))
                    bank = work[g % 2]
                    pe.matmul(bank[:, :], core.identb[:, :], core.causal[:, :, :].rearrange("p g k -> p (g k)"),
                              start=True, stop=False)
                    for h in range(G):
                        mm = pe.matmul(bank[:, h * P:(h + 1) * P], qT[:, g * G + h, :], kT[:, g * G + h, :],
                                       start=False, stop=(h == G - 1))
                    mm.then_inc(work_made.sem, 1)
                return run

            def turn_sparse(b):
                pe.wait_ge(s_prob.sem, s_prob.of(b))
                for g in range(NG):
                    mm = pe.transpose(p_c[:, g * P:(g + 1) * P],
                                      es[:, g * G:(g + 1) * G, :].rearrange("p h c -> p (h c)"), core.ident[:, :])
                mm.then_inc(c_made.sem, 1)

            def output(b, g):
                pe.wait_ge(cT_read.sem, cT_read.of(b, g + 1))
                if g == 0:
                    pe.wait_ge(o_read.sem, o_read.of(b - 1))
                    pe.matmul(p_o[:, 0:H], core.ones[:, :], core.bias("L0_attn_bo"), start=True, stop=False)
                for h in range(G):
                    mm = pe.matmul(p_o[:, 0:H], cT[g % 2][:, h, :], w_o[:, g * G + h, :],
                                   start=False, stop=(g == NG - 1 and h == G - 1))
                if g == NG - 1:
                    mm.then_inc(o_made.sem, 1)

            def group(g):
                def run(b):
                    pe.wait_ge(l_prob.sem, l_prob.of(b, g + 1))
                    pe.wait_ge(pT_read.sem, pT_read.of(b, g))
                    for h in range(G):
                        mm = pe.transpose(p_pT[:, h * P:(h + 1) * P], prob[g % 2][:, h, :], core.ident[:, :])
                    mm.then_inc(pT_made.sem, 1)
                    if g + 2 < NG:
                        scores(g + 2)(b)
                    if g >= 1:
                        output(b, g - 1)
                    pe.wait_ge(pT_read.sem, pT_read.of(b, g + 1))
                    pe.wait_ge(cT_read.sem, cT_read.of(b, g))
                    if g == 0:
                        pe.wait_ge(proj_read.sem, proj_read.of(b))
                        pe.wait_ge(c_read.sem, c_read.of(b))
                    for h in range(G):
                        o = p_cT[:, h * P:(h + 1) * P]
                        at = (g * G + h) * D
                        pe.matmul(o, raw[2][:, at:at + D], pT[g % 2][:, h, :], start=(h == 0), stop=False)
                        mm = pe.matmul(o, cv[:, h, :], psT[:, g, :], start=False, stop=(h == G - 1))
                    mm.then_inc(cT_made.sem, 1)
                return run

            def last_output(b):
                output(b, NG - 1)

            pieces = {"turn_q": turn_heads(0), "sparse": sparse_scores, "turn_k": turn_heads(1), "in": turn_in,
                      "s0": scores(0), "s1": scores(1), "q": project(0, Q_AT), "k": project(1, K_AT),
                      "turn_sparse": turn_sparse, "entries": entries, "out": last_output,
                      "comp_kv": compressed_kv, "v": project(2, V_AT), "comp_key": compressed_key}
            pieces.update({f"m{g}": group(g) for g in range(NG)})
            pipeline(pe, order, pieces, B)

        @block.scalar
        def _(act):
            for c in (work_read, proj_read, c_read, s_exp, l_exp, pT_read, cT_read):
                c.open(act)
            act.wait_ge(tables, TABLES)

            def inputs_up(b):
                act.wait_ge(proj_made.sem, proj_made.of(b, 1))
                act.copy(xT[:, :, :].rearrange("p t n -> p (t n)"), proj[0][:, 0:KT * P]).then_inc(proj_read.sem, 1)

            def entries_up(b):
                act.wait_ge(c_made.sem, c_made.of(b, 1))
                act.wait_ge(proj_made.sem, proj_made.of(b - 1))
                for j in range(4):
                    i = act.copy(entT[:, :, j, :], p_c[:, 0:KT * NC].rearrange("p (t c) -> p t c", t=KT))
                i.then_inc(c_read.sem, 1)

            def projected(i, at):
                def run(b):
                    if i < 2:
                        act.wait_ge(rotated.sem, rotated.of(b - 1, i + 1))
                        act.wait_ge(squared.sem, squared.of(b - 1, i + 1))
                    else:
                        act.wait_ge(cT_made.sem, cT_made.of(b - 1))
                    for c in range(NG):
                        act.wait_ge(proj_made.sem, proj_made.of(b, at + c + 1))
                        act.copy(raw[i][:, c * BANK:(c + 1) * BANK], proj[(at + c) % 2][:, :]).then_inc(proj_read.sem, 1)
                return run

            def compressed_up(b):
                act.wait_ge(proj_made.sem, proj_made.of(b, C_AT + 1))
                act.wait_ge(cT_made.sem, cT_made.of(b - 1))
                act.wait_ge(crot_up.sem, crot_up.of(b - 1))
                bank = proj[C_AT % 2]
                act.copy(ckr[:, :], bank[:, 0:D])
                for h in range(G):
                    q = slice(NC * h, NC * (h + 1))
                    last = act.copy(cv[q, h, :], bank[q, D:2 * D])
                last.then_inc(proj_read.sem, 1)

            def compressed_key_up(b):
                act.wait_ge(c_made.sem, c_made.of(b, 2))
                act.copy(ckT[:, :], p_c[:, 0:P]).then_inc(c_read.sem, 1)

            def heads_up(j):
                def run(b):
                    for g in range(NG):
                        n = j * NG + g
                        act.wait_ge(work_made.sem, work_made.of(b, n + 1))
                        dst = (qT, kT)[j][:, g * G:(g + 1) * G, :]
                        act.copy(dst.rearrange("p h t -> p (h t)"), work[n % 2][:, :]).then_inc(work_read.sem, 1)
                return run

            def sparse_exp(b):
                act.wait_ge(s_arg.sem, s_arg.of(b))
                act.wait_ge(c_made.sem, c_made.of(b - 1))
                act.activation(es[:, :, :], scm[:, :, :], ACT.Exp).then_inc(s_exp.sem, 1)

            def exps(g):
                def run(b):
                    act.wait_ge(bias_up.sem, bias_up.of(b, g + 1))
                    act.wait_ge(l_prob.sem, l_prob.of(b, g - 1) if g >= 2 else l_prob.of(b - 1, NG - 1 + g))
                    act.wait_ge(pT_made.sem, pT_made.of(b, g - 1) if g >= 2 else pT_made.of(b - 1, NG - 1 + g))
                    for h in range(G):
                        n = g * G + h
                        i = act.activation(prob[g % 2][:, h, :], work[g % 2][:, h * P:(h + 1) * P], ACT.Exp,
                                           bias=nbias[:, n:n + 1], scale=rqs[:, n:n + 1],
                                           accum_out=lsum[:, n:n + 1])
                    i.then_inc(l_exp.sem, 1)
                return run

            def sparse_up(b):
                act.wait_ge(c_made.sem, c_made.of(b, 4))
                act.wait_ge(cT_made.sem, cT_made.of(b - 1))
                act.copy(psT[:, :, :].rearrange("p g t -> p (g t)"), p_c[:, :]).then_inc(c_read.sem, 1)

            def group(g):
                def run(b):
                    act.wait_ge(pT_made.sem, pT_made.of(b, g + 1))
                    act.wait_ge(cT_made.sem, cT_made.of(b, g - 1) if g >= 2 else cT_made.of(b - 1, NG - 1 + g))
                    act.copy(pT[g % 2][:, :, :].rearrange("p g t -> p (g t)"), p_pT[:, :]).then_inc(pT_read.sem, 1)
                    if g + 2 < NG:
                        exps(g + 2)(b)
                    act.wait_ge(cT_made.sem, cT_made.of(b, g + 1))
                    if g == 0:
                        act.wait_ge(o_made.sem, o_made.of(b - 1))
                    act.copy(cT[g % 2][:, :, :].rearrange("p g t -> p (g t)"), p_cT[:, :]).then_inc(cT_read.sem, 1)
                return run

            pieces = {"turn_q": heads_up(0), "turn_k": heads_up(1), "in": inputs_up, "q": projected(0, Q_AT),
                      "k": projected(1, K_AT), "sparse_exp": sparse_exp, "e0": exps(0), "e1": exps(1),
                      "turn_sparse": sparse_up, "entries": entries_up, "comp_kv": compressed_up,
                      "v": projected(2, V_AT), "comp_key": compressed_key_up}
            pieces.update({f"m{g}": group(g) for g in range(NG)})
            pipeline(act, order, pieces, B)

        @block.vector
        def _(dve):
            for c in (rotated, summed, wsel_up, c_sum, crot_up, rqs_up, s_arg, s_prob, bias_up, l_prob, o_read,
                      var_up, x_up):
                c.open(dve)
            dve.wait_ge(loaded, 16 * LOADS)
            for j, (cos, sin) in enumerate(((cq, sq_tab), (ck_tab, sk_tab), (cc, sc_tab))):
                w = wn[:, min(j, 1), :]
                dve.tensor_tensor(cos[:, :], cos[:, :], w, ALU.mult).then_inc(tables, 1)
                for lo, hi in ((0, ROPE // 2), (ROPE // 2, 0)):
                    dve.tensor_tensor(sin[:, lo:lo + ROPE // 2], sin[:, lo:lo + ROPE // 2],
                                      w[:, hi:hi + ROPE // 2], ALU.mult).then_inc(tables, 1)
            dve.memset(cv[:, :, :], 0.0).then_inc(tables, 1)
            dve.tensor_copy(cmask[:, :, :], over_heads(cmask_f[:, :], NH)).then_inc(tables, 1)
            dve.wait_ge(tables, TABLES)
            comp, turned, sparse, local, tail = (
                Chain(dve, s, n) for s, n in ((comp_steps, 5), (rot_steps, 8), (sparse_steps, 41),
                                              (local_steps, 2 * NG), (tail_steps, 3)))

            def rotate(ch, dst, hbuf, src, cos, sin, heads):
                d3 = dst.rearrange("p (h d) -> p h d", h=heads)
                s3 = src.rearrange("p (h d) -> p h d", h=heads)
                h3 = hbuf.rearrange("p (h d) -> p h d", h=heads)
                ch.mark(dve.tensor_tensor(d3, s3, over_heads(cos[:, :], heads), ALU.mult))
                for lo, hi in ((0, ROPE // 2), (ROPE // 2, 0)):
                    ch.mark(dve.tensor_tensor(h3[:, :, lo:lo + ROPE // 2], s3[:, :, hi:hi + ROPE // 2],
                                              over_heads(sin[:, lo:lo + ROPE // 2], heads), ALU.mult))
                ch.wait()
                return dve.tensor_tensor(d3[:, :, 0:ROPE], d3[:, :, 0:ROPE], h3, ALU.add)

            def token_weights(b):
                dve.wait_ge(c_made.sem, c_made.of(b - 1, 1))
                dve.tensor_scalar(wsel[:, :], member[:, :], wcol[:, bass.ds(b, 1)], None, ALU.mult).then_inc(wsel_up.sem, 1)

            def compressed_keys(b):
                comp.start(b)
                dve.wait_ge(proj_read.sem, proj_read.of(b, C_AT + 1))
                dve.wait_ge(c_made.sem, c_made.of(b - 1, 2))
                dve.wait_ge(root_c.sem, root_c.of(b - 1))
                comp.link(dve.tensor_tensor_reduce(out=csq[:, :], in0=ckr[:, :], in1=ckr[:, :], scale=1.0, scalar=0.0,
                                                   op0=ALU.mult, op1=ALU.add, accum_out=cst[:, 0:1]))
                dve.tensor_scalar(cst[:, 1:2], cst[:, 0:1], 1.0 / D, RMS_EPS, ALU.mult, ALU.add).then_inc(c_sum.sem, 1)
                comp.link(rotate(comp, crot[:, :], chalf[:, :], ckr[:, :], cc, sc_tab, 1))
                dve.wait_ge(root_c.sem, root_c.of(b))
                dve.tensor_scalar(crot[:, :], crot[:, :], cst[:, 2:3], None, ALU.mult).then_inc(crot_up.sem, 1)
                dve.wait_ge(crot_up.sem, crot_up.of(b))
                comp.end()

            def turn(j):
                cos, sin = ((cq, sq_tab), (ck_tab, sk_tab))[j]

                def run(b):
                    turned.b, turned.n = b, 4 * j
                    dve.wait_ge(work_made.sem, work_made.of(b - 1, NG * (j + 1)))
                    dve.wait_ge(proj_read.sem, proj_read.of(b, (Q_AT, K_AT)[j] + 4))
                    dve.wait_ge(rotated.sem, before(rotated, b, j + 1, 1))
                    rotate(turned, rot[j][:, :], half[:, :], raw[j][:, :], cos, sin, NH).then_inc(rotated.sem, 1)
                return run

            def sums(j):
                def run(b):
                    turned.b, turned.n = b, 4 * j + 3
                    dve.wait_ge(squared.sem, squared.of(b, j + 1))
                    dve.wait_ge(root_h.sem, root_h.of(b - 1, j + 1))
                    hs = ssq[:, j * NH:(j + 1) * NH]
                    turned.link(dve.tensor_reduce(hs, sq[:, :].rearrange("p (h d) -> p h d", h=NH), AX.X, ALU.add))
                    dve.tensor_scalar(hs, hs, 1.0 / D, RMS_EPS, ALU.mult, ALU.add).then_inc(summed.sem, 1)
                return run

            def largest(b):
                sparse.start(b)
                dve.wait_ge(root_h.sem, root_h.of(b, 1))
                dve.wait_ge(l_exp.sem, l_exp.of(b - 1))
                dve.tensor_scalar(rqs[:, :], rstd[:, 0:NH], float(D) ** -0.5, None, ALU.mult).then_inc(rqs_up.sem, 1)
                dve.wait_ge(c_made.sem, c_made.of(b, 3))
                dve.wait_ge(s_exp.sem, s_exp.of(b - 1))
                sparse.link(dve.tensor_copy(scm[:, :, :].rearrange("p h c -> p (h c)"), p_c[:, :]))
                sparse.settle()
                for h in range(NH):
                    sparse.mark(dve.max(top[:, h, :], scm[:, h, :]))
                sparse.wait()
                sparse.settle()
                for h in range(NH):
                    sparse.mark(dve.match_replace(repl[:, h, :], top[:, h, :], scm[:, h, :], CHOSEN))
                sparse.link(dve.tensor_scalar(tmax[:, :], top[:, :, 0], NEG / 2, None, ALU.max))
                sparse.link(dve.tensor_tensor(scm[:, :, :], scm[:, :, :], bcast(tmax[:, :], [P, NH, NC]), ALU.subtract))
                dve.wait_ge(rqs_up.sem, rqs_up.of(b))
                dve.tensor_tensor(scm[:, :, :], scm[:, :, :], bcast(rqs[:, :], [P, NH, NC]), ALU.mult).then_inc(s_arg.sem, 1)

            def sparse_prob(b):
                dve.wait_ge(s_exp.sem, s_exp.of(b))
                sparse.link(dve.scalar_tensor_tensor(out=es[:, :, :].rearrange("p h c -> p (h c)"),
                                                     in0=repl[:, :, :].rearrange("p h c -> p (h c)"), scalar=CHOSEN,
                                                     in1=es[:, :, :].rearrange("p h c -> p (h c)"),
                                                     op0=ALU.is_ge, op1=ALU.mult))
                sparse.link(dve.tensor_reduce(tsum[:, :], es[:, :, :], AX.X, ALU.add))
                sparse.link(dve.tensor_scalar(tsum[:, :], tsum[:, :], 1e-9, None, ALU.max))
                sparse.link(dve.reciprocal(tmax[:, :], tsum[:, :]))
                dve.scalar_tensor_tensor(out=es[:, :, :], in0=es[:, :, :], scalar=0.5,
                                         in1=bcast(tmax[:, :], [P, NH, NC]), op0=ALU.mult,
                                         op1=ALU.mult).then_inc(s_prob.sem, 1)
                sparse.end()

            def row_max(g):
                def run(b):
                    local.b, local.n = b, (0, 1, 3, 6)[g]
                    dve.wait_ge(work_made.sem, work_made.of(b, 2 * NG + g + 1))
                    hs = slice(g * G, (g + 1) * G)
                    local.link(dve.tensor_reduce(lmax[:, hs], work[g % 2][:, :].rearrange("p (h k) -> p h k", h=G),
                                                 AX.X, ALU.max))
                    dve.scalar_tensor_tensor(out=nbias[:, hs], in0=lmax[:, hs], scalar=-1.0, in1=rqs[:, hs],
                                             op0=ALU.mult, op1=ALU.mult).then_inc(bias_up.sem, 1)
                return run

            def group(g):
                def run(b):
                    local.b, local.n = b, (2, 4, 5, 7)[g]
                    hs = slice(g * G, (g + 1) * G)
                    dve.wait_ge(l_exp.sem, l_exp.of(b, g + 1))
                    local.link(dve.reciprocal(lrec[:, hs], lsum[:, hs]))
                    dve.scalar_tensor_tensor(out=prob[g % 2][:, :, :], in0=prob[g % 2][:, :, :], scalar=0.5,
                                             in1=bcast(lrec[:, hs], [P, G, P]), op0=ALU.mult,
                                             op1=ALU.mult).then_inc(l_prob.sem, 1)
                return run

            def statistics(b):
                tail.start(b)
                xt = core.x[:, bass.ds(b, 1), :].rearrange("p o h -> p (o h)")
                dve.wait_ge(o_made.sem, o_made.of(b))
                dve.tensor_tensor(y[:, :], p_o[:, 0:H], xt, ALU.add).then_inc(o_read.sem, 1)
                dve.wait_ge(o_read.sem, o_read.of(b))
                tail.link(dve.bn_stats(stats[:, :], y[:, :]))
                tail.settle()
                tail.link(dve.bn_aggr(mv[:, :], stats[:, :]))
                dve.tensor_scalar(mv[:, 1:2], mv[:, 1:2], LN_EPS, None, ALU.add).then_inc(var_up.sem, 1)
                tail.end()

            def layer_norm(b):
                xt = core.x[:, bass.ds(b, 1), :].rearrange("p o h -> p (o h)")
                dve.wait_ge(root_l.sem, root_l.of(b))
                dve.tensor_scalar(xt, y[:, :], mv[:, 0:1], ln_r[:, 0:1], ALU.subtract, ALU.mult).then_inc(x_up.sem, 1)

            pieces = {"sparse": largest, "s0": row_max(0), "s1": row_max(1), "norm1": statistics, "rot_q": turn(0),
                      "sum_q": sums(0), "norm2": layer_norm, "sparse_prob": sparse_prob, "in": token_weights,
                      "top2": row_max(2), "top3": row_max(3), "m0": group(0), "m1": group(1), "even2": group(2),
                      "m3": group(3), "rot_k": turn(1), "sum_k": sums(1), "comp_kv": compressed_keys}
            pipeline(dve, order, pieces, B)


def l0_token_weights(core, wcol, weights):
    nc, A = core.nc, core.A
    with ExitStack() as ctx:
        def sb(name, shape, dt=F32):
            return ctx.enter_context(nc.sbuf_tensor(name, shape, dt))

        prod = sb("w0_prod", [P, B, H])
        logit = sb("w0_logit", [P, B])
        shifted = sb("w0_shifted", [B, P])
        grown = sb("w0_grown", [B, P])
        stat = sb("w0_stat", [B, 3, NC])
        turned = ctx.enter_context(nc.psum_tensor("w0_turned", [B, P], F32))
        back = ctx.enter_context(nc.psum_tensor("w0_back", [P, B], F32))
        sem = semaphores(nc, ctx)
        steps, turns, exped = (sem("w0_" + n) for n in ("steps", "turns", "exped"))
        block = ctx.enter_context(nc.Block())

        @block.vector
        def _(dve):
            ch = Chain(dve, steps, 9)
            ch.start(0)
            dve.wait_ge(weights.cmp_in, 32)
            ch.link(dve.tensor_tensor(prod[:, :, :], core.x[:, :, :], over_heads(weights.cmp[:, :], B), ALU.mult))
            ch.link(dve.tensor_reduce(logit[:, :], prod[:, :, :], AX.X, ALU.add))
            ch.link(dve.tensor_scalar(logit[:, :], logit[:, :], weights.cmp_bias[:, 0:1], None, ALU.add))
            dve.wait_ge(turns, 1)
            logits = turned[:, :].rearrange("b (c r) -> b c r", r=RATIO)
            ch.link(dve.tensor_reduce(stat[:, 0, :], logits, AX.X, ALU.max))
            ch.link(dve.tensor_tensor(shifted[:, :].rearrange("b (c r) -> b c r", r=RATIO), logits,
                                      bcast(stat[:, 0, :], [B, NC, RATIO]), ALU.subtract))
            dve.wait_ge(exped, 1)
            g3 = grown[:, :].rearrange("b (c r) -> b c r", r=RATIO)
            ch.link(dve.tensor_reduce(stat[:, 1, :], g3, AX.X, ALU.add))
            ch.link(dve.reciprocal(stat[:, 2, :], stat[:, 1, :]))
            ch.link(dve.tensor_tensor(g3, g3, bcast(stat[:, 2, :], [B, NC, RATIO]), ALU.mult))
            dve.wait_ge(turns, 2)
            ch.link(dve.tensor_copy(wcol[:, :], back[:, :]))
            ch.end()

        @block.scalar
        def _(act):
            act.wait_ge(steps, 5)
            act.activation(grown[:, :], shifted[:, :], ACT.Exp).then_inc(exped, 1)

        @block.tensor
        def _(pe):
            pe.wait_ge(steps, 3)
            pe.transpose(turned[:, :], logit[:, :], core.ident[:, :]).then_inc(turns, 1)
            pe.wait_ge(steps, 8)
            pe.transpose(back[:, :], grown[:, :], core.ident[0:B, 0:B]).then_inc(turns, 1)


XH, XD = 16, 16
PAIRS = XH // 2
ROUND = 1.5 * 2.0 ** 23
QMAX = 127.0
AMAX = 255.0
FLOOR = 1e-8


def norm_statistics(dve, ch, core, b, y, stats, mv, ln_r, made, p_y, read, var_up, rooted, x_up):
    ch.start(b)
    xt = core.x[:, bass.ds(b, 1), :].rearrange("p o h -> p (o h)")
    dve.wait_ge(made.sem, made.of(b))
    dve.wait_ge(x_up.sem, x_up.of(b - 1))
    dve.tensor_tensor(y[:, :], p_y, xt, ALU.add).then_inc(read.sem, 1)
    dve.wait_ge(read.sem, read.of(b))
    ch.link(dve.bn_stats(stats[:, :], y[:, :]))
    ch.settle()
    ch.link(dve.bn_aggr(mv[:, :], stats[:, :]))
    dve.tensor_scalar(mv[:, 1:2], mv[:, 1:2], LN_EPS, None, ALU.add).then_inc(var_up.sem, 1)
    ch.end()


def norm_apply(dve, ch, core, b, y, stats, mv, ln_r, made, p_y, read, var_up, rooted, x_up):
    xt = core.x[:, bass.ds(b, 1), :].rearrange("p o h -> p (o h)")
    dve.wait_ge(rooted.sem, rooted.of(b))
    dve.tensor_scalar(xt, y[:, :], mv[:, 0:1], ln_r[:, 0:1], ALU.subtract, ALU.mult).then_inc(x_up.sem, 1)


def l0_cross_attention(core, ahead):
    nc = core.nc
    with ExitStack() as ctx:
        def sb(name, shape, dt=F32):
            return ctx.enter_context(nc.sbuf_tensor("x0_" + name, shape, dt))

        qz = sb("qz", [P, 2, PAIRS, B, P], BF16)
        kT = sb("kT", [P, PAIRS, B * P], BF16)
        vi = sb("vi", [P, B, H], BF16)
        sv = sb("sv", [P, H])
        sq = sb("sq", [P, 2, PAIRS, B])
        att = sb("att", [P, B * H])
        esum = sb("esum", [P, PAIRS, B, 2, 3])
        x0_operands(core, qz, kT, vi, sv, sq, att[:, :].rearrange("p (b h) -> p b h", b=B))
        x0_attend(core, qz, kT, vi, sq, att, esum)
        x0_output(core, sv, att, esum, ahead)


def x0_operands(core, qz, kT, vi, sv, sq, vraw):
    nc, A = core.nc, core.A
    with ExitStack() as ctx:
        def sb(name, shape, dt=F32):
            return ctx.enter_context(nc.sbuf_tensor("x1_" + name, shape, dt))

        def ps(name, shape, dt=F32):
            return ctx.enter_context(nc.psum_tensor("x1_" + name, shape, dt))

        named = semaphores(nc, ctx)

        def sem(name):
            return named("x1_" + name)

        def count(name, per):
            return Count(sem(name), per)

        wq = sb("wq", [P, KT, H])
        wkv = sb("wkv", [P, KT, 2 * H])
        xb, cb = sb("xb", [P, H]), sb("cb", [P, H])
        inT = sb("inT", [P, 2 * KT, P])
        kq, kqn = sb("kq", [P, 2, H]), sb("kqn", [P, 2, H])
        amax, scl, rec = (sb(n, [P, 2 * XH]) for n in ("amax", "scl", "rec"))
        kval = sb("kval", [P, H])
        krep = sb("krep", [P, XH, 4, XD], BF16)
        qrep = sb("qrep", [P, XH, 4, XD], BF16)
        cmax = sb("cmax", [P, H])
        vstat = sb("vstat", [P, 2, KT])
        svcol = sb("svcol", [P, KT, P])
        rsv = sb("rsv", [P, H])
        p_in, p_kv, p_q = (ps(n, [P, BANK]) for n in ("p_in", "p_kv", "p_q"))
        p_kT, p_qT = (ps(n, [P, 2 * BANK], BF16) for n in ("p_kT", "p_qT"))
        p_v = ps("p_v", [P, BANK])

        loaded, zeroed = sem("loaded"), sem("zeroed")
        ctx_in = count("ctx_in", 16)
        tile_in = count("tile_in", 1)
        turned, in_up = count("turned", 1), count("in_up", 1)
        made = count("made", 2)
        kv_read, q_read = count("kv_read", 1), count("q_read", 1)
        reps, kq_used = count("reps", 1), count("kq_used", 1)
        rep_made, rep_read = count("rep_made", 1), count("rep_read", 2)
        steps = sem("steps")
        v_steps, v_turn = sem("v_steps"), sem("v_turn")
        DVE_STEPS = 11
        order = [("project", 1), ("in", 0), ("reps", 2)]
        block = ctx.enter_context(nc.Block())

        @block.sync
        def _(sp):
            ctx_in.open(sp)
            sp.dma_start(wq[:, :, :], A["L0_xattn_Wq"].rearrange("(t p) n -> p t n", p=P)).then_inc(loaded, 16)
            sp.dma_start(wkv[:, :, :], A["L0_xattn_Wkv"].rearrange("(t p) n -> p t n", p=P)).then_inc(loaded, 16)
            with sp.Fori(0, B) as b:
                sp.wait_ge(turned.sem, turned.of(b - 1))
                sp.dma_start(cb[:, :], A["ctx_2048"][bass.ds(b, 1), :, :].rearrange("o p h -> (o p) h")).then_inc(ctx_in.sem, 16)
            sp.wait_ge(ctx_in.sem, ctx_in.of(B - 1))
            sp.wait_ge(loaded, 32)

        @block.gpsimd
        def _(pool):
            tile_in.open(pool)
            pool.memset(qz[XD * 4:P, 0, :, :, :].rearrange("p a b t -> p (a b t)"), 0.0).then_inc(zeroed, 1)
            pool.wait_ge(zeroed, 1)
            pool.memset(qz[0:XD * 4, 1, :, :, :].rearrange("p a b t -> p (a b t)"), 0.0).then_inc(zeroed, 1)
            pool.wait_ge(zeroed, 2)
            with pool.Fori(0, B) as b:
                pool.wait_ge(turned.sem, turned.of(b - 1))
                pool.tensor_copy(xb[:, :], core.x[:, bass.ds(b, 1), :].rearrange("p o h -> p (o h)")).then_inc(tile_in.sem, 1)

        @block.tensor
        def _(pe):
            for c in (turned, made, rep_made):
                c.open(pe)
            pe.wait_ge(loaded, 32)

            def turn_in(b):
                pe.wait_ge(tile_in.sem, tile_in.of(b))
                pe.wait_ge(ctx_in.sem, ctx_in.of(b))
                pe.wait_ge(in_up.sem, in_up.of(b - 1))
                for t in range(KT):
                    pe.transpose(p_in[:, t * P:(t + 1) * P], xb[:, t * P:(t + 1) * P], core.ident[:, :])
                for t in range(KT):
                    mm = pe.transpose(p_in[:, (KT + t) * P:(KT + t + 1) * P], cb[:, t * P:(t + 1) * P], core.ident[:, :])
                mm.then_inc(turned.sem, 1)

            def project(b):
                pe.wait_ge(in_up.sem, in_up.of(b))
                for j, (bank, w, name, n) in enumerate(((p_kv, wkv, "L0_xattn_bkv", 2 * H), (p_q, wq, "L0_xattn_bq", H))):
                    pe.wait_ge((kv_read, q_read)[j].sem, (kv_read, q_read)[j].of(b - 1))
                    pe.matmul(bank[:, 0:n], core.ones[:, :], core.bias(name), start=True, stop=False)
                    for t in range(KT):
                        mm = pe.matmul(bank[:, 0:n], inT[:, (1 - j) * KT + t, :], w[:, t, :],
                                       start=False, stop=(t == KT - 1))
                    mm.then_inc(made.sem, 1)

            def turn_reps(b):
                pe.wait_ge(reps.sem, reps.of(b))
                pe.wait_ge(rep_read.sem, rep_read.of(b - 1))
                for bank, src in ((p_kT, krep), (p_qT, qrep)):
                    for h in range(PAIRS):
                        mm = pe.transpose(bank[:, h * P:(h + 1) * P],
                                          src[:, 2 * h:2 * h + 2, :, :].rearrange("p a c d -> p (a c d)"), core.identb[:, :])
                mm.then_inc(rep_made.sem, 1)

            pipeline(pe, order, {"in": turn_in, "project": project, "reps": turn_reps}, B)
            pe.wait_ge(v_steps, 1)
            for t in range(KT):
                mm = pe.transpose(p_v[:, t * P:(t + 1) * P], cmax[:, t * P:(t + 1) * P], core.ident[:, :])
            mm.then_inc(v_turn, 1)
            pe.wait_ge(v_steps, 4)
            for t in range(KT):
                mm = pe.matmul(p_v[:, t * P:(t + 1) * P], svcol[:, t, :], core.ident[:, :], start=True, stop=True)
            mm.then_inc(v_turn, 1)

        @block.scalar
        def _(act):
            for c in (in_up, kv_read, rep_read):
                c.open(act)
            act.wait_ge(zeroed, 2)

            def inputs_up(b):
                act.wait_ge(turned.sem, turned.of(b))
                act.wait_ge(made.sem, made.of(b - 1))
                act.copy(inT[:, :, :].rearrange("p t n -> p (t n)"), p_in[:, :]).then_inc(in_up.sem, 1)

            def projected(b):
                act.wait_ge(made.sem, made.of(b, 1))
                act.wait_ge(kq_used.sem, kq_used.of(b - 1))
                act.copy(kq[:, 0, :], p_kv[:, 0:H])
                act.copy(vraw[:, bass.ds(b, 1), :].rearrange("p o h -> p (o h)"), p_kv[:, H:2 * H]).then_inc(kv_read.sem, 1)

            def reps_up(b):
                act.wait_ge(rep_made.sem, rep_made.of(b))
                for par in range(2):
                    r = slice(64 * par, 64 * par + 64)
                    i = act.copy(qz[r, par, :, bass.ds(b, 1), :].rearrange("p a o t -> p a (o t)"),
                                 p_qT[r, :].rearrange("p (a t) -> p a t", a=PAIRS))
                i.then_inc(rep_read.sem, 1)
                act.copy(kT[:, :, bass.ds(b * P, P)], p_kT[:, :].rearrange("p (a t) -> p a t", a=PAIRS)).then_inc(rep_read.sem, 1)

            pipeline(act, order, {"in": inputs_up, "project": projected, "reps": reps_up}, B)
            act.wait_ge(rep_read.sem, rep_read.of(B - 1))

        @block.vector
        def _(dve):
            for c in (reps, kq_used, q_read):
                c.open(dve)
            dve.memset(krep[:, :, 3, :], 0.0)
            dve.memset(qrep[:, :, 3, :], 0.0)
            ch = Chain(dve, steps, DVE_STEPS)
            kq3 = kq[:, :, :].rearrange("p j (h d) -> p (j h) d", d=XD)
            kqn3 = kqn[:, :, :].rearrange("p j (h d) -> p (j h) d", d=XD)
            kv3 = kval[:, :].rearrange("p (h d) -> p h d", d=XD)
            with dve.Fori(0, B) as b:
                ch.start(b)
                dve.wait_ge(made.sem, made.of(b, 2))
                dve.tensor_scalar(kq[:, 1, :], p_q[:, 0:H], float(XD) ** -0.5, None, ALU.mult).then_inc(q_read.sem, 1)
                dve.wait_ge(q_read.sem, q_read.of(b))
                dve.wait_ge(kv_read.sem, kv_read.of(b))
                ch.link(dve.tensor_reduce(amax[:, :], kq3, AX.X, ALU.max, apply_absolute_value=True))
                ch.link(dve.tensor_scalar(scl[:, :], amax[:, :], 1.0 / QMAX, FLOOR, ALU.mult, ALU.max))
                ch.mark(dve.reciprocal(rec[:, :], scl[:, :]))
                ch.link(dve.tensor_copy(sq[:, :, :, bass.ds(b, 1)].rearrange("p r a o -> p a (r o)"),
                                        scl[:, XH:].rearrange("p (a r) -> p a r", r=2)))
                dve.tensor_tensor(kqn3, kq3, bcast(rec[:, :], [P, 2 * XH, XD]), ALU.mult).then_inc(kq_used.sem, 1)
                dve.wait_ge(kq_used.sem, kq_used.of(b))
                ch.link(dve.tensor_scalar(kqn[:, :, :], kqn[:, :, :], ROUND, ROUND, ALU.add, ALU.subtract))
                dve.wait_ge(rep_made.sem, rep_made.of(b - 1))
                ch.mark(dve.tensor_tensor(kv3, kqn3[:, 0:XH, :], bcast(scl[:, 0:XH], [P, XH, XD]), ALU.mult))
                ch.mark(dve.tensor_copy(qrep[:, :, 0:3, :],
                                        kqn3[:, XH:, :].unsqueeze(2).to_broadcast([P, XH, 3, XD])))
                ch.wait()
                for j in range(3):
                    i = dve.tensor_copy(krep[:, :, j, :], kv3)
                    if j < 2:
                        ch.link(i)
                        i = dve.tensor_tensor(kv3, kv3, krep[:, :, j, :], ALU.subtract)
                        ch.link(i)
                    else:
                        i.then_inc(reps.sem, 1)
                ch.end()
            dve.wait_ge(kv_read.sem, kv_read.of(B - 1))
            dve.tensor_reduce(cmax[:, :], vraw[:, :, :].rearrange("p b h -> p h b"), AX.X, ALU.max,
                              apply_absolute_value=True).then_inc(v_steps, 1)
            dve.wait_ge(v_turn, 1)
            dve.tensor_reduce(vstat[:, 0, :], p_v[:, 0:H].rearrange("p (t n) -> p t n", t=KT), AX.X, ALU.max).then_inc(v_steps, 1)
            dve.wait_ge(v_steps, 2)
            dve.tensor_scalar(vstat[:, 1, :], vstat[:, 0, :], 1.0 / QMAX, FLOOR, ALU.mult, ALU.max).then_inc(v_steps, 1)
            dve.wait_ge(v_steps, 3)
            dve.tensor_copy(svcol[:, :, :], bcast(vstat[:, 1, :], [P, KT, P])).then_inc(v_steps, 1)
            dve.wait_ge(v_turn, 2)
            dve.tensor_copy(sv[:, :], p_v[:, 0:H]).then_inc(v_steps, 1)
            dve.wait_ge(v_steps, 5)
            dve.reciprocal(rsv[:, :], sv[:, :]).then_inc(v_steps, 1)
            dve.wait_ge(v_steps, 6)
            dve.tensor_tensor(vraw[:, :, :], vraw[:, :, :], over_heads(rsv[:, :], B), ALU.mult).then_inc(v_steps, 1)
            dve.wait_ge(v_steps, 7)
            dve.tensor_scalar(vi[:, :, :], vraw[:, :, :], ROUND, ROUND, ALU.add, ALU.subtract).then_inc(v_steps, 1)
            dve.wait_ge(v_steps, 8)


def x0_attend(core, qz, kT, vi, sq, att, esum):
    nc = core.nc
    HALF = B * P // 2
    LOG_AMAX = float(np.log(AMAX))
    with ExitStack() as ctx:
        def sb(name, shape, dt=F32):
            return ctx.enter_context(nc.sbuf_tensor("x2_" + name, shape, dt))

        def ps(name, shape, dt=F32):
            return ctx.enter_context(nc.psum_tensor("x2_" + name, shape, dt))

        sem = semaphores(nc, ctx)

        def count(name, per):
            return Count(sem("x2_" + name), per)

        ints = [sb(f"ints{i}", [P, 2, HALF], U16) for i in range(2)]
        turned = [sb(f"turned{i}", [P, B, P], BF16) for i in range(2)]
        hmax = sb("hmax", [P, 2, 2])
        top = sb("top", [P, 2])
        nb = sb("nb", [P, 2])
        p_s = [[ps("p_s00", [P, HALF]), ps("p_s10", [P, HALF])], [ps("p_s1", [P, HALF])] * 2]
        p_t = ps("p_t", [P, HALF], BF16)
        p_o = ps("p_o", [P, BANK])
        PASSES = PAIRS * B

        s_made = count("s_made", 4)
        max_up = count("max_up", 4)
        top_up = count("top_up", 2)
        bias_up = count("bias_up", 2)
        e_up = count("e_up", 6)
        t_made = count("t_made", 4)
        t_act = count("t_act", 2)
        t_dve = count("t_dve", 2)
        o_made = count("o_made", 2)
        o_read = count("o_read", 2)
        block = ctx.enter_context(nc.Block())

        @block.tensor
        def _(pe):
            for c in (s_made, t_made, o_made):
                c.open(pe)

            def scores(a, n, par, half, c):
                return pe.matmul(p_s[half][par][:, c * BANK:(c + 1) * BANK],
                          qz[:, par, :, :, :].rearrange("p a b t -> p (a b) t")[:, bass.ds(n, 1), :].rearrange("p o t -> p (o t)"),
                          kT[:, bass.ds(a, 1), half * HALF + c * BANK:half * HALF + (c + 1) * BANK].rearrange("p a n -> p (a n)"),
                          start=True, stop=True)

            def scores0(a, n, par):
                pe.wait_ge(e_up.sem, e_up.of(n - 1, 3 * par + 3))
                for c in range(2):
                    mm = scores(a, n, par, 0, c)
                mm.then_inc(s_made.sem, 1)

            def scores1(a, n, par):
                for c in range(2):
                    pe.wait_ge(e_up.sem, e_up.of(n, c + 1) if par else e_up.of(n - 1, 3 + c + 1))
                    mm = scores(a, n, par, 1, c)
                mm.then_inc(s_made.sem, 1)

            def turn(a, n, par, half):
                if half:
                    pe.wait_ge(e_up.sem, e_up.of(n, 3 * par + 2))
                    pe.wait_ge(t_dve.sem, t_dve.of(n, 1) if par else t_dve.of(n - 1))
                else:
                    pe.wait_ge(e_up.sem, e_up.of(n, 3 * par + 3))
                    pe.wait_ge(t_act.sem, t_act.of(n, par + 1))
                for c in range(8):
                    mm = pe.transpose(p_t[:, c * P:(c + 1) * P],
                                      ints[par][:, half, c * P:(c + 1) * P].bitcast(BF16), core.identb[:, :])
                mm.then_inc(t_made.sem, 1)

            def values(a, n, par):
                pe.wait_ge(o_read.sem, o_read.of(n, 1) if par else o_read.of(n - 1))
                pe.wait_ge(t_act.sem, t_act.of(n, par + 1))
                pe.wait_ge(t_dve.sem, t_dve.of(n, par + 1))
                for k in range(B):
                    mm = pe.matmul(p_o[:, 0:XD], turned[par][:, k, :],
                                   vi[:, k, bass.ds(a * (2 * XD) + par * XD, XD)], start=(k == 0), stop=(k == B - 1))
                mm.then_inc(o_made.sem, 1)

            def emit(*passes):
                line = [p and (*p, par) for p in passes for par in (1, 0)]
                for par in range(2):
                    here, last, earlier, oldest = (line + [None])[1 - par:][:4]
                    if last:
                        scores1(*last)
                    if earlier:
                        turn(*earlier, 1)
                    if here:
                        scores0(*here)
                    if oldest:
                        values(*oldest)
                    if earlier:
                        turn(*earlier, 0)

            emit((0, 0), None, None)
            emit((0, 1), (0, 0), None)
            with pe.Fori(2, B) as t:
                emit((0, t), (0, t - 1), (0, t - 2))
            with pe.Fori(1, PAIRS) as a:
                n = a * B
                emit((a, n), (a - 1, n - 1), (a - 1, n - 2))
                emit((a, n + 1), (a, n), (a - 1, n - 1))
                with pe.Fori(2, B) as t:
                    emit((a, n + t), (a, n + t - 1), (a, n + t - 2))
            emit(None, (PAIRS - 1, PASSES - 1), (PAIRS - 1, PASSES - 2))
            emit(None, None, (PAIRS - 1, PASSES - 1))

        def of_pass(ap, n):
            return ap[:, bass.ds(n, 1)].rearrange("p o -> p (o)")

        @block.scalar
        def _(act):
            for c in (e_up, t_act):
                c.open(act)

            def leave(par):
                def run(n):
                    act.wait_ge(t_made.sem, t_made.of(n, 2 * par + 1))
                    act.wait_ge(o_made.sem, o_made.of(n - 1, par + 1))
                    act.copy(turned[par][:, 8:16, :].rearrange("p k n -> p (k n)"), p_t[:, :].bitcast(U16)).then_inc(t_act.sem, 1)
                return run

            def exps(par):
                def run(n):
                    act.wait_ge(bias_up.sem, bias_up.of(n, par + 1))
                    act.wait_ge(t_made.sem, t_made.of(n - 1, 2 * par + 2))
                    for i, (half, lo, hi) in enumerate(((1, 0, BANK), (1, BANK, HALF), (0, 0, HALF))):
                        act.activation(ints[par][:, half, lo:hi], p_s[half][par][:, lo:hi], ACT.Exp, bias=nb[:, par:par + 1],
                                       scale=of_pass(sq[:, par, :, :].rearrange("p a b -> p (a b)"), n),
                                       accum_out=of_pass(esum[:, :, :, par, i].rearrange("p a b -> p (a b)"), n)
                                       ).then_inc(e_up.sem, 1)
                return run

            pipeline(act, [("leave1", 1), ("exp0", 0), ("leave0", 0), ("exp1", 0)],
                     {"leave1": leave(1), "exp0": exps(0), "leave0": leave(0), "exp1": exps(1)}, PASSES)

        @block.vector
        def _(dve):
            for c in (max_up, top_up, bias_up, t_dve, o_read):
                c.open(dve)

            def half_max(par, half):
                def run(n):
                    dve.wait_ge(s_made.sem, s_made.of(n, 2 * par + half + 1))
                    dve.tensor_reduce(hmax[:, par, half:half + 1], p_s[half][par][:, :], AX.X, ALU.max).then_inc(max_up.sem, 1)
                return run

            def row_max(par):
                def run(n):
                    half_max(par, 1)(n)
                    dve.wait_ge(max_up.sem, max_up.of(n, 2 * par + 2))
                    dve.tensor_scalar(top[:, par:par + 1], hmax[:, par, 0:1], hmax[:, par, 1:2],
                                      of_pass(sq[:, par, :, :].rearrange("p a b -> p (a b)"), n),
                                      ALU.max, ALU.mult).then_inc(top_up.sem, 1)
                    dve.wait_ge(top_up.sem, top_up.of(n, par + 1))
                    dve.wait_ge(e_up.sem, e_up.of(n - 1, 3 * par + 3))
                    dve.tensor_scalar(nb[:, par:par + 1], top[:, par:par + 1], -1.0, LOG_AMAX, ALU.mult, ALU.add).then_inc(bias_up.sem, 1)
                return run

            def leave(par):
                def run(n):
                    dve.wait_ge(t_made.sem, t_made.of(n, 2 * par + 2))
                    dve.wait_ge(o_made.sem, o_made.of(n - 1, par + 1))
                    dve.tensor_copy(turned[par][:, 0:8, :].rearrange("p k n -> p (k n)"), p_t[:, :].bitcast(U16)).then_inc(t_dve.sem, 1)
                return run

            def keep(par):
                def run(n):
                    dve.wait_ge(o_made.sem, o_made.of(n, par + 1))
                    dve.tensor_copy(att[:, bass.ds(n * (2 * XD) + par * XD, XD)], p_o[:, 0:XD]).then_inc(o_read.sem, 1)
                return run

            pipeline(dve, [("max0", 0), ("leave0", 1), ("keep1", 2), ("row0", 0),
                           ("max1", 0), ("leave1", 1), ("keep0", 1), ("row1", 0)],
                     {"max0": half_max(0, 0), "max1": half_max(1, 0), "row0": row_max(0), "row1": row_max(1),
                      "leave0": leave(0), "leave1": leave(1), "keep0": keep(0), "keep1": keep(1)}, PASSES)


def x0_output(core, sv, att, esum, ahead):
    nc, A = core.nc, core.A
    with ExitStack() as ctx:
        def sb(name, shape, dt=F32):
            return ctx.enter_context(nc.sbuf_tensor("x3_" + name, shape, dt))

        def ps(name, shape, dt=F32):
            return ctx.enter_context(nc.psum_tensor("x3_" + name, shape, dt))

        sem = semaphores(nc, ctx)

        def count(name, per):
            return Count(sem("x3_" + name), per)

        wp = sb("wp", [P, KT, H])
        den, rden = sb("den", [P, XH]), sb("rden", [P, XH])
        o = sb("o", [P, H])
        oT = sb("oT", [P, KT, P])
        y, stats, mv, ln_r = sb("y", [P, H]), sb("stats", [P, 6]), sb("mv", [P, 2]), sb("ln_r", [P, 1])
        p_oT, p_y = ps("p_oT", [P, BANK]), ps("p_y", [P, BANK])
        loaded = sem("x3_loaded")
        steps, tail_steps = sem("x3_steps"), sem("x3_tail_steps")
        o_up, turned, oT_up = count("o_up", 1), count("turned", 1), count("oT_up", 1)
        made, read = count("made", 1), count("read", 1)
        var_up, rooted, x_up = count("var_up", 1), count("rooted", 1), count("x_up", 1)
        block = ctx.enter_context(nc.Block())

        @block.sync
        def _(sp):
            sp.dma_start(wp[:, :, :], A["L0_xattn_Wp"].rearrange("(t p) n -> p t n", p=P)).then_inc(loaded, 16)
            ahead.load(sp)
            sp.wait_ge(loaded, 16)

        order = [("scale", 0), ("norm1", 1), ("turn", 0), ("project", 0), ("norm2", 1)]

        @block.gpsimd
        def _(pool):
            rooted.open(pool)

            def root(b):
                pool.wait_ge(var_up.sem, var_up.of(b))
                pool.tensor_tensor(ln_r[:, :], mv[:, 1:2], core.neghalf[:, 0:1], ALU.pow).then_inc(rooted.sem, 1)

            pipeline(pool, order, {"norm1": root}, B)

        @block.tensor
        def _(pe):
            turned.open(pe)
            made.open(pe)
            pe.wait_ge(loaded, 16)

            def turn(b):
                pe.wait_ge(o_up.sem, o_up.of(b))
                pe.wait_ge(oT_up.sem, oT_up.of(b - 1))
                for t in range(KT):
                    mm = pe.transpose(p_oT[:, t * P:(t + 1) * P], o[:, t * P:(t + 1) * P], core.ident[:, :])
                mm.then_inc(turned.sem, 1)

            def project(b):
                pe.wait_ge(oT_up.sem, oT_up.of(b))
                pe.wait_ge(read.sem, read.of(b - 1))
                pe.matmul(p_y[:, 0:H], core.ones[:, :], core.bias("L0_xattn_bp"), start=True, stop=False)
                for t in range(KT):
                    mm = pe.matmul(p_y[:, 0:H], oT[:, t, :], wp[:, t, :], start=False, stop=(t == KT - 1))
                mm.then_inc(made.sem, 1)

            pipeline(pe, order, {"turn": turn, "project": project}, B)

        @block.scalar
        def _(act):
            oT_up.open(act)

            def turned_up(b):
                act.wait_ge(turned.sem, turned.of(b))
                act.wait_ge(made.sem, made.of(b - 1))
                act.copy(oT[:, :, :].rearrange("p t n -> p (t n)"), p_oT[:, 0:H]).then_inc(oT_up.sem, 1)

            pipeline(act, order, {"turn": turned_up}, B)

        @block.vector
        def _(dve):
            for c in (o_up, read, var_up, x_up):
                c.open(dve)
            first, tail = Chain(dve, steps, 3), Chain(dve, tail_steps, 3)
            heads = att[:, :].rearrange("p (a b r d) -> p a b r d", a=PAIRS, b=B, r=2)

            def scale(b):
                first.start(b)
                dve.wait_ge(turned.sem, turned.of(b - 1))
                first.link(dve.tensor_reduce(den[:, :].rearrange("p (a c) -> p a c", c=2),
                                             esum[:, :, bass.ds(b, 1), :, :].rearrange("p a o c k -> p (a o) c k"), AX.X, ALU.add))
                first.link(dve.reciprocal(rden[:, :], den[:, :]))
                first.link(dve.tensor_tensor(o[:, :].rearrange("p (a r d) -> p a r d", r=2, d=XD),
                                             heads[:, :, bass.ds(b, 1), :, :].rearrange("p a o r d -> p a (o r) d"),
                                             rden[:, :].rearrange("p (a r) -> p a r", r=2).unsqueeze(3).to_broadcast([P, PAIRS, 2, XD]),
                                             ALU.mult))
                dve.tensor_tensor(o[:, :], o[:, :], sv[:, :], ALU.mult).then_inc(o_up.sem, 1)
                first.end()

            def norm(part):
                def run(b):
                    part(dve, tail, core, b, y, stats, mv, ln_r, made, p_y[:, 0:H], read, var_up, rooted, x_up)
                return run

            pipeline(dve, order, {"scale": scale, "norm1": norm(norm_statistics), "norm2": norm(norm_apply)}, B)


def small_attention(core, tag, heads, wqkv, wo, causal, source=None, biases=None, norms=None, bias_o=None, ahead=None):
    nc, A = core.nc, core.A
    dk = H // heads
    per_tile = P // dk
    NG = heads // G
    inputs = 2 if source else 1
    with ExitStack() as ctx:
        def sb(name, shape, dt=F32):
            return ctx.enter_context(nc.sbuf_tensor(f"{tag}_{name}", shape, dt))

        def ps(name, shape, dt=F32):
            return ctx.enter_context(nc.psum_tensor(f"{tag}_{name}", shape, dt))

        named = semaphores(nc, ctx)

        def sem(name):
            return named(f"{tag}_{name}")

        def count(name, per):
            return Count(sem(name), per)

        w = sb("w", [P, KT, 3 * H])
        w_o = sb("w_o", [P, KT, H])
        owner = sb("owner", [P, per_tile])
        gains = sb("gains", [P, 2, H])
        xb, cb = sb("xb", [P, H]), sb("cb", [P, H])
        inT = sb("inT", [P, inputs * KT, P])
        qk = sb("qk", [P, 2, H])
        vaug = sb("vaug", [P, heads, dk + 1])
        sq, ssq, rstd = sb("sq", [P, 2, H]), sb("ssq", [P, 2]), sb("rstd", [P, 2])
        qkT = sb("qkT", [P, 2, KT, P])
        kz = sb("kz", [P, KT, per_tile, P])
        rmax = sb("rmax", [P, heads])
        e = [sb(f"e{i}", [P, G, P]) for i in range(2)]
        eT = [sb(f"eT{i}", [P, G, P]) for i in range(2)]
        rden = sb("rden", [P, heads])
        o = sb("o", [P, H])
        oT = sb("oT", [P, KT, P])
        y, stats, mv, ln_r = sb("y", [P, H]), sb("stats", [P, 6]), sb("mv", [P, 2]), sb("ln_r", [P, 1])
        p_in, p_qk, p_v, p_e, p_o, p_y = (ps(n, [P, BANK]) for n in ("p_in", "p_qk", "p_v", "p_e", "p_o", "p_y"))
        p_s = [ps(f"p_s{i}", [P, BANK]) for i in range(2)]

        loaded, ready = sem("loaded"), sem("ready")
        front_steps, mid_steps, out_steps, tail_steps = (sem(n) for n in ("front_steps", "mid_steps", "out_steps", "tail_steps"))
        ctx_in = count("ctx_in", 16)
        tile_in = count("tile_in", 1)
        in_turned, in_up = count("in_turned", 1), count("in_up", 1)
        qk_turned, qkT_up = count("qk_turned", 1), count("qkT_up", KT)
        o_turned, oT_up = count("o_turned", 1), count("oT_up", 1)
        made, up = count("made", 2), count("up", 2)
        squares_up, qk_root, qk_up, kz_up = count("squares_up", 1), count("qk_root", 1), count("qk_up", 1), count("kz_up", KT)
        s_made, s_read, e_up = count("s_made", NG), count("s_read", NG), count("e_up", NG)
        e_turned, eT_up, o_part = count("e_turned", NG), count("eT_up", NG), count("o_part", NG)
        o_up = count("o_up", 1)
        y_made, y_read, var_up = count("y_made", 1), count("y_read", 1), count("var_up", 1)
        ln_root, x_up = count("ln_root", 1), count("x_up", 1)
        LOADS = 5 + 2 * bool(norms)
        half = NG // 2
        block = ctx.enter_context(nc.Block())

        if NG == 8:
            lag, beats = 1, [[("t_out", 2), ("f_in", 0)], [("t_turn", 2), ("f_project", 0)],
                             [("f_norm", 0), ("t_project", 2)], [("t_norm1", 2), ("f_turn", 0), ("f_cols0", 0)], [],
                             [("t_norm2", 2)], [("f_cols1", 0), ("s0", 0)], [("e0", 0), ("s1", 0)], [("f_values", 0)]]
        else:
            lag, beats = 2, [[("t_out", 3), ("f_norm", 1)], [("f_turn", 1), ("f_cols0", 1), ("t_turn", 3)],
                             [("f_cols1", 1), ("t_project", 3), ("s0", 1), ("f_in", 0)],
                             [("t_norm1", 3), ("e0", 1), ("s1", 1), ("t_norm2", 3)], [("f_values", 1), ("f_project", 0)]]
        order = []
        for g, beat in enumerate(beats):
            order += [(f"m{g}" if g < NG else "m_last", lag), *beat]

        @block.sync
        def _(sp):
            for j, name in enumerate(wqkv):
                sp.dma_start(w[:, :, j * H:(j + 1) * H], A[name].rearrange("(t p) n -> p t n", p=P)).then_inc(loaded, 16)
            sp.dma_start(w_o[:, :, :], A[wo].rearrange("(t p) n -> p t n", p=P)).then_inc(loaded, 16)
            sp.dma_start(owner[:, :], A[f"c_owner{dk}"]).then_inc(loaded, 16)
            for j, name in enumerate(norms or ()):
                sp.dma_start(gains[:, j, :], A[name].partition_broadcast(P)).then_inc(loaded, 16)
            if source:
                ctx_in.open(sp)
                with sp.Fori(0, B) as b:
                    sp.wait_ge(in_turned.sem, in_turned.of(b - 1))
                    sp.dma_start(cb[:, :], A[source][bass.ds(b, 1), :, :].rearrange("o p h -> (o p) h")).then_inc(ctx_in.sem, 16)
                sp.wait_ge(ctx_in.sem, ctx_in.of(B - 1))
            sp.wait_ge(loaded, 16 * LOADS)

        @block.gpsimd
        def _(pool):
            for c in (tile_in, qk_root, kz_up, ln_root):
                c.open(pool)
            pool.wait_ge(loaded, 16 * LOADS)

            def tile_copy(b):
                pool.wait_ge(in_turned.sem, in_turned.of(b - 1))
                pool.tensor_copy(xb[:, :], core.x[:, bass.ds(b, 1), :].rearrange("p o h -> p (o h)")).then_inc(tile_in.sem, 1)

            def norm(b):
                pool.wait_ge(squares_up.sem, squares_up.of(b))
                pool.tensor_tensor(rstd[:, :], ssq[:, :], core.neghalf[:, 0:2], ALU.pow).then_inc(qk_root.sem, 1)

            def spread_keys(t):
                def run(b):
                    pool.wait_ge(qkT_up.sem, qkT_up.of(b, t + 1))
                    pool.wait_ge(s_made.sem, s_made.of(b - 1, (t + 1) * half))
                    pool.tensor_tensor(kz[:, t, :, :], over_heads(qkT[:, 1, t, :], per_tile),
                                       bcast(owner[:, :], [P, per_tile, P]), ALU.mult).then_inc(kz_up.sem, 1)
                return run

            def root(b):
                pool.wait_ge(var_up.sem, var_up.of(b))
                pool.tensor_tensor(ln_r[:, :], mv[:, 1:2], core.neghalf[:, 0:1], ALU.pow).then_inc(ln_root.sem, 1)

            pieces = {"f_in": tile_copy, "f_cols0": spread_keys(0), "f_cols1": spread_keys(1), "t_norm1": root}
            if norms:
                pieces["f_norm"] = norm
            pipeline(pool, order, pieces, B)

        @block.tensor
        def _(pe):
            for c in (in_turned, qk_turned, o_turned, made, s_made, e_turned, o_part, y_made):
                c.open(pe)
            pe.wait_ge(loaded, 16 * LOADS)

            def turn_in(b):
                pe.wait_ge(tile_in.sem, tile_in.of(b))
                pe.wait_ge(qkT_up.sem, qkT_up.of(b - 1))
                if source:
                    pe.wait_ge(ctx_in.sem, ctx_in.of(b))
                for i, src in enumerate((xb, cb)[:inputs]):
                    for t in range(KT):
                        mm = pe.transpose(p_in[:, (i * KT + t) * P:(i * KT + t + 1) * P], src[:, t * P:(t + 1) * P], core.ident[:, :])
                mm.then_inc(in_turned.sem, 1)

            def project(b):
                pe.wait_ge(in_up.sem, in_up.of(b))

                def one(out, i, first, last=True):
                    at = KT * (inputs - 1) * (i > 0)
                    if biases:
                        pe.matmul(out, core.ones[:, :], core.bias(biases[i]), start=first, stop=False)
                    for t in range(KT):
                        mm = pe.matmul(out, inT[:, at + t, :], w[:, t, i * H:(i + 1) * H],
                                       start=first and not biases and t == 0, stop=last and t == KT - 1)
                    return mm

                pe.wait_ge(up.sem, up.of(b - 1))
                one(p_qk[:, 0:H], 0, True, last=False)
                one(p_qk[:, H:2 * H], 1, False).then_inc(made.sem, 1)
                one(p_v[:, 0:H], 2, True).then_inc(made.sem, 1)

            def turn_qk(b):
                pe.wait_ge(qk_up.sem, qk_up.of(b))
                for j in range(2):
                    for t in range(KT):
                        mm = pe.transpose(p_in[:, (j * KT + t) * P:(j * KT + t + 1) * P], qk[:, j, t * P:(t + 1) * P], core.ident[:, :])
                mm.then_inc(qk_turned.sem, 1)

            def scores(g):
                def run(b):
                    t, lo = g // half, g * G % per_tile
                    pe.wait_ge(kz_up.sem, kz_up.of(b, t + 1))
                    pe.wait_ge(s_read.sem, s_read.of(b, g - 1) if g >= 2 else s_read.of(b - 1, NG - 1 + g))
                    if causal:
                        pe.matmul(p_s[g % 2][:, :], core.identb[:, :], core.causal[:, :, :].rearrange("p g k -> p (g k)"),
                                  start=True, stop=False)
                    pe.matmul(p_s[g % 2][:, :], qkT[:, 0, t, :], kz[:, t, lo:lo + G, :].rearrange("p g k -> p (g k)"),
                              start=not causal, stop=True).then_inc(s_made.sem, 1)
                return run

            def heads_out(b, g):
                pe.wait_ge(eT_up.sem, eT_up.of(b, g + 1))
                if g == 0:
                    pe.wait_ge(o_up.sem, o_up.of(b - 1))
                    pe.wait_ge(up.sem, up.of(b))
                for h in range(G):
                    n = g * G + h
                    mm = pe.matmul(p_o[:, n * (dk + 1):(n + 1) * (dk + 1)], eT[g % 2][:, h, :], vaug[:, n, :],
                                   start=(n == 0), stop=(n == heads - 1))
                mm.then_inc(o_part.sem, 1)

            def group(g):
                def run(b):
                    pe.wait_ge(e_up.sem, e_up.of(b, g + 1))
                    pe.wait_ge(eT_up.sem, eT_up.of(b, g))
                    for h in range(G):
                        mm = pe.transpose(p_e[:, h * P:(h + 1) * P], e[g % 2][:, h, :], core.ident[:, :])
                    mm.then_inc(e_turned.sem, 1)
                    if g + 2 < NG:
                        scores(g + 2)(b)
                    if g:
                        heads_out(b, g - 1)
                return run

            def last_group(b):
                heads_out(b, NG - 1)

            def turn_out(b):
                pe.wait_ge(o_up.sem, o_up.of(b))
                pe.wait_ge(y_read.sem, y_read.of(b - 1))
                for t in range(KT):
                    mm = pe.transpose(p_y[:, H + t * P:H + (t + 1) * P], o[:, t * P:(t + 1) * P], core.ident[:, :])
                mm.then_inc(o_turned.sem, 1)

            def output(b):
                pe.wait_ge(oT_up.sem, oT_up.of(b))
                if bias_o:
                    pe.matmul(p_y[:, 0:H], core.ones[:, :], core.bias(bias_o), start=True, stop=False)
                for t in range(KT):
                    mm = pe.matmul(p_y[:, 0:H], oT[:, t, :], w_o[:, t, :], start=(not bias_o and t == 0), stop=(t == KT - 1))
                mm.then_inc(y_made.sem, 1)

            pieces = {"f_in": turn_in, "f_project": project, "f_turn": turn_qk, "s0": scores(0), "s1": scores(1),
                      "m_last": last_group, "t_turn": turn_out, "t_project": output}
            pieces.update({f"m{g}": group(g) for g in range(NG)})
            pipeline(pe, order, pieces, B)

        @block.scalar
        def _(act):
            for c in (in_up, qkT_up, oT_up, up, e_up, eT_up):
                c.open(act)
            if ahead:
                ahead.load(act)
            act.wait_ge(ready, 1)

            def inputs_up(b):
                act.wait_ge(in_turned.sem, in_turned.of(b))
                act.wait_ge(made.sem, made.of(b - 1))
                act.copy(inT[:, :, :].rearrange("p t n -> p (t n)"), p_in[:, 0:inputs * H]).then_inc(in_up.sem, 1)

            def queries_up(b):
                act.wait_ge(made.sem, made.of(b, 1))
                act.wait_ge(qk_turned.sem, qk_turned.of(b - 1))
                act.copy(qk[:, :, :].rearrange("p j n -> p (j n)"), p_qk[:, :]).then_inc(up.sem, 1)

            def values_up(b):
                act.wait_ge(made.sem, made.of(b, 2))
                act.wait_ge(o_part.sem, o_part.of(b - 1))
                act.copy(vaug[:, :, 0:dk], p_v[:, 0:H].rearrange("p (h d) -> p h d", d=dk)).then_inc(up.sem, 1)

            def columns(t):
                def run(b):
                    act.wait_ge(qk_turned.sem, qk_turned.of(b))
                    act.wait_ge(s_made.sem, s_made.of(b - 1, (t + 1) * half))
                    act.wait_ge(kz_up.sem, kz_up.of(b - 1, t + 1))
                    act.copy(qkT[:, :, t, :], p_in[:, :].rearrange("p (j t n) -> p j t n", j=2, t=KT)[:, :, t, :]).then_inc(qkT_up.sem, 1)
                return run

            def exps(g):
                def run(b):
                    act.wait_ge(s_read.sem, s_read.of(b, g + 1))
                    ef = e[g % 2][:, :, :].rearrange("p g k -> p (g k)")
                    act.activation(ef, ef, ACT.Exp, scale=float(dk) ** -0.5).then_inc(e_up.sem, 1)
                return run

            def group(g):
                def run(b):
                    act.wait_ge(e_turned.sem, e_turned.of(b, g + 1))
                    act.wait_ge(o_part.sem, o_part.of(b, g - 1) if g >= 2 else o_part.of(b - 1, NG - 1 + g))
                    act.copy(eT[g % 2][:, :, :].rearrange("p g k -> p (g k)"), p_e[:, :]).then_inc(eT_up.sem, 1)
                    if g + 1 < NG:
                        exps(g + 1)(b)
                return run

            def output_up(b):
                act.wait_ge(o_turned.sem, o_turned.of(b))
                act.wait_ge(y_made.sem, y_made.of(b - 1))
                act.copy(oT[:, :, :].rearrange("p t n -> p (t n)"), p_y[:, H:2 * H]).then_inc(oT_up.sem, 1)

            pieces = {"f_in": inputs_up, "f_project": queries_up, "f_values": values_up, "f_cols0": columns(0),
                      "f_cols1": columns(1), "e0": exps(0), "t_turn": output_up}
            pieces.update({f"m{g}": group(g) for g in range(NG)})
            pipeline(act, order, pieces, B)

        @block.vector
        def _(dve):
            for c in (squares_up, qk_up, s_read, o_up, y_read, var_up, x_up):
                c.open(dve)
            dve.memset(vaug[:, :, dk:dk + 1], 1.0).then_inc(ready, 1)
            dve.wait_ge(loaded, 16 * LOADS)
            front = Chain(dve, front_steps, 2)
            mid = Chain(dve, mid_steps, NG)
            out, tail = Chain(dve, out_steps, 1), Chain(dve, tail_steps, 3)

            def sums(b):
                front.start(b)
                dve.wait_ge(up.sem, up.of(b, 1))
                front.link(dve.tensor_tensor(sq[:, :, :], qk[:, :, :], qk[:, :, :], ALU.mult))
                dve.wait_ge(qk_root.sem, qk_root.of(b - 1))
                front.link(dve.tensor_reduce(ssq[:, :], sq[:, :, :], AX.X, ALU.add))
                dve.tensor_scalar(ssq[:, :], ssq[:, :], 1.0 / H, RMS_EPS, ALU.mult, ALU.add).then_inc(squares_up.sem, 1)
                front.end()

            def norm(b):
                dve.wait_ge(qk_root.sem, qk_root.of(b))
                for j in range(2):
                    i = dve.scalar_tensor_tensor(out=qk[:, j, :], in0=qk[:, j, :], scalar=rstd[:, j:j + 1],
                                                 in1=gains[:, j, :], op0=ALU.mult, op1=ALU.mult)
                i.then_inc(qk_up.sem, 1)

            def no_norm(b):
                dve.wait_ge(up.sem, up.of(b, 1))
                dve.sem_inc(qk_up.sem, 1)

            def shift(g):
                def run(b):
                    dve.wait_ge(s_made.sem, s_made.of(b, g + 1))
                    dve.wait_ge(e_turned.sem, e_turned.of(b, g - 1) if g >= 2 else e_turned.of(b - 1, NG - 1 + g))
                    s3 = p_s[g % 2][:, :].rearrange("p (h k) -> p h k", h=G)
                    top = rmax[:, g * G:(g + 1) * G]
                    mid.b, mid.n = b, g
                    mid.link(dve.tensor_reduce(top, s3, AX.X, ALU.max))
                    dve.tensor_tensor(e[g % 2][:, :, :], s3, bcast(top, [P, G, P]), ALU.subtract).then_inc(s_read.sem, 1)
                return run

            def output(b):
                out.start(b)
                dve.wait_ge(o_part.sem, o_part.of(b))
                dve.wait_ge(o_turned.sem, o_turned.of(b - 1))
                o3 = p_o[:, 0:heads * (dk + 1)].rearrange("p (h d) -> p h d", d=dk + 1)
                out.link(dve.reciprocal(rden[:, :].unsqueeze(2), o3[:, :, dk:dk + 1]))
                dve.tensor_tensor(o[:, :].rearrange("p (h d) -> p h d", d=dk), o3[:, :, 0:dk],
                                  bcast(rden[:, :], [P, heads, dk]), ALU.mult).then_inc(o_up.sem, 1)

            def layer_norm(part):
                def run(b):
                    part(dve, tail, core, b, y, stats, mv, ln_r, y_made, p_y[:, 0:H], y_read, var_up, ln_root, x_up)
                return run

            pieces = {"f_project": sums if norms else no_norm, "s0": shift(0), "s1": shift(1),
                      "t_out": output, "t_norm1": layer_norm(norm_statistics),
                      "t_norm2": layer_norm(norm_apply)}
            if norms:
                pieces["f_norm"] = norm
            pieces.update({f"m{g}": shift(g + 2) for g in range(NG - 2)})
            pipeline(dve, order, pieces, B)


def l1_self_attention(core):
    small_attention(core, "s1", 32, ("L1_attn_Wq", "L1_attn_Wk", "L1_attn_Wv"), "L1_attn_Wo", causal=True)


def l1_cross_attention(core, ahead):
    small_attention(core, "c1", 16, ("L1_xattn_Wq", "L1_xattn_Wk_img", "L1_xattn_Wv_img"), "L1_xattn_Wo", causal=False,
                    source="ctx_2048", biases=("L1_xattn_bq", "L1_xattn_bk_img", "L1_xattn_bv_img"),
                    norms=("L1_xattn_gq", "L1_xattn_gk_img"), bias_o="L1_xattn_bo", ahead=ahead)


EXPERTS, CHOICES = 16, 6
EI, SI = 176, 352
GROUP = 4
NT = GROUP * P


class Weights:

    def __init__(self, core, ctx, tag, width, loads, experts=False):
        nc = core.nc
        self.tiles = -(-width // P)
        self.width = width

        def sb(name, shape):
            return ctx.enter_context(nc.sbuf_tensor(f"{tag}_{name}", shape, F32))

        self.wg, self.wu = sb("wg", [P, KT, width]), sb("wu", [P, KT, width])
        self.wd = sb("wd", [P, self.tiles, H])
        self.loads = list(loads(core.A, self.wg, self.wu, self.wd))
        if experts:
            self.router = sb("w_r", [P, KT, EXPERTS])
            self.owners = ctx.enter_context(nc.sbuf_tensor(f"{tag}_owners", [64, self.tiles, P], F32))
            self.loads += [(self.router[:, :, :], core.A["L1_ffn_gate_w"].rearrange("(t p) n -> p t n", p=P)),
                           (self.owners[:, :, :], core.A["c_spread"].rearrange("t e p -> e t p"))]
        self.loaded = semaphores(nc, ctx)(tag + "_weights_in")
        self.all_in = 16 * len(self.loads)

    def load(self, eng):
        for dst, src in self.loads:
            eng.dma_start(dst, src).then_inc(self.loaded, 16)


def feed_forward(core, tag, weights, experts):
    nc, A = core.nc, core.A
    width, tiles, wg, wu, wd = weights.width, weights.tiles, weights.wg, weights.wu, weights.wd
    with ExitStack() as ctx:
        def sb(name, shape, dt=F32):
            return ctx.enter_context(nc.sbuf_tensor(f"{tag}_{name}", shape, dt))

        def ps(name, shape, dt=F32):
            return ctx.enter_context(nc.psum_tensor(f"{tag}_{name}", shape, dt))

        named = semaphores(nc, ctx)

        def sem(name):
            return named(f"{tag}_{name}")

        def count(name, per):
            return Count(sem(name), per)

        x4 = sb("x4", [P, GROUP, H])
        xT = sb("xT", [P, KT, NT])
        act_g = [sb(f"act_g{i}", [P, NT]) for i in range(2)]
        h = [sb(f"h{i}", [P, NT]) for i in range(2)]
        y = sb("y", [P, GROUP, H])
        stats, mv, ln_r = sb("stats", [P, GROUP, 6]), sb("mv", [P, GROUP, 2]), sb("ln_r", [P, GROUP])
        p_g = [ps(f"p_g{i}", [P, BANK]) for i in range(2)]
        p_u = [ps(f"p_u{i}", [P, BANK]) for i in range(2)]
        p_c = [ps(f"p_c{i}", [P, BANK]) for i in range(2)]
        p_y = [ps(f"p_y{i}", [P, BANK]) for i in range(2)]
        if experts:
            w_r = weights.router
            spread = sb("spread", [64, tiles, P], BF16)
            rstat = sb("rstat", [P, 3, GROUP])
            logit = sb("logit", [P, GROUP, EXPERTS])
            prob = sb("prob", [P, GROUP, EXPERTS + 2])
            repl = sb("repl", [P, GROUP, EXPERTS + 2])
            best = sb("best", [P, GROUP, 8])
            comb = sb("comb", [P, GROUP, EXPERTS])
            parts = sb("parts", [P, GROUP, 4, EXPERTS], BF16)
            combT = sb("combT", [64, NT], BF16)

        route_steps, norm_chain = sem("route_steps"), sem("norm_steps")
        tile_in = count("tile_in", 1)
        turned, xT_up = count("turned", 1), count("xT_up", 1)
        gate_made, up_made = count("gate_made", tiles), count("up_made", tiles)
        gate_up, h_up = count("gate_up", tiles), count("h_up", tiles)
        down = count("down", tiles)
        y_read, var_up, rooted, x_up = count("y_read", 1), count("var_up", 1), count("rooted", 1), count("x_up", 1)
        if experts:
            r_made, r_in, r_exp = count("r_made", 2), count("r_in", 1), count("r_exp", 1)
            parts_up, combT_up, c_made = count("parts_up", 1), count("combT_up", 1), count("c_made", tiles)
            h_raw = count("h_raw", tiles)
            spread_up = sem("spread_up")
        order = [("in", 0), ("route", 0), ("tile0", 0), ("norm1", 1), ("tile1", 0), ("norm2", 1), ("others", 0),
                 ("sum", 0)]
        block = ctx.enter_context(nc.Block())

        @block.sync
        def _(sp):
            sp.wait_ge(weights.loaded, weights.all_in)

        @block.gpsimd
        def _(pool):
            for c in (tile_in, rooted):
                c.open(pool)

            def tile_copy(b):
                pool.wait_ge(turned.sem, turned.of(b - 1))
                pool.tensor_copy(x4[:, :, :], core.x[:, bass.ds(b * GROUP, GROUP), :]).then_inc(tile_in.sem, 1)

            def root(b):
                pool.wait_ge(var_up.sem, var_up.of(b))
                pool.tensor_tensor(ln_r[:, :], mv[:, :, 1], core.neghalf[:, 0:GROUP], ALU.pow).then_inc(rooted.sem, 1)

            pipeline(pool, order, {"in": tile_copy, "norm1": root}, B // GROUP)

        @block.tensor
        def _(pe):
            for c in (turned, gate_made, up_made, down) + ((r_made, c_made) if experts else ()):
                c.open(pe)
            pe.wait_ge(weights.loaded, weights.all_in)
            with pe.Fori(0, B // GROUP) as b:
                pe.wait_ge(tile_in.sem, tile_in.of(b))
                pe.wait_ge(gate_up.sem, gate_up.of(b - 1))
                for t in range(KT):
                    for j in range(GROUP):
                        mm = pe.transpose(p_g[t][:, j * P:(j + 1) * P], x4[:, j, t * P:(t + 1) * P], core.ident[:, :])
                mm.then_inc(turned.sem, 1)
                pe.wait_ge(xT_up.sem, xT_up.of(b))

                def tile_rows(n):
                    return min(P, width - n * P)

                def gate_and_up(n):
                    m = tile_rows(n)
                    for bank, w, c, freed in ((p_g, wg, gate_made, gate_up), (p_u, wu, up_made, h_raw if experts else h_up)):
                        pe.wait_ge(freed.sem, freed.of(b, n - 1) if n >= 2 else freed.of(b - 1))
                        for t in range(KT):
                            mm = pe.matmul(bank[n % 2][0:m, :], w[:, t, n * P:n * P + m], xT[:, t, :],
                                           start=(t == 0), stop=(t == KT - 1))
                        mm.then_inc(c.sem, 1)

                def token_weights(n):
                    m = tile_rows(n)
                    pe.wait_ge(h_up.sem, h_up.of(b, n - 1) if n >= 2 else h_up.of(b - 1))
                    pe.matmul(p_c[n % 2][0:m, :], spread[:, n, 0:m], combT[:, :], start=True, stop=True).then_inc(c_made.sem, 1)

                def project(n):
                    m = tile_rows(n)
                    pe.wait_ge(h_up.sem, h_up.of(b, n + 1))
                    if n == 0:
                        pe.wait_ge(y_read.sem, y_read.of(b - 1))
                    for j in range(GROUP):
                        mm = pe.matmul(p_y[j // 2][:, (j % 2) * H:(j % 2 + 1) * H], h[n % 2][0:m, j * P:(j + 1) * P],
                                       wd[0:m, n, :], start=(n == 0 and j % 2 == 0), stop=(n == tiles - 1 and j % 2 == 1))
                    mm.then_inc(down.sem, 1)

                if experts:
                    pe.wait_ge(h_up.sem, h_up.of(b - 1))
                    for j in range(GROUP):
                        for t in range(KT):
                            mm = pe.matmul(p_c[0][:, j * EXPERTS:(j + 1) * EXPERTS], xT[:, t, j * P:(j + 1) * P], w_r[:, t, :],
                                           start=(j == 0 and t == 0), stop=(j == GROUP - 1 and t == KT - 1))
                    mm.then_inc(r_made.sem, 1)
                gate_and_up(0)
                gate_and_up(1)
                if experts:
                    pe.wait_ge(spread_up, 1)
                    pe.wait_ge(parts_up.sem, parts_up.of(b))
                    for j in range(GROUP):
                        mm = pe.transpose(p_c[1][0:64, 0:NT // 2].bitcast(BF16)[:, j * P:(j + 1) * P],
                                          parts[:, j, :, :].rearrange("p a e -> p (a e)"), core.identb[:, :])
                    mm.then_inc(r_made.sem, 1)
                    pe.wait_ge(combT_up.sem, combT_up.of(b))
                    token_weights(0)
                for n in range(tiles):
                    if experts and n + 1 < tiles:
                        token_weights(n + 1)
                    if n + 2 < tiles:
                        gate_and_up(n + 2)
                    project(n)

        @block.scalar
        def _(act):
            for c in (xT_up, gate_up) + ((r_exp, combT_up) if experts else ()):
                c.open(act)
            with act.Fori(0, B // GROUP) as b:
                act.wait_ge(turned.sem, turned.of(b))
                act.wait_ge(up_made.sem, up_made.of(b - 1))
                for t in range(KT):
                    i = act.copy(xT[:, t, :], p_g[t][:, :])
                i.then_inc(xT_up.sem, 1)
                if experts:
                    act.wait_ge(r_in.sem, r_in.of(b))
                    act.activation(prob[:, :, 0:EXPERTS], logit[:, :, :], ACT.Exp).then_inc(r_exp.sem, 1)
                    act.wait_ge(r_made.sem, r_made.of(b, 2))
                    act.wait_ge(c_made.sem, c_made.of(b - 1))
                    act.copy(combT[:, :], p_c[1][0:64, 0:NT // 2].bitcast(BF16)).then_inc(combT_up.sem, 1)
                for n in range(tiles):
                    m = min(P, width - n * P)
                    act.wait_ge(gate_made.sem, gate_made.of(b, n + 1))
                    freed = h_raw if experts else h_up
                    act.wait_ge(freed.sem, freed.of(b, n - 1) if n >= 2 else freed.of(b - 1))
                    act.activation(act_g[n % 2][0:m, :], p_g[n % 2][0:m, :], ACT.Silu).then_inc(gate_up.sem, 1)

        @block.vector
        def _(dve):
            for c in (h_up, y_read, var_up, x_up) + ((r_in, parts_up, h_raw) if experts else ()):
                c.open(dve)
            if experts:
                dve.memset(prob[:, :, EXPERTS:], 2.0)
                dve.memset(parts[:, :, 3, :], 0.0).then_inc(route_steps, 1)
                dve.wait_ge(route_steps, 1)
                dve.memset(parts[:, :, 3, 0:1], 1.0).then_inc(route_steps, 1)
                dve.wait_ge(weights.loaded, weights.all_in)
                dve.tensor_copy(spread[:, :, :], weights.owners[:, :, :]).then_inc(spread_up, 1)
            ch, tail = Chain(dve, route_steps, 13, base=2), Chain(dve, norm_chain, 3)

            def route(b):
                ch.start(b)
                dve.wait_ge(r_made.sem, r_made.of(b, 1))
                r3 = p_c[0][:, 0:GROUP * EXPERTS].rearrange("p (g e) -> p g e", e=EXPERTS)
                pr = prob[:, :, 0:EXPERTS]
                ch.link(dve.tensor_reduce(rstat[:, 0, :], r3, AX.X, ALU.max))
                dve.tensor_tensor(logit[:, :, :], r3, bcast(rstat[:, 0, :], [P, GROUP, EXPERTS]), ALU.subtract).then_inc(r_in.sem, 1)
                dve.wait_ge(r_exp.sem, r_exp.of(b))
                ch.link(dve.tensor_reduce(rstat[:, 1, :], pr, AX.X, ALU.add))
                ch.link(dve.reciprocal(rstat[:, 2, :], rstat[:, 1, :]))
                ch.link(dve.tensor_tensor(pr, pr, bcast(rstat[:, 2, :], [P, GROUP, EXPERTS]), ALU.mult))
                ch.settle()
                for j in range(GROUP):
                    i = dve.max(best[:, j, :], prob[:, j, :])
                ch.link(i)
                ch.settle()
                for j in range(GROUP):
                    i = dve.match_replace(repl[:, j, :], best[:, j, :], prob[:, j, :], CHOSEN)
                ch.link(i)
                ch.link(dve.scalar_tensor_tensor(out=comb[:, :, :], in0=repl[:, :, 0:EXPERTS], scalar=CHOSEN, in1=pr,
                                                 op0=ALU.is_ge, op1=ALU.mult))
                dve.wait_ge(r_made.sem, r_made.of(b - 1))
                for j in range(3):
                    i = dve.tensor_copy(parts[:, :, j, :], comb[:, :, :])
                    if j < 2:
                        ch.link(i)
                        ch.link(dve.tensor_tensor(comb[:, :, :], comb[:, :, :], parts[:, :, j, :], ALU.subtract))
                    else:
                        i.then_inc(parts_up.sem, 1)
                ch.end()

            def rows(*which):
                def run(b):
                    for n in which:
                        m = min(P, width - n * P)
                        dve.wait_ge(up_made.sem, up_made.of(b, n + 1))
                        dve.wait_ge(gate_up.sem, gate_up.of(b, n + 1))
                        dve.wait_ge(down.sem, down.of(b, n - 1) if n >= 2 else down.of(b - 1))
                        i = dve.tensor_tensor(h[n % 2][0:m, :], act_g[n % 2][0:m, :], p_u[n % 2][0:m, :], ALU.mult)
                        if experts:
                            i.then_inc(h_raw.sem, 1)
                            dve.wait_ge(h_raw.sem, h_raw.of(b, n + 1))
                            dve.wait_ge(c_made.sem, c_made.of(b, n + 1))
                            i = dve.tensor_tensor(h[n % 2][0:m, :], h[n % 2][0:m, :], p_c[n % 2][0:m, :], ALU.mult)
                        i.then_inc(h_up.sem, 1)
                return run

            def add_residual(b):
                dve.wait_ge(down.sem, down.of(b))
                dve.wait_ge(x_up.sem, x_up.of(b - 1))
                for i in range(2):
                    ins = dve.tensor_tensor(y[:, 2 * i:2 * i + 2, :], p_y[i][:, :].rearrange("p (g h) -> p g h", h=H),
                                            core.x[:, bass.ds(b * GROUP + 2 * i, 2), :], ALU.add)
                ins.then_inc(y_read.sem, 1)

            def statistics(b):
                tail.start(b)
                dve.wait_ge(y_read.sem, y_read.of(b))
                for j in range(GROUP):
                    ins = dve.bn_stats(stats[:, j, :], y[:, j, :])
                tail.link(ins)
                tail.settle()
                for j in range(GROUP):
                    ins = dve.bn_aggr(mv[:, j, :], stats[:, j, :])
                tail.link(ins)
                dve.tensor_scalar(mv[:, :, 1], mv[:, :, 1], LN_EPS, None, ALU.add).then_inc(var_up.sem, 1)
                tail.end()

            def layer_norm(b):
                dve.wait_ge(rooted.sem, rooted.of(b))
                for j in range(GROUP):
                    ins = dve.tensor_scalar(core.x[:, bass.ds(b * GROUP + j, 1), :].rearrange("p o h -> p (o h)"), y[:, j, :],
                                            mv[:, j, 0:1], ln_r[:, j:j + 1], ALU.subtract, ALU.mult)
                ins.then_inc(x_up.sem, 1)

            pieces = {"tile0": rows(0), "norm1": statistics, "tile1": rows(1), "norm2": layer_norm,
                      "others": rows(*range(2, tiles)), "sum": add_residual}
            if experts:
                pieces["route"] = route
            pipeline(dve, order, pieces, B // GROUP)


def l0_ffn_weights(core, ctx):
    inter = 1024

    def loads(A, wg, wu, wd):
        w = A["L0_ffn_w_gate_up"].rearrange("(t p) n -> p t n", p=P)
        yield wg[:, :, :], w[:, :, 0:inter]
        yield wu[:, :, :], w[:, :, inter:]
        yield wd[:, :, :], A["L0_ffn_w_down"].rearrange("(k p) n -> p k n", p=P)

    return Weights(core, ctx, "f0", inter, loads)


def l1_ffn_weights(core, ctx):
    wide = EXPERTS * EI

    def loads(A, wg, wu, wd):
        for t in range(KT):
            rows = slice(t * P, (t + 1) * P)
            for j, dst in enumerate((wg, wu)):
                yield (dst[:, t, 0:wide].rearrange("p (e i) -> p e i", i=EI),
                       A["L1_ffn_w1"][rows, :, j * EI:(j + 1) * EI])
                yield dst[:, t, wide:], A["L1_ffn_shared_w1"][rows, j * SI:(j + 1) * SI]
        yield (wd[:, 0:wide // P, :],
               A["L1_ffn_w2"].rearrange("e i h -> (e i) h").rearrange("(k p) h -> p k h", p=P))
        whole = SI // P
        yield (wd[:, wide // P:wide // P + whole, :],
               A["L1_ffn_shared_w2"][0:whole * P, :].rearrange("(k p) h -> p k h", p=P))
        yield wd[0:SI - whole * P, wide // P + whole, :], A["L1_ffn_shared_w2"][whole * P:, :]

    return Weights(core, ctx, "f1", wide + SI, loads, experts=True)


def constants():
    pos = np.arange(P)
    half = ROPE // 2
    inv = (1.0 / np.power(np.float32(10000.0), np.arange(half, dtype=np.float32) * np.float32(2.0 / ROPE))).astype(np.float32)

    def rope(at):
        ang = at.astype(np.float32)[:, None] * inv[None, :]
        cos, sin = np.cos(ang), np.sin(ang)
        return (np.concatenate([cos, cos, np.ones((len(at), D - ROPE))], axis=1).astype(np.float32),
                np.concatenate([-sin, sin], axis=1).astype(np.float32))

    c = {}
    c["c_ident"] = np.eye(P, dtype=np.float32)
    c["c_causal"] = np.where(pos[None, :] <= pos[:, None], 0, NEG).astype(np.float32)
    c["c_cos"], c["c_sin"] = rope(pos)
    ends = np.arange(1, NC + 1) * RATIO - 1
    c["c_cos_c"], c["c_sin_c"] = rope(ends[pos % NC])
    c["c_cmask"] = np.where(ends[None, :] <= pos[:, None], 0, NEG).astype(np.float32)
    c["c_member"] = (pos[:, None] // RATIO == np.arange(NC)[None, :]).astype(np.float32)
    for dk in (8, 16):
        c[f"c_owner{dk}"] = (pos[:, None] // dk == np.arange(P // dk)[None, :]).astype(np.float32)
    wide = EXPERTS * EI
    row = np.arange(-(-(wide + SI) // P) * P)
    owner = np.where(row < wide, row // EI, 3 * EXPERTS)
    spread = np.zeros((64, len(row)), np.float32)
    for j in range(3):
        spread += np.arange(64)[:, None] == np.where(row < wide, owner + j * EXPERTS, -1)[None, :]
    spread[3 * EXPERTS, :] = row >= wide
    c["c_spread"] = np.ascontiguousarray(spread.reshape(64, -1, P).transpose(1, 0, 2))
    return c


def program(nc, A, out):
    with ExitStack() as ctx:
        core = Core(nc, ctx, A, out)
        with ExitStack() as own:
            weights = AttentionWeights(core, own)
            wcol = own.enter_context(nc.sbuf_tensor("token_weights", [P, B], F32))
            setup(core, weights)
            l0_token_weights(core, wcol, weights)
            l0_attention(core, wcol, weights)
        with ExitStack() as own:
            weights = l0_ffn_weights(core, own)
            l0_cross_attention(core, weights)
            feed_forward(core, "f0", weights, experts=False)
        l1_self_attention(core)
        with ExitStack() as own:
            weights = l1_ffn_weights(core, own)
            l1_cross_attention(core, weights)
            feed_forward(core, "f1", weights, experts=True)
        store(core)


def store(core):
    nc = core.nc
    with ExitStack() as ctx:
        stored = semaphores(nc, ctx)("stored")
        block = ctx.enter_context(nc.Block())

        @block.sync
        def _(sp):
            sp.dma_start(core.out.rearrange("b p h -> p b h"), core.x[:, :, :]).then_inc(stored, 16)
            sp.wait_ge(stored, 16)


UNUSED = ("L1_xattn_context_lens", "L1_xattn_Wk", "L1_xattn_bk", "L1_xattn_gk", "L1_xattn_Wv", "L1_xattn_bv")
TRANSPOSED = ("L0_ffn_w_gate_up", "L0_ffn_w_down", "L1_attn_Wq", "L1_attn_Wk", "L1_attn_Wv", "L1_attn_Wo",
              "L1_ffn_gate_w", "L1_ffn_shared_w1", "L1_ffn_shared_w2")
OUT = ((B, P, H), "float32")


def kernel(**inputs):
    import numpy as _np
    import concourse.bacc as _bacc
    from concourse import mybir as _mybir
    from concourse.bass_utils import run_bass_kernel_spmd as _run

    given = {}
    for name, a in inputs.items():
        if name in UNUSED:
            continue
        if name in TRANSPOSED:
            a = _np.asarray(a).T
        elif name == "L1_ffn_w1":
            a = _np.asarray(a).transpose(2, 0, 1)
        elif name == "L1_ffn_w2":
            a = _np.asarray(a).transpose(0, 2, 1)
        given[name] = _np.ascontiguousarray(a)
    given.update(constants())
    nc = _bacc.Bacc("TRN2", target_bir_lowering=False, num_devices=1)
    arrays, A = {}, {}
    for name, a in given.items():
        arrays[f"in_{name}_dram"] = a
        A[name] = nc.dram_tensor(f"in_{name}_dram", a.shape, _mybir.dt.from_np(a.dtype), kind="ExternalInput").ap()
    out = nc.dram_tensor("out_0_dram", OUT[0], _mybir.dt.from_np(_np.dtype(OUT[1])), kind="ExternalOutput").ap()
    program(nc, A, out)
    r = _run(nc, [arrays], core_ids=[0])
    return r.results[0]["out_0_dram"]
```
